# Optimizing a Trainium2 kernel written in Bass

```python
import numpy as np
import jax
import jax.numpy as jnp

def _softmax(x, axis=-1):
    return jax.nn.softmax(x, axis=axis)

def _gelu(x):
    return jax.nn.gelu(x, approximate=True)

def _silu(x):
    return jax.nn.silu(x)

def _sigmoid(x):
    return jax.nn.sigmoid(x)

def _layernorm(x, axis=-1, eps=1e-05):
    m = jnp.mean(x, axis=axis, keepdims=True)
    v = jnp.var(x, axis=axis, keepdims=True)
    return (x - m) / jnp.sqrt(v + eps)

def _scatter_add(tgt, idx, src, axis=0):
    return tgt.at[idx].add(src)

def _segment_sum(src, seg, n):
    return jax.ops.segment_sum(src, seg, n)
kernel_name = 'mk_gnn_ffn_d1_gnn_r32_d85fd0'

def setup_inputs(seed: int=0):
    np.random.seed(seed)
    _w = jnp.asarray

    def _rec_inputs():
        import jax
        import jax.numpy as jnp
        _gk = jax.random.key(seed)
        x = -6.415e-05 + 1 * jax.random.normal(jax.random.fold_in(_gk, 1), (625, 512), jnp.float32)
        _s = jax.random.randint(jax.random.fold_in(_gk, 2), (5000,), 0, 625, jnp.int32)
        _d = jax.random.randint(jax.random.fold_in(_gk, 3), (5000,), 0, 625, jnp.int32)
        _loop = jnp.arange(625, dtype=jnp.int32)
        src = jnp.concatenate([_s, _d, _loop])
        dst = jnp.concatenate([_d, _s, _loop])
        _o = jnp.argsort(dst, stable=True)
        src = src[_o]
        dst = dst[_o]
        edge_type_8 = jax.random.randint(jax.random.fold_in(_gk, 12), (10625,), 0, 8, jnp.int32)
        return (x, src, dst, edge_type_8)
    x, src, dst, edge_type_8 = _rec_inputs()

    def _L0_gnn_setup():
        import jax, jax.numpy as jnp
        import numpy as np
        N = 625
        E = 5000
        D = 512
        R = 8
        key = jax.random.key(seed)
        ks = jax.random.split(key, 8)
        inp = {'input': jax.random.normal(ks[0], (N, D), dtype=jnp.float32), 'heads': jax.random.randint(ks[1], (E,), 0, N), 'tails': jax.random.randint(ks[2], (E,), 0, N), 'rel': jax.random.randint(ks[3], (E,), 0, R), 'W_self': jax.random.normal(ks[4], (D, D), dtype=jnp.float32) * 0.03, 'b_self': jnp.zeros((D,), dtype=jnp.float32), 'W_rel': jax.random.normal(ks[5], (2 * R, D, D), dtype=jnp.float32) * 0.03, 'b_rel': jnp.zeros((2 * R, D), dtype=jnp.float32)}
        return inp
    _L0_gnn_all = _L0_gnn_setup()
    _L0_gnn_in = {k: v for k, v in _L0_gnn_all.items() if k in ('W_self', 'b_self', 'W_rel', 'b_rel')}
    del _L0_gnn_all

    def _L0_ffn_setup():
        import jax, jax.numpy as jnp
        import numpy as np
        B, S, H, E, F, TOP_K = (4, 64, 512, 16, 1024, 2)

        def _moe_forward(inputs, router_w, gate_w, up_w, down_w):
            b, s, h = inputs.shape
            x = inputs.reshape(-1, h)
            T = x.shape[0]
            router_logits = x @ router_w.T
            top_vals, top_idx = jax.lax.top_k(router_logits, TOP_K)
            weights = jax.nn.softmax(top_vals.astype(jnp.float32), axis=-1)
            combine = jnp.zeros((T, router_w.shape[0]), jnp.float32)
            combine = combine.at[jnp.arange(T)[:, None], top_idx].set(weights)

            def step(acc, ew):
                wg, wu, wd, ce = ew
                hid = jax.nn.silu(x @ wg) * (x @ wu)
                y = hid @ wd
                return (acc + ce[:, None] * y, None)
            out0 = jnp.zeros_like(x)
            out, _ = jax.lax.scan(step, out0, (gate_w, up_w, down_w, combine.T))
            return (out.reshape(b, s, h), router_logits, top_idx)
        key = jax.random.key(seed)
        k0, k1, k2, k3, k4 = jax.random.split(key, 5)
        scale = 0.02
        return {'inputs': jax.random.normal(k0, (B, S, H), dtype=jnp.float32), 'router_w': jax.random.normal(k1, (E, H), dtype=jnp.float32) * scale, 'gate_w': jax.random.normal(k2, (E, H, F), dtype=jnp.float32) * scale, 'up_w': jax.random.normal(k3, (E, H, F), dtype=jnp.float32) * scale, 'down_w': jax.random.normal(k4, (E, F, H), dtype=jnp.float32) * scale}
    _L0_ffn_all = _L0_ffn_setup()
    _L0_ffn_in = {k: v for k, v in _L0_ffn_all.items() if k in ('router_w', 'gate_w', 'up_w', 'down_w')}
    del _L0_ffn_all
    return {'x': x, 'src': src, 'dst': dst, 'edge_type_8': edge_type_8, 'L0_gnn_W_self': _L0_gnn_in['W_self'], 'L0_gnn_b_self': _L0_gnn_in['b_self'], 'L0_gnn_W_rel': _L0_gnn_in['W_rel'], 'L0_gnn_b_rel': _L0_gnn_in['b_rel'], 'L0_ffn_router_w': _L0_ffn_in['router_w'], 'L0_ffn_gate_w': _L0_ffn_in['gate_w'], 'L0_ffn_up_w': _L0_ffn_in['up_w'], 'L0_ffn_down_w': _L0_ffn_in['down_w']}

def reference(x, src, dst, edge_type_8, L0_gnn_W_self, L0_gnn_b_self, L0_gnn_W_rel, L0_gnn_b_rel, L0_ffn_router_w, L0_ffn_gate_w, L0_ffn_up_w, L0_ffn_down_w):
    import jax
    import jax.numpy as jnp

    def _L0_gnn_ref(input, heads, tails, rel, W_self, b_self, W_rel, b_rel):
        import jax, jax.numpy as jnp
        import numpy as np
        N = 625
        E = 5000
        D = 512
        R = 8
        h_self = input @ W_self.T + b_self
        H_all = jnp.einsum('rod,nd->rno', W_rel, input) + b_rel[:, None, :]
        msg_to_heads = H_all[rel, tails]
        msg_to_tails = H_all[rel + R, heads]
        agg = jax.ops.segment_sum(msg_to_heads, heads, num_segments=N) + jax.ops.segment_sum(msg_to_tails, tails, num_segments=N)
        return jax.nn.relu(h_self + agg)

    def _L0_ffn_ref(inputs, router_w, gate_w, up_w, down_w):
        import jax, jax.numpy as jnp
        import numpy as np
        B, S, H, E, F, TOP_K = (4, 64, 512, 16, 1024, 2)

        def _moe_forward(inputs, router_w, gate_w, up_w, down_w):
            b, s, h = inputs.shape
            x = inputs.reshape(-1, h)
            T = x.shape[0]
            router_logits = x @ router_w.T
            top_vals, top_idx = jax.lax.top_k(router_logits, TOP_K)
            weights = jax.nn.softmax(top_vals.astype(jnp.float32), axis=-1)
            combine = jnp.zeros((T, router_w.shape[0]), jnp.float32)
            combine = combine.at[jnp.arange(T)[:, None], top_idx].set(weights)

            def step(acc, ew):
                wg, wu, wd, ce = ew
                hid = jax.nn.silu(x @ wg) * (x @ wu)
                y = hid @ wd
                return (acc + ce[:, None] * y, None)
            out0 = jnp.zeros_like(x)
            out, _ = jax.lax.scan(step, out0, (gate_w, up_w, down_w, combine.T))
            return (out.reshape(b, s, h), router_logits, top_idx)
        out, router_logits, selected_experts = _moe_forward(inputs, router_w, gate_w, up_w, down_w)
        return out
    x = x + _L0_gnn_ref(_layernorm(x, axis=-1), src, dst, edge_type_8, L0_gnn_W_self, L0_gnn_b_self, L0_gnn_W_rel, L0_gnn_b_rel)
    x = x + _L0_ffn_ref(_layernorm(x, axis=-1)[None], L0_ffn_router_w, L0_ffn_gate_w, L0_ffn_up_w, L0_ffn_down_w)[0]
    return x

_drawn_inputs = setup_inputs


def setup_inputs(seed=0):
    import zlib

    import numpy as np

    out = dict(_drawn_inputs(seed))
    spreads = {'L0_gnn_b_self': (0.0, 0.334), 'L0_gnn_b_rel': (0.0, 0.1)}
    factors = {'L0_ffn_router_w': 3.696,
     'L0_ffn_gate_w': 3.525,
     'L0_ffn_up_w': 3.447,
     'L0_ffn_down_w': 3.456}
    for name, (base, spread) in spreads.items():
        noise = np.random.default_rng([zlib.crc32(name.encode()), seed]).standard_normal(out[name].shape)
        drawn = base * np.exp(spread * noise) if base else spread * noise
        out[name] = jnp.asarray(drawn.astype(out[name].dtype))
    for name, factor in factors.items():
        out[name] = (out[name] * factor).astype(out[name].dtype)
    return out
```

```python
from contextlib import ExitStack

import concourse.bass as bass
from concourse import mybir

F32 = mybir.dt.float32
F32R = mybir.dt.float32r
F16 = mybir.dt.float16
I32 = mybir.dt.int32
U32 = mybir.dt.uint32
ALU = mybir.AluOpType
ACT = mybir.ActivationFunctionType
AX = mybir.AxisListType

P = 128
N, D = 625, 512
TP, T = 125, 5
KC = D // P
R = 8
E = 10625
EP, EC = 125, 85
WIN = 16
NW = 40
NPAD = NW * WIN
CH = 3
CAP = CH * P
ROUNDS = -(-E // CAP)
EDGES = 87 * P
KEY = 1024
NX, F = 16, 1024
SLOTS = T * P
FC = F // P
MAXOV = (2 * N - NX) // P
LN_EPS = 1e-5


def build(nc, x, src, dst, edge_type, w_self, b_self, w_rel, b_rel, router_w, gate_w, up_w, down_w, out, stop=None):
    ctx = ExitStack()
    with ctx:
        def sb(name, shape, dt, c=ctx):
            return c.enter_context(nc.sbuf_tensor(name, shape, dt))

        def ps(name, shape, dt, c):
            return c.enter_context(nc.psum_tensor(name, shape, dt))

        def sem(name):
            return ctx.enter_context(nc.semaphore(name))

        edges_dram = nc.dram_tensor("edges_dram", [EDGES, 2], F32).ap()
        ln2_dram = nc.dram_tensor("ln2_dram", [N, D], F32).ap()
        slot_token_dram = nc.dram_tensor("slot_token_dram", [NX * SLOTS, 1], I32).ap()
        y_dram = nc.dram_tensor("y_dram", [(NX + MAXOV) * P, D], F32).ap()

        ident = sb("ident", [P, P], F32)
        ident16 = sb("ident16", [P, P], F16)
        ones = sb("ones", [P, P], F32)
        x_sb = sb("x_sb", [TP, T, D], F32)
        agg_sb = sb("agg_sb", [TP, T, D], F32)
        stats = sb("stats", [TP, T, 6], F32)
        meanvar = sb("meanvar", [TP, T, 2], F32)
        rstd = sb("rstd", [TP, T], F32)
        stage_gate = sb("stage_gate", [P, KC, F], F32)
        before = sb("before", [TP, TP], F32)
        expert_iota = sb("expert_iota", [TP, NX], F32)
        token_id = sb("token_id", [TP, T], I32)
        tile_iota = sb("tile_iota", [1, MAXOV], F32)
        router_sb = sb("router_sb", [NX, D], F32)

        chain = {e: sem(f"{e}_chain") for e in ("dve", "act", "pool")}
        consts_ready = sem("consts_ready")
        x_loaded = sem("x_loaded")
        edge_loaded = sem("edge_loaded")
        wself_loaded = sem("wself_loaded")
        small_loaded = sem("small_loaded")
        edges_packed, edges_stored = sem("edges_packed"), sem("edges_stored")
        var_ready, root_ready, ln_ready = sem("var_ready"), sem("root_ready"), sem("ln_ready")
        tr_full, tr_hi, tr_lo = sem("tr_full"), sem("tr_hi"), sem("tr_lo")
        self_full, self_copied = sem("self_full"), sem("self_copied")
        count_ready, count_full = sem("count_ready"), sem("count_full")

        zero_ready = sem("zero_ready")
        win_loaded = [sem(f"win_loaded{i}") for i in range(4)]
        onehot_ready, a_full, a_stored = sem("onehot_ready"), sem("a_full"), sem("a_stored")
        wa_loaded, wb_loaded = sem("wa_loaded"), sem("wb_loaded")
        t_full, wt_hi, wt_lo = sem("t_full"), sem("wt_hi"), sem("wt_lo")
        a_ready, at_ready = sem("a_ready"), sem("at_ready")
        h_full, h_hi, h_lo = sem("h_full"), sem("h_hi"), sem("h_lo")
        deg_full, deg_copied, agg_full = sem("deg_full"), sem("deg_copied"), sem("agg_full")
        agg_added = sem("agg_added")
        round_sems = range(zero_ready.num, agg_added.num + 1)
        assert len(round_sems) == 22

        route_consts = sem("route_consts")
        slots_cleared, gate0_loaded = sem("slots_cleared"), sem("gate0_loaded")
        router_full, router_copied = sem("router_full"), sem("router_copied")
        x2_full, x2_even, x2_odd, logits_full = sem("x2_full"), sem("x2_even"), sem("x2_odd"), sem("logits_full")
        ln2_stored, gap_ready, exp_ready = sem("ln2_stored"), sem("gap_ready"), sem("exp_ready")
        mask_ready, rank_full, places_ready = sem("mask_ready"), sem("rank_full"), sem("places_ready")
        slots_filled, slots_loaded = sem("slots_filled"), sem("slots_loaded")
        loaded = {k: [sem(f"{k}{i}_loaded") for i in range(2)] for k in "gud"}
        split_hi = {k: sem(f"{k}_hi") for k in "gud"}
        split_lo = {k: sem(f"{k}_lo") for k in "gud"}
        done = {k: sem(f"{k}_done") for k in "gud"}
        column_copied, column_waited, tokens_loaded = sem("column_copied"), sem("column_waited"), sem("tokens_loaded")
        xt_full, xt_hi_ready, xt_lo_ready = sem("xt_full"), sem("xt_hi_ready"), sem("xt_lo_ready")
        silu_ready, hid_ready = sem("silu_ready"), sem("hid_ready")
        ht_full, ht_hi_ready, ht_lo_ready = sem("ht_full"), sem("ht_hi_ready"), sem("ht_lo_ready")
        y_copied, y_stored = sem("y_copied"), sem("y_stored")
        o_tokens = sem("o_tokens")
        o_loaded = {k: sem(f"o_{k}_loaded") for k in "gud"}
        o_column = sem("o_column")
        o_xt_full, o_xt, o_gate, o_up = sem("o_xt_full"), sem("o_xt"), sem("o_gate"), sem("o_up")
        o_silu, o_hid, o_ht_full, o_ht = sem("o_silu"), sem("o_hid"), sem("o_ht_full"), sem("o_ht")
        o_y_full, o_y, o_stored = sem("o_y_full"), sem("o_y"), sem("o_stored")
        over_sems = range(o_loaded["g"].num, o_stored.num + 1)
        assert len(over_sems) == 15
        first_loaded = [sem(f"first_loaded{t}") for t in range(T)]
        second_loaded = [sem(f"second_loaded{t}") for t in range(T)]
        combined, out_stored = sem("combined"), sem("out_stored")

        steps_done = {"dve": 0, "act": 0, "pool": 0}

        def link(name, engine, instruction):
            steps_done[name] += 1
            instruction.then_inc(chain[name], 1)
            engine.wait_ge(chain[name], steps_done[name])

        def normalize(dve, xs, xn, nth):
            v = nc.vector
            for t in range(T):
                i = v.bn_stats(stats[:, t], xs[:, t])
            link("dve", dve, i)
            for t in range(T):
                i = v.bn_aggr(meanvar[:, t], stats[:, t])
            link("dve", dve, i)
            v.tensor_scalar(rstd[:], meanvar[:, :, 1], LN_EPS, None, ALU.add).then_inc(var_ready, 1)
            dve.wait_ge(root_ready, nth + 1)
            link("dve", dve, v.reciprocal(rstd[:], rstd[:]))
            for t in range(T):
                v.tensor_scalar(xn[:, t], xs[:, t], meanvar[:, t, 0:1], rstd[:, t:t + 1],
                                ALU.subtract, ALU.mult).then_inc(ln_ready, 1)

        def roots(act, nth):
            act.wait_ge(var_ready, nth + 1)
            nc.scalar.activation(rstd[:], rstd[:], ACT.Sqrt).then_inc(root_ready, 1)

        with ExitStack() as g:
            a16 = sb("a16", [TP, T, R, NPAD], F16, g)
            xt_hi = sb("xt_hi", [P, KC, N], F32R, g)
            xt_lo = sb("xt_lo", [P, KC, N], F32R, g)
            w_nat = sb("w_nat", [P, 2, 4, D], F32, g)
            wt_hi_sb = sb("wt_hi_sb", [P, 2, KC, D], F32R, g)
            wt_lo_sb = sb("wt_lo_sb", [P, 2, KC, D], F32R, g)
            iota_row = sb("iota_row", [P, NPAD], F16, g)
            win_key = sb("win_key", [P, NW], F32, g)
            offs = sb("offs", [1, NW + 8], I32, g)
            b_rel_sb = sb("b_rel_sb", [2 * R, D], F32, g)

            with ExitStack() as f:
                xn = sb("xn", [TP, T, D], F32, f)
                b_self_sb = sb("b_self_sb", [1, D], F32, f)
                iota_i = sb("iota_i", [P, NPAD], I32, f)
                e_src = sb("e_src", [EP, EC], I32, f)
                e_dst = sb("e_dst", [EP, EC + 1], I32, f)
                e_type = sb("e_type", [EP, EC], I32, f)
                e_win = sb("e_win", [EP, EC], I32, f)
                e_winf = sb("e_winf", [EP, EC], F32, f)
                e_in = sb("e_in", [EP, EC], I32, f)
                e_key = sb("e_key", [EP, EC], F32, f)
                e_pack = sb("e_pack", [EP, EC, 2], F32, f)
                e_pad = sb("e_pad", [7, 73, 2], F32, f)
                below = sb("below", [EP, NW + 1, EC], F32, f)
                win_f = sb("win_f", [EP, NW + 1], F32, f)
                counts = sb("counts", [EP, NW + 2], F32, f)
                crow = sb("crow", [1, NW + 2], F32, f)
                cdiff = sb("cdiff", [1, NW], F32, f)
                flags = sb("flags", [1, 4], F32, f)
                zero_rows = sb("zero_rows", [P, D], F32, f)
                no_token = sb("no_token", [P, NX * T], I32, f)
                tile_iota_i = sb("tile_iota_i", [1, MAXOV], I32, f)
                expert_iota_i = sb("expert_iota_i", [TP, NX], I32, f)
                p_t = ps("p_t", [P, 2, 1024], F32, f)
                p_self = ps("p_self", [P, 2, 512], F32, f)
                p_count = ps("p_count", [P, 512], F32, f)

                block = f.enter_context(nc.Block())

                @block.sync
                def _(sp):
                    sp.dma_start(x_sb[:], x.rearrange("(t p) d -> p t d", p=TP)).then_inc(x_loaded, 16)
                    sp.wait_ge(consts_ready, 2)
                    sp.dma_start(e_dst[0:EP - 1, :], bass.AP(dst.tensor, 0, [[EC, EP - 1], [1, EC + 1]])).then_inc(edge_loaded, 16)
                    sp.dma_start(e_dst[EP - 1:EP, 0:EC], dst[(EP - 1) * EC:E].rearrange("(a b) -> a b", a=1)).then_inc(edge_loaded, 16)
                    sp.dma_start(e_src[:], src.rearrange("(p c) -> p c", p=EP)).then_inc(edge_loaded, 16)
                    sp.dma_start(e_type[:], edge_type.rearrange("(p c) -> p c", p=EP)).then_inc(edge_loaded, 16)
                    sp.dma_start(w_nat[:, 0], w_self.rearrange("(c p) d -> p c d", p=P)).then_inc(wself_loaded, 16)
                    sp.dma_start(router_sb[:], router_w).then_inc(small_loaded, 16)
                    sp.dma_start(b_rel_sb[:], b_rel).then_inc(small_loaded, 16)
                    sp.dma_start(b_self_sb[:], b_self.rearrange("(a d) -> a d", a=1)).then_inc(small_loaded, 16)
                    sp.wait_ge(edges_packed, 1)
                    sp.wait_ge(consts_ready, 5)
                    sp.dma_start(edges_dram[0:E, :].rearrange("(p c) k -> p (c k)", p=EP),
                                 e_pack[:].rearrange("p c k -> p (c k)")).then_inc(edges_stored, 16)
                    sp.dma_start(edges_dram[E:EDGES, :].rearrange("(p c) k -> p (c k)", p=7),
                                 e_pad[:].rearrange("p c k -> p (c k)")).then_inc(edges_stored, 16)
                    for i in range(2):
                        sp.dma_start(stage_gate[:, 2 * i:2 * i + 2], gate_w[0].rearrange("(c p) f -> p c f", p=P)[:, 2 * i:2 * i + 2]
                                     ).then_inc(loaded["g"][i], 16)
                    sp.wait_ge(route_consts, 2)
                    sp.dma_start(slot_token_dram.rearrange("(p c) k -> p (c k)", p=P), no_token[:]).then_inc(slots_cleared, 16)
                    sp.dma_start(y_dram[NX * P:(NX + MAXOV) * P, :].rearrange("(c p) d -> p c d", p=P),
                                 zero_rows[:].unsqueeze(1).to_broadcast([P, MAXOV, D])).then_inc(slots_cleared, 16)
                    sp.wait_ge(edges_stored, 32)
                    sp.wait_ge(slots_cleared, 32)

                @block.gpsimd
                def _(pool):
                    nc.gpsimd.memset(ones[:], 1.0).then_inc(consts_ready, 1)
                    nc.gpsimd.memset(e_dst[:], 1 << 20).then_inc(consts_ready, 1)
                    pool.wait_ge(consts_ready, 1)
                    nc.gpsimd.affine_select(out=ident[:], in_=ones[:], compare_op=ALU.is_equal, fill=0.0, base=0,
                                            pattern=[[-1, P]], channel_multiplier=1).then_inc(consts_ready, 1)
                    nc.gpsimd.iota(iota_i[:], [[1, NPAD]], base=0, channel_multiplier=0).then_inc(consts_ready, 1)
                    nc.gpsimd.memset(e_pad[:], -1.0).then_inc(consts_ready, 1)
                    nc.gpsimd.memset(no_token[:], 0).then_inc(route_consts, 1)
                    nc.gpsimd.memset(zero_rows[:], 0.0).then_inc(route_consts, 1)
                    nc.gpsimd.affine_select(out=before[:], in_=ones[0:TP, 0:TP], compare_op=ALU.is_gt, fill=0.0, base=0,
                                            pattern=[[1, TP]], channel_multiplier=-1)
                    nc.gpsimd.iota(token_id[:], [[TP, T]], base=0, channel_multiplier=1)
                    nc.gpsimd.iota(tile_iota_i[:], [[1, MAXOV]], base=0, channel_multiplier=0)
                    link("pool", pool, nc.gpsimd.iota(expert_iota_i[:], [[1, NX]], base=0, channel_multiplier=0))
                    nc.gpsimd.tensor_copy(tile_iota[:], tile_iota_i[:])
                    nc.gpsimd.tensor_copy(expert_iota[:], expert_iota_i[:])

                @block.vector
                def _(dve):
                    v = nc.vector
                    dve.wait_ge(x_loaded, 16)
                    normalize(dve, x_sb, xn, 0)
                    dve.wait_ge(edge_loaded, 64)
                    dve.wait_ge(consts_ready, 5)
                    v.tensor_scalar(e_win[:], e_dst[:, 0:EC], 4, None, ALU.arith_shift_right)
                    v.tensor_scalar(e_in[:], e_dst[:, 0:EC], WIN - 1, None, ALU.bitwise_and)
                    v.tensor_copy(iota_row[:], iota_i[:])
                    v.tensor_scalar(win_key[:], iota_i[:, 0:NW], float(KEY), None, ALU.mult)
                    v.tensor_copy(e_pack[:, :, 1], e_src[:])
                    v.tensor_tensor(below[:, 0, :], e_dst[:, 0:EC], e_dst[:, 1:EC + 1], ALU.is_gt)
                    link("dve", dve, v.tensor_copy(win_f[:], iota_i[0:EP, 0:NW + 1]))
                    v.tensor_copy(e_winf[:], e_win[:])
                    v.tensor_reduce(counts[:, NW + 1:NW + 2], below[:, 0, :], AX.X, ALU.add)
                    link("dve", dve, v.scalar_tensor_tensor(e_key[:], e_type[:], float(WIN), e_in[:], ALU.mult, ALU.add))
                    v.scalar_tensor_tensor(e_pack[:, :, 0], e_winf[:], float(KEY), e_key[:], ALU.mult, ALU.add).then_inc(edges_packed, 1)
                    link("dve", dve, v.tensor_tensor(below[:], e_winf[:].unsqueeze(1).to_broadcast([EP, NW + 1, EC]),
                                                    win_f[:].unsqueeze(2).to_broadcast([EP, NW + 1, EC]), ALU.is_lt))
                    v.tensor_reduce(counts[:, 0:NW + 1], below[:], AX.X, ALU.add).then_inc(count_ready, 1)
                    n = 0
                    for dc in range(KC):
                        for a, b in ((0, 4 * TP), (4 * TP, N)):
                            n += 1
                            dve.wait_ge(tr_hi, n)
                            c = 0 if a == 0 else 512
                            v.tensor_tensor(xt_lo[:, dc, a:b], p_t[:, dc % 2, c:c + b - a], xt_hi[:, dc, a:b].bitcast(F32),
                                            ALU.subtract).then_inc(tr_lo, 1)
                    for dc in range(KC):
                        n += 1
                        dve.wait_ge(tr_hi, n)
                        v.tensor_tensor(wt_lo_sb[:, 0, dc], p_t[:, dc % 2, 0:D], wt_hi_sb[:, 0, dc].bitcast(F32),
                                        ALU.subtract).then_inc(tr_lo, 1)
                    dve.wait_ge(count_full, 1)
                    link("dve", dve, v.tensor_copy(crow[:], p_count[0:1, 0:NW + 2]))
                    link("dve", dve, v.tensor_tensor(cdiff[:], crow[:, 1:NW + 1], crow[:, 0:NW], ALU.subtract))
                    link("dve", dve, v.tensor_reduce(flags[:, 0:1], cdiff[:], AX.X, ALU.max))
                    link("dve", dve, v.tensor_scalar(flags[:, 1:2], flags[:, 0:1], float(CAP), None, ALU.is_gt))
                    link("dve", dve, v.tensor_tensor(flags[:, 2:3], flags[:, 1:2], crow[:, NW + 1:NW + 2], ALU.add))
                    link("dve", dve, v.tensor_scalar(flags[:, 3:4], flags[:, 2:3], 0.0, None, ALU.is_equal))
                    v.tensor_scalar(offs[:, 0:NW], crow[:, 0:NW], flags[:, 3:4], None, ALU.mult)
                    v.tensor_scalar(offs[:, NW:NW + 1], flags[:, 3:4], float(1 - ROUNDS), float(ROUNDS), ALU.mult, ALU.add)
                    for t in range(T):
                        dve.wait_ge(self_full, t + 1)
                        v.tensor_copy(agg_sb[:, t], p_self[0:TP, t % 2, :]).then_inc(self_copied, 1)

                @block.scalar
                def _(act):
                    s = nc.scalar
                    roots(act, 0)
                    act.wait_ge(consts_ready, 3)
                    s.copy(ident16[:], ident[:])
                    n = 0
                    for dc in range(KC):
                        act.wait_ge(tr_full, dc + 1)
                        s.copy(xt_hi[:, dc, 0:4 * TP], p_t[:, dc % 2, 0:4 * TP]).then_inc(tr_hi, 1)
                        s.copy(xt_hi[:, dc, 4 * TP:N], p_t[:, dc % 2, 512:512 + TP]).then_inc(tr_hi, 1)
                    for dc in range(KC):
                        act.wait_ge(tr_full, KC + dc + 1)
                        s.copy(wt_hi_sb[:, 0, dc], p_t[:, dc % 2, 0:D]).then_inc(tr_hi, 1)

                @block.tensor
                def _(pe):
                    m = nc.tensor
                    pe.wait_ge(consts_ready, 3)
                    pe.wait_ge(ln_ready, T)
                    for dc in range(KC):
                        if dc >= 2:
                            pe.wait_ge(tr_lo, 2 * (dc - 1))
                        for t in range(T):
                            c = t * TP if t < 4 else 512
                            i = m.transpose(p_t[:, dc % 2, c:c + TP], xn[:, t, dc * P:(dc + 1) * P], ident[0:TP, 0:TP])
                        i.then_inc(tr_full, 1)
                    pe.wait_ge(wself_loaded, 16)
                    for dc in range(KC):
                        pe.wait_ge(tr_lo, 2 * (KC - 1 + dc) if dc < 2 else 2 * KC + dc - 1)
                        for oc in range(4):
                            i = m.transpose(p_t[:, dc % 2, oc * P:(oc + 1) * P], w_nat[:, 0, oc, dc * P:(dc + 1) * P], ident[:])
                        i.then_inc(tr_full, 1)
                    pe.wait_ge(small_loaded, 48)
                    pe.wait_ge(tr_lo, 2 * KC + KC)
                    for t in range(T):
                        if t >= 2:
                            pe.wait_ge(self_copied, t - 1)
                        o = p_self[0:TP, t % 2, :]
                        m.matmul(o, ones[0:1, 0:TP], b_self_sb[:], start=True, stop=False)
                        i = split_product(m, o, xt_hi, xt_lo, wt_hi_sb, wt_lo_sb, 0, t, start=False, stop=True)
                        i.then_inc(self_full, 1)
                        if t == 0:
                            pe.wait_ge(count_ready, 1)
                            m.matmul(p_count[0:1, 0:NW + 2], ones[0:EP, 0:1], counts[:], start=True, stop=True).then_inc(count_full, 1)

            with ExitStack() as f:
                win_edges = sb("win_edges", [P, 4, CH, 2], F32, f)
                key_hot = sb("key_hot", [P, 2, CH, P], F16, f)
                src_hot = sb("src_hot", [P, 2, CH, NPAD], F16, f)
                lhs_a = sb("lhs_a", [TP, T, N], F32R, f)
                lhs_at = sb("lhs_at", [TP, T, N], F32R, f)
                h_hi_sb = sb("h_hi_sb", [TP, 2, D], F32R, f)
                h_lo_sb = sb("h_lo_sb", [TP, 2, D], F32R, f)
                degree = sb("degree", [TP, T, 2 * R], F32, f)
                degree_t = sb("degree_t", [2 * R, N], F32, f)
                zero_row = sb("zero_row", [1, D], F32R, f)
                p_agg = ps("p_agg", [P, T, 512], F32, f)
                p_h = ps("p_h", [P, 2, 512], F32, f)
                p_tr = ps("p_tr", [P, 512], F32, f)
                p_a = p_agg[:].rearrange("p t n -> p (t n)")

                p_tr16 = p_tr[0:TP].bitcast(F16)[:, 0:T * (TP + 1)].rearrange("p (t n) -> p t n", t=T)

                rounds = nc.values_load(offs[0:1, NW:NW + 1], min_val=1, max_val=ROUNDS)
                with nc.Fori(0, rounds):
                    with nc.Block() as block:
                        @block.sync
                        def _(sp):
                            def w_load(slot, m, signal):
                                sp.dma_start(w_nat[:, slot], w_rel[m].rearrange("(c p) d -> p c d", p=P)
                                             if isinstance(m, int) else
                                             w_rel[bass.ds(m, 1)].rearrange("a (c p) d -> p (a c) d", p=P)).then_inc(signal, 16)

                            def window(q, k):
                                at = sp.value_load(offs[0:1, bass.ds(4 * q + k, 1)], min_val=0, max_val=EDGES - CAP)
                                sp.dma_start(win_edges[:, k], edges_dram[bass.ds(at, CAP), :].rearrange("(p c) k -> p c k", c=CH)
                                             ).then_inc(win_loaded[k], 16)

                            w_load(0, R, wa_loaded)
                            for k in range(4):
                                window(0, k)
                            w_load(1, 0, wb_loaded)
                            with sp.Fori(1, NW // 4) as q:
                                for k in range(4):
                                    sp.wait_ge(onehot_ready, 4 * q + k - 3)
                                    window(q, k)
                            with sp.Fori(0, R - 1) as r:
                                sp.wait_ge(t_full, 13 * r + 4)
                                w_load(0, r + R + 1, wa_loaded)
                                sp.wait_ge(t_full, 13 * r + 11)
                                w_load(1, r + 1, wb_loaded)

                        @block.vector
                        def _(dve):
                            v = nc.vector
                            v.memset(zero_row[:].bitcast(F32), 0.0).then_inc(zero_ready, 1)

                            def window(q, k):
                                dve.wait_ge(win_loaded[k], 16 * q + 16)
                                if not (isinstance(q, int) and k < 2):
                                    dve.wait_ge(a_full, 4 * q + k - 1)
                                for c in range(CH):
                                    v.tensor_scalar(key_hot[:, k % 2, c], iota_row[:, 0:P], win_key[:, bass.ds(4 * q + k, 1)],
                                                    win_edges[:, k, c, 0:1], ALU.add, ALU.is_equal)
                                for c in range(CH):
                                    i = v.tensor_scalar(src_hot[:, k % 2, c, 0:N], iota_row[:, 0:N], win_edges[:, k, c, 1:2], None, ALU.is_equal)
                                i.then_inc(onehot_ready, 1)

                            def w_low(slot, dc, hi):
                                dve.wait_ge(wt_hi, hi)
                                v.tensor_tensor(wt_lo_sb[:, slot, dc], p_tr[:], wt_hi_sb[:, slot, dc].bitcast(F32),
                                                ALU.subtract).then_inc(wt_lo, 1)

                            def h_low(n, hi):
                                dve.wait_ge(h_hi, hi)
                                v.tensor_tensor(h_lo_sb[:, n % 2], p_h[0:TP, n % 2], h_hi_sb[:, n % 2].bitcast(F32),
                                                ALU.subtract).then_inc(h_lo, 1)

                            for dc in range(KC):
                                w_low(0, dc, dc + 1)
                            h_low(0, 1)
                            for k in range(4):
                                window(0, k)
                            with dve.Fori(1, NW // 4) as q:
                                for k in range(4):
                                    window(q, k)
                            v.tensor_scalar(offs[:, 0:NW], offs[:, 0:NW], float(CAP), None, ALU.add)

                            def steps(r, last):
                                for n in range(2 * T):
                                    if n < 2 * T - 1 or not last:
                                        h_low((n + 1), 10 * r + n + 2)
                                    if n < KC:
                                        w_low(1, n, 8 * r + 4 + n + 1)
                                    if n >= T and n < T + KC and not last:
                                        w_low(0, n - T, 8 * r + 8 + n - T + 1)

                            with dve.Fori(0, R - 1) as r:
                                steps(r, False)
                            steps(R - 1, True)
                            dve.wait_ge(deg_full, 1)
                            v.tensor_copy(degree_t[:, 0:4 * TP], p_tr[0:2 * R, 0:4 * TP])
                            v.tensor_copy(degree_t[:, 4 * TP:N], p_h[0:2 * R, 0, 0:TP]).then_inc(deg_copied, 1)
                            for t in range(T):
                                dve.wait_ge(agg_full, t + 1)
                                v.tensor_tensor(agg_sb[:, t], agg_sb[:, t], p_agg[0:TP, t], ALU.add).then_inc(agg_added, 1)

                        @block.scalar
                        def _(act):
                            s = nc.scalar

                            def w_high(slot, dc, full):
                                act.wait_ge(t_full, full)
                                s.copy(wt_hi_sb[:, slot, dc], p_tr[:]).then_inc(wt_hi, 1)

                            def h_high(n, full):
                                act.wait_ge(h_full, full)
                                s.copy(h_hi_sb[:, n % 2], p_h[0:TP, n % 2]).then_inc(h_hi, 1)

                            def a_direct(r, st):
                                s.activation(lhs_a[:, st], a16[:, st, r, 0:N] if isinstance(r, int) else a16[:, st, bass.ds(r, 1), 0:N].rearrange("p a n -> p (a n)"),
                                             ACT.Copy, accum_out=degree[:, st, bass.ds(r, 1)]).then_inc(a_ready, 1)

                            def a_turned(r, dt, full):
                                act.wait_ge(t_full, full)
                                s.activation(lhs_at[:, dt].rearrange("p (t n) -> p t n", t=T), p_tr16[:, :, 0:TP], ACT.Copy,
                                             accum_out=degree[:, dt, bass.ds(r + R, 1)]).then_inc(at_ready, 1)

                            for dc in range(KC):
                                w_high(0, dc, dc + 1)
                            h_high(0, 1)
                            with act.Fori(0, NW // 4) as q:
                                for k in range(4):
                                    act.wait_ge(a_full, 4 * q + k + 1)
                                    c = 1024 * (k % 2)
                                    s.copy(a16[:, :, :, bass.ds((4 * q + k) * WIN, WIN)],
                                           p_a[0:TP, c:c + T * P].rearrange("p (t r d) -> p t r d", t=T, r=R)).then_inc(a_stored, 1)
                            act.wait_ge(a_stored, NW)
                            for st in range(T):
                                a_direct(0, st)

                            def steps(r, last):
                                base = 13 * r + 4
                                g = 0
                                for n in range(2 * T):
                                    if n < 2 * T - 1 or not last:
                                        h_high(n + 1, 10 * r + n + 2)
                                    if n < KC:
                                        g += 1
                                        w_high(1, n, base + g)
                                    if n < T:
                                        g += 1
                                        a_turned(r, n, base + g)
                                    if n >= T and not last:
                                        if n < T + KC:
                                            g += 1
                                            w_high(0, n - T, base + g)
                                        a_direct(r + 1, n - T)

                            with act.Fori(0, R - 1) as r:
                                steps(r, False)
                            steps(R - 1, True)

                        @block.tensor
                        def _(pe):
                            m = nc.tensor

                            def w_turn(slot, dc):
                                for oc in range(4):
                                    i = m.transpose(p_tr[:, oc * P:(oc + 1) * P], w_nat[:, slot, oc, dc * P:(dc + 1) * P], ident[:])
                                i.then_inc(t_full, 1)
                                return i

                            def a_turn(r, dt):
                                for st in range(T):
                                    i = m.transpose(p_tr16[:, st, 0:TP],
                                                    a16[:, st, bass.ds(r, 1), dt * TP:(dt + 1) * TP].rearrange("p a n -> p (a n)"),
                                                    ident16[0:TP, 0:TP])
                                i.then_inc(t_full, 1)

                            def h_product(n):
                                split_product(m, p_h[0:TP, n % 2, :], xt_hi, xt_lo, wt_hi_sb, wt_lo_sb,
                                              (n // T) % 2, n % T, start=True, stop=True).then_inc(h_full, 1)

                            def add_messages(n):
                                lhs = lhs_a if n < T else lhs_at
                                for t in range(T):
                                    w = lhs[:, n % T, t * TP:(t + 1) * TP]
                                    m.matmul(p_agg[0:TP, t], w, h_hi_sb[:, n % 2], start=False, stop=False)
                                    i = m.matmul(p_agg[0:TP, t], w, h_lo_sb[:, n % 2], start=False, stop=False)

                            pe.wait_ge(wa_loaded, 16)
                            for dc in range(KC):
                                if dc:
                                    pe.wait_ge(wt_lo, dc)
                                w_turn(0, dc)
                            pe.wait_ge(wt_lo, KC)
                            h_product(0)

                            def window(q, k):
                                pe.wait_ge(onehot_ready, 4 * q + k + 1)
                                if not (isinstance(q, int) and k < 2):
                                    pe.wait_ge(a_stored, 4 * q + k - 1)
                                for st in range(T):
                                    for c in range(CH):
                                        o = 1024 * (k % 2) + st * P
                                        i = m.matmul(p_a[0:TP, o:o + P], src_hot[:, k % 2, c, st * TP:(st + 1) * TP],
                                                     key_hot[:, k % 2, c], start=(c == 0), stop=(c == CH - 1))
                                i.then_inc(a_full, 1)

                            for k in range(4):
                                window(0, k)
                            with pe.Fori(1, NW // 4) as q:
                                for k in range(4):
                                    window(q, k)
                            pe.wait_ge(a_stored, NW)
                            pe.wait_ge(zero_ready, 1)
                            for t in range(T):
                                m.matmul(p_agg[0:TP, t], zero_row[:, 0:TP], zero_row[:], start=True, stop=False)

                            def steps(r, last):
                                for n in range(2 * T):
                                    if n < 2 * T - 1 or not last:
                                        if n + 1 == T:
                                            pe.wait_ge(wt_lo, 8 * r + 8)
                                        if n + 1 == 2 * T:
                                            pe.wait_ge(wt_lo, 8 * r + 12)
                                        h_product((n + 1) % (2 * T))
                                    if n < KC:
                                        if n == 0:
                                            pe.wait_ge(wb_loaded, 16 * r + 16)
                                            pe.wait_ge(wt_lo, 8 * r + 4)
                                        else:
                                            pe.wait_ge(at_ready, 5 * r + n)
                                        w_turn(1, n)
                                    if T <= n < T + KC and not last:
                                        if n == T:
                                            pe.wait_ge(wa_loaded, 16 * r + 32)
                                            pe.wait_ge(at_ready, 5 * r + T)
                                        else:
                                            pe.wait_ge(wt_lo, 8 * r + 8 + n - T)
                                        w_turn(0, n - T)
                                    pe.wait_ge(h_lo, 10 * r + n + 1)
                                    if n < T:
                                        pe.wait_ge(a_ready, 5 * r + n + 1)
                                    else:
                                        pe.wait_ge(at_ready, 5 * r + n - T + 1)
                                    add_messages(n)
                                    if n < T:
                                        if n < KC:
                                            pe.wait_ge(wt_lo, 8 * r + 4 + n + 1)
                                        else:
                                            pe.wait_ge(at_ready, 5 * r + n)
                                        a_turn(r, n)

                            with pe.Fori(0, R - 1) as r:
                                steps(r, False)
                            steps(R - 1, True)
                            pe.wait_ge(at_ready, R * T)
                            pe.wait_ge(a_ready, R * T)
                            for t in range(T):
                                o = p_tr[0:2 * R, t * TP:(t + 1) * TP] if t < 4 else p_h[0:2 * R, 0, 0:TP]
                                i = m.transpose(o, degree[:, t], ident[0:TP, 0:TP])
                            i.then_inc(deg_full, 1)
                            pe.wait_ge(deg_copied, 1)
                            for t in range(T):
                                m.matmul(p_agg[0:TP, t], degree_t[:, t * TP:(t + 1) * TP], b_rel_sb[:],
                                         start=False, stop=True).then_inc(agg_full, 1)

                    nc.all_engine_barrier(sems_to_clear=round_sems)

            if stop == "gnn":
                with nc.Block() as block:
                    @block.vector
                    def _(dve):
                        for t in range(T):
                            nc.vector.scalar_tensor_tensor(x_sb[:, t], agg_sb[:, t], 0.0, x_sb[:, t], ALU.max, ALU.add).then_inc(agg_added, 1)

                    @block.sync
                    def _(sp):
                        sp.wait_ge(agg_added, T)
                        sp.dma_start(out.rearrange("(t p) d -> p t d", p=TP), x_sb[:]).then_inc(x_loaded, 16)
                        sp.wait_ge(x_loaded, 32)
                return

        w_dram = {"g": gate_w, "u": up_w, "d": down_w}
        with ExitStack() as g:
            stage = {"g": stage_gate[:], "u": sb("stage_up", [P, KC, F], F32, g)[:],
                     "d": sb("stage_down", [P, FC, D], F32, g)[:]}
            shape = {"g": [P, KC, F], "u": [P, KC, F], "d": [P, FC, D]}
            w_hi = {k: sb(f"{k}_hi_sb", shape[k], F32R, g) for k in "gud"}
            w_lo = {k: sb(f"{k}_lo_sb", shape[k], F32R, g) for k in "gud"}
            tokens = sb("tokens", [P, D], F32, g)
            slot_token = sb("slot_token", [P, NX * T], I32, g)
            column = sb("column", [P, 1], I32, g)
            xs_hi = sb("xs_hi", [P, KC, P], F32R, g)
            xs_lo = sb("xs_lo", [P, KC, P], F32R, g)
            silu = sb("silu", [P, F], F32, g)
            hid = sb("hid", [P, F], F32, g)
            hs_hi = sb("hs_hi", [P, FC, P], F32R, g)
            hs_lo = sb("hs_lo", [P, FC, P], F32R, g)
            y_sb = sb("y_sb", [P, D], F32, g)
            router_t = sb("router_t", [P, KC, NX], F32, g)
            logits = sb("logits", [TP, T, NX], F32, g)
            rest = sb("rest", [TP, T, NX], F32, g)
            cand = sb("cand", [TP, T, NX], F32, g)
            hot = sb("hot", [TP, 2, T, NX], F32, g)
            mask = sb("mask", [TP, T, NX], F32, g)
            best = sb("best", [TP, 2, T], F32, g)
            choice = sb("choice", [TP, 2, T], F32, g)
            rank = sb("rank", [TP, T + 1, NX], F32, g)
            picked = sb("picked", [TP, 2, T, NX], F32, g)
            place = sb("place", [TP, 2, T], F32, g)
            nth_tile = sb("nth_tile", [TP, 2, T], F32, g)
            tile_of = sb("tile_of", [TP, 2, T], F32, g)
            later = sb("later", [TP, 2, T], F32, g)
            step = sb("step", [TP, 2, T], F32, g)
            slot_at = sb("slot_at", [TP, 2 * T], I32, g)
            y_at = sb("y_at", [TP, 2 * T], I32, g)
            weight = sb("weight", [TP, 2, T], F32, g)
            gap = sb("gap", [TP, T], F32, g)
            extra = sb("extra", [TP, NX], F32, g)
            upto = sb("upto", [TP, 2, NX], F32, g)
            le = sb("le", [1, 2, MAXOV, NX], F32, g)
            over_f = sb("over_f", [1, 3, MAXOV], F32, g)
            over = sb("over", [1, 2 * MAXOV + 1], I32, g)

            xn2 = stage["d"].rearrange("p c d -> p (c d)")[0:TP, 0:T * D].rearrange("p (t d) -> p t d", t=T)
            xt2 = stage["u"].rearrange("p c f -> p (c f)")[:, 0:KC * N].rearrange("p (c n) -> p c n", c=KC)

            def w_piece(k, e, i):
                w = w_dram[k][e] if isinstance(e, int) else w_dram[k][bass.ds(e, 1)].rearrange("a r f -> (a r) f")
                rows = w.shape[0] // 2
                return w[i * rows:(i + 1) * rows, :].rearrange("(c p) f -> p c f", p=P)

            def half(ap, k, i):
                c = shape[k][1] // 2
                return ap[:, i * c:(i + 1) * c]

            with ExitStack() as f:
                p_gate = ps("p_gate", [P, F], F32, f)
                p_up = ps("p_up", [P, F], F32, f)
                p_ht = ps("p_ht", [P, F], F32, f)
                p_x = ps("p_x", [P, 512], F32, f)
                p_y = ps("p_y", [P, 512], F32, f)
                p_t = [p_gate[:], p_up[:]]
                p_router = p_y[:, 0:KC * NX].rearrange("p (c e) -> p c e", c=KC)
                p_logits = p_x[0:TP, 0:T * NX].rearrange("p (t e) -> p t e", t=T)
                p_rank = p_ht[0:TP, 0:(T + 1) * NX].rearrange("p (t e) -> p t e", t=T + 1)
                block = f.enter_context(nc.Block())

                @block.sync
                def _(sp):
                    def load(k, e, i):
                        sp.dma_start(half(stage[k], k, i), w_piece(k, e, i)).then_inc(loaded[k][i], 16)

                    sp.wait_ge(ln_ready, 2 * T)
                    sp.dma_start(ln2_dram.rearrange("(t p) d -> p t d", p=TP), xn2).then_inc(ln2_stored, 16)
                    sp.wait_ge(logits_full, T)
                    load("u", 0, 0)
                    load("u", 0, 1)
                    sp.wait_ge(ln2_stored, 16)
                    load("d", 0, 0)
                    load("d", 0, 1)
                    sp.wait_ge(slots_filled, 16 * 2 * T)
                    sp.dma_start(slot_token[:], slot_token_dram.rearrange("(p c) k -> p (c k)", p=P)).then_inc(slots_loaded, 16)

                    def reload(k, e):
                        for i in range(2):
                            sp.wait_ge(split_lo[k], 2 * e - 1 + i)
                            load(k, e, i)

                    reload("g", 1)
                    reload("u", 1)
                    reload("g", 2)
                    with sp.Fori(1, NX - 2) as e:
                        reload("u", e + 1)
                        reload("d", e)
                        reload("g", e + 2)
                    reload("u", NX - 1)
                    reload("d", NX - 2)
                    reload("d", NX - 1)

                @block.gpsimd
                def _(pool):
                    q = nc.gpsimd
                    pool.wait_ge(slots_cleared, 32)
                    pool.wait_ge(places_ready, 1)
                    for c in range(2 * T):
                        q.indirect_dma_start(slot_token_dram, bass.IndirectOffsetOnAxis(ap=slot_at[:, c:c + 1].bitcast(U32), axis=0),
                                             token_id[:, c % T:c % T + 1], None).then_inc(slots_filled, 16)
                    pool.wait_ge(slots_loaded, 16)
                    pool.wait_ge(ln2_stored, 16)

                    def gather(e):
                        q.tensor_copy(column[:], slot_token[:, bass.ds(T * e, 1)]).then_inc(column_copied, 1)
                        pool.wait_ge(column_copied, e + 1)
                        pool.sem_inc(column_waited, 1)
                        q.indirect_dma_start(tokens[:], None, ln2_dram, bass.IndirectOffsetOnAxis(ap=column[:].bitcast(U32), axis=0)
                                             ).then_inc(tokens_loaded, 16)

                    gather(0)
                    with pool.Fori(1, NX) as e:
                        pool.wait_ge(xt_full, e)
                        gather(e)

                @block.vector
                def _(dve):
                    v = nc.vector
                    for t in range(T):
                        i = v.scalar_tensor_tensor(x_sb[:, t], agg_sb[:, t], 0.0, x_sb[:, t], ALU.max, ALU.add)
                    link("dve", dve, i)
                    normalize(dve, x_sb, xn2, 1)
                    dve.wait_ge(router_full, 1)
                    v.tensor_copy(router_t[:], p_router).then_inc(router_copied, 1)
                    for dc in range(0, KC, 2):
                        dve.wait_ge(x2_full, dc + 1)
                        v.tensor_copy(xt2[:, dc, 0:4 * TP], p_t[0][:, 0:4 * TP])
                        v.tensor_copy(xt2[:, dc, 4 * TP:N], p_t[0][:, 512:512 + TP]).then_inc(x2_even, 1)
                    dve.wait_ge(logits_full, T)
                    link("dve", dve, v.tensor_copy(logits[:], p_logits))
                    iota = expert_iota[:].unsqueeze(1).to_broadcast([TP, T, NX])

                    def wide(a):
                        return a.unsqueeze(2).to_broadcast([TP, T, NX])

                    for c in range(2):
                        src_logits = logits if c == 0 else rest
                        link("dve", dve, v.tensor_reduce(best[:, c], src_logits[:], AX.X, ALU.max))
                        link("dve", dve, v.tensor_tensor(cand[:], src_logits[:], wide(best[:, c]), ALU.not_equal))
                        link("dve", dve, v.scalar_tensor_tensor(cand[:], cand[:], float(NX), iota, ALU.mult, ALU.add))
                        link("dve", dve, v.tensor_reduce(choice[:, c], cand[:], AX.X, ALU.min))
                        link("dve", dve, v.tensor_tensor(hot[:, c], iota, wide(choice[:, c]), ALU.is_equal))
                        if c == 0:
                            link("dve", dve, v.scalar_tensor_tensor(rest[:], hot[:, 0], -3.0e38, logits[:], ALU.mult, ALU.add))
                    v.tensor_tensor(mask[:], hot[:, 0], hot[:, 1], ALU.add).then_inc(mask_ready, 1)
                    v.tensor_tensor(gap[:], best[:, 1], best[:, 0], ALU.subtract).then_inc(gap_ready, 1)
                    dve.wait_ge(exp_ready, 1)
                    link("dve", dve, v.tensor_scalar(best[:, 0], gap[:], 1.0, None, ALU.add))
                    link("dve", dve, v.reciprocal(weight[:, 0], best[:, 0]))
                    v.tensor_tensor(weight[:, 1], weight[:, 0], gap[:], ALU.mult)
                    dve.wait_ge(rank_full, 1)
                    link("dve", dve, v.tensor_copy(rank[:], p_rank))
                    for c in range(2):
                        i = v.tensor_tensor(picked[:, c], hot[:, c], rank[:, 0:T], ALU.mult)
                    link("dve", dve, i)
                    link("dve", dve, v.tensor_reduce(place[:], picked[:], AX.X, ALU.add))
                    link("dve", dve, v.tensor_scalar(nth_tile[:], place[:], float(P), None, ALU.is_ge))
                    for k in range(2, T):
                        link("dve", dve, v.scalar_tensor_tensor(nth_tile[:], place[:], float(k * P), nth_tile[:], ALU.is_ge, ALU.add))
                    link("dve", dve, v.scalar_tensor_tensor(step[:], nth_tile[:], -float(P), place[:], ALU.mult, ALU.add))
                    link("dve", dve, v.scalar_tensor_tensor(tile_of[:], choice[:], float(T), nth_tile[:], ALU.mult, ALU.add))
                    v.scalar_tensor_tensor(slot_at[:].rearrange("p (c t) -> p c t", c=2), step[:], float(NX * T), tile_of[:], ALU.mult, ALU.add).then_inc(places_ready, 1)
                    n_tok, n_extra, cum = rank[:, T], extra[:], upto
                    link("dve", dve, v.tensor_scalar(n_extra, n_tok, float(P), None, ALU.is_gt))
                    for k in range(2, T):
                        link("dve", dve, v.scalar_tensor_tensor(n_extra, n_tok, float(k * P), n_extra, ALU.is_gt, ALU.add))
                    link("dve", dve, v.tensor_copy(cum[:, 0], n_extra))
                    for k, shift in enumerate((1, 2, 4, 8)):
                        a, b = cum[:, k % 2], cum[:, (k + 1) % 2]
                        v.tensor_copy(b[:, 0:shift], a[:, 0:shift])
                        link("dve", dve, v.tensor_tensor(b[:, shift:NX], a[:, shift:NX], a[:, 0:NX - shift], ALU.add))
                    link("dve", dve, v.tensor_tensor(n_extra, cum[:, 0], n_extra, ALU.subtract))
                    for c in range(2):
                        i = v.tensor_tensor(picked[:, c], hot[:, c], n_extra.unsqueeze(1).to_broadcast([TP, T, NX]), ALU.mult)
                    link("dve", dve, i)
                    link("dve", dve, v.tensor_reduce(later[:], picked[:], AX.X, ALU.add))
                    link("dve", dve, v.tensor_tensor(later[:], later[:], nth_tile[:], ALU.add))
                    link("dve", dve, v.scalar_tensor_tensor(later[:], later[:], float(NX - 1), choice[:], ALU.add, ALU.subtract))
                    link("dve", dve, v.scalar_tensor_tensor(later[:], nth_tile[:], 0.0, later[:], ALU.is_gt, ALU.mult))
                    link("dve", dve, v.tensor_tensor(later[:], later[:], choice[:], ALU.add))
                    v.scalar_tensor_tensor(y_at[:].rearrange("p (c t) -> p c t", c=2), later[:], float(P), step[:], ALU.mult, ALU.add)
                    ends = cum[0:1, 0].unsqueeze(1).to_broadcast([1, MAXOV, NX])
                    nth = tile_iota[:].unsqueeze(2).to_broadcast([1, MAXOV, NX])
                    link("dve", dve, v.tensor_tensor(le[:, 0], ends, nth, ALU.is_le))
                    link("dve", dve, v.tensor_tensor(le[:, 1], le[:, 0], ends, ALU.mult))
                    v.tensor_reduce(over_f[:, 0], le[:, 0], AX.X, ALU.add)
                    link("dve", dve, v.tensor_reduce(over_f[:, 1], le[:, 1], AX.X, ALU.max))
                    link("dve", dve, v.tensor_tensor(over_f[:, 2], tile_iota[:], over_f[:, 1], ALU.subtract))
                    v.tensor_scalar(over[:, 0:MAXOV], over_f[:, 0], float(NX - 1), None, ALU.min)
                    v.tensor_scalar(over[:, MAXOV:2 * MAXOV], over_f[:, 2], 1.0, None, ALU.add)
                    v.tensor_copy(over[:, 2 * MAXOV:2 * MAXOV + 1], cum[0:1, 0, NX - 1:NX])

                    def low(k, e, i):
                        dve.wait_ge(split_hi[k], 2 * e + i + 1)
                        v.tensor_tensor(half(w_lo[k][:], k, i), half(stage[k], k, i), half(w_hi[k][:], k, i).bitcast(F32),
                                        ALU.subtract).then_inc(split_lo[k], 1)

                    def x_low(e):
                        dve.wait_ge(xt_hi_ready, e + 1)
                        v.tensor_tensor(xs_lo[:].rearrange("p c n -> p (c n)"), p_x[:], xs_hi[:].rearrange("p c n -> p (c n)").bitcast(F32),
                                        ALU.subtract).then_inc(xt_lo_ready, 1)

                    def hidden(e):
                        dve.wait_ge(done["u"], e + 1)
                        for i in range(2):
                            dve.wait_ge(silu_ready, 2 * e + i + 1)
                            v.tensor_tensor(hid[:, i * 512:(i + 1) * 512], silu[:, i * 512:(i + 1) * 512], p_up[:, i * 512:(i + 1) * 512],
                                            ALU.mult).then_inc(hid_ready, 1)

                    def h_low(e):
                        for i in range(2):
                            dve.wait_ge(ht_hi_ready, 2 * e + i + 1)
                            v.tensor_tensor(hs_lo[:, 4 * i:4 * i + 4].rearrange("p c n -> p (c n)"), p_ht[:, i * 512:(i + 1) * 512],
                                            hs_hi[:, 4 * i:4 * i + 4].rearrange("p c n -> p (c n)").bitcast(F32),
                                            ALU.subtract).then_inc(ht_lo_ready, 1)

                    for k in "gu":
                        low(k, 0, 0)
                        low(k, 0, 1)
                    x_low(0)
                    low("g", 1, 0)
                    low("g", 1, 1)
                    x_low(1)

                    def body(e, first, last):
                        hidden(e - 1)
                        low("u", e, 0)
                        low("u", e, 1)
                        h_low(e - 1)
                        low("d", e - 1, 0)
                        low("d", e - 1, 1)
                        if not last:
                            low("g", e + 1, 0)
                            low("g", e + 1, 1)
                            x_low(e + 1)

                    body(1, True, False)
                    with dve.Fori(2, NX - 1) as e:
                        body(e, False, False)
                    body(NX - 1, False, True)
                    hidden(NX - 1)
                    h_low(NX - 1)
                    low("d", NX - 1, 0)
                    low("d", NX - 1, 1)

                @block.scalar
                def _(act):
                    s = nc.scalar
                    roots(act, 1)
                    for dc in range(1, KC, 2):
                        act.wait_ge(x2_full, dc + 1)
                        s.copy(xt2[:, dc, 0:4 * TP], p_t[1][:, 0:4 * TP])
                        s.copy(xt2[:, dc, 4 * TP:N], p_t[1][:, 512:512 + TP]).then_inc(x2_odd, 1)
                    act.wait_ge(gap_ready, 1)
                    s.activation(gap[:], gap[:], ACT.Exp).then_inc(exp_ready, 1)

                    def high(k, e, i):
                        act.wait_ge(loaded[k][i], 16 * e + 16)
                        s.copy(half(w_hi[k][:], k, i), half(stage[k], k, i)).then_inc(split_hi[k], 1)

                    def x_high(e):
                        act.wait_ge(xt_full, e + 1)
                        s.copy(xs_hi[:].rearrange("p c n -> p (c n)"), p_x[:]).then_inc(xt_hi_ready, 1)

                    def silus(e):
                        act.wait_ge(done["g"], e + 1)
                        for i in range(2):
                            s.activation(silu[:, i * 512:(i + 1) * 512], p_gate[:, i * 512:(i + 1) * 512], ACT.Silu).then_inc(silu_ready, 1)

                    def h_high(e):
                        for i in range(2):
                            act.wait_ge(ht_full, 2 * e + i + 1)
                            s.copy(hs_hi[:, 4 * i:4 * i + 4].rearrange("p c n -> p (c n)"), p_ht[:, i * 512:(i + 1) * 512]).then_inc(ht_hi_ready, 1)

                    def y_copy(e, first):
                        act.wait_ge(done["d"], e + 1)
                        if not first:
                            act.wait_ge(y_stored, 16 * e)
                        s.copy(y_sb[:], p_y[:]).then_inc(y_copied, 1)
                        act.wait_ge(y_copied, e + 1)
                        act.dma_start(y_dram[bass.ds(e * P, P), :], y_sb[:]).then_inc(y_stored, 16)

                    for k in "gu":
                        high(k, 0, 0)
                        high(k, 0, 1)
                    x_high(0)
                    silus(0)
                    high("g", 1, 0)
                    high("g", 1, 1)
                    x_high(1)

                    def body(e, first, last):
                        if not first:
                            y_copy(e - 2, False) if not isinstance(e, int) or e > 2 else y_copy(e - 2, True)
                        act.wait_ge(done["u"], e)
                        high("u", e, 0)
                        high("u", e, 1)
                        act.wait_ge(hid_ready, 2 * e)
                        silus(e)
                        h_high(e - 1)
                        if not first:
                            act.wait_ge(done["d"], e - 1)
                        high("d", e - 1, 0)
                        high("d", e - 1, 1)
                        if not last:
                            act.wait_ge(done["g"], e + 1)
                            high("g", e + 1, 0)
                            high("g", e + 1, 1)
                            x_high(e + 1)

                    body(1, True, False)
                    body(2, False, False)
                    with act.Fori(3, NX - 1) as e:
                        body(e, False, False)
                    body(NX - 1, False, True)
                    y_copy(NX - 2, False)
                    h_high(NX - 1)
                    high("d", NX - 1, 0)
                    high("d", NX - 1, 1)
                    y_copy(NX - 1, False)
                    act.wait_ge(y_stored, 16 * NX)

                @block.tensor
                def _(pe):
                    m = nc.tensor
                    for dc in range(KC):
                        i = m.transpose(p_router[:, dc], router_sb[:, dc * P:(dc + 1) * P], ident[0:NX, 0:NX])
                    i.then_inc(router_full, 1)
                    pe.wait_ge(ln_ready, 2 * T)
                    for dc in range(KC):
                        if dc >= 2:
                            pe.wait_ge(x2_even if dc == 2 else x2_odd, 1)
                        for t in range(T):
                            c = t * TP if t < 4 else 512
                            i = m.transpose(p_t[dc % 2][:, c:c + TP], xn2[:, t, dc * P:(dc + 1) * P], ident[0:TP, 0:TP])
                        i.then_inc(x2_full, 1)
                    pe.wait_ge(x2_even, 2)
                    pe.wait_ge(x2_odd, 2)
                    pe.wait_ge(router_copied, 1)
                    for t in range(T):
                        for dc in range(KC):
                            i = m.matmul(p_logits[:, t], xt2[:, dc, t * TP:(t + 1) * TP], router_t[:, dc],
                                         start=(dc == 0), stop=(dc == KC - 1))
                        i.then_inc(logits_full, 1)
                    pe.wait_ge(mask_ready, 1)
                    for t in range(T + 1):
                        for k in range(min(t + 1, T)):
                            i = m.matmul(p_rank[:, t], before[:] if k == t else ones[0:TP, 0:TP], mask[:, k],
                                         start=(k == 0), stop=(k == min(t, T - 1)))
                    i.then_inc(rank_full, 1)

                    def wide_product(k, e, into):
                        for c in range(KC):
                            if c % 2 == 0:
                                pe.wait_ge(split_lo[k], 2 * e + c // 2 + 1)
                            for x_part, w_part in ((xs_hi, w_hi), (xs_hi, w_lo), (xs_lo, w_hi)):
                                for h in range(2):
                                    i = m.matmul(into[:, h * 512:(h + 1) * 512], x_part[:, c], w_part[k][:, c, h * 512:(h + 1) * 512],
                                                 start=(c == 0 and x_part is xs_hi and w_part is w_hi),
                                                 stop=(c == KC - 1 and x_part is xs_lo))
                        i.then_inc(done[k], 1)

                    def turn_tokens(e):
                        pe.wait_ge(tokens_loaded, 16 * e + 16)
                        for c in range(KC):
                            i = m.transpose(p_x[:, c * P:(c + 1) * P], tokens[:, c * P:(c + 1) * P], ident[:])
                        i.then_inc(xt_full, 1)

                    def turn_hidden(e):
                        for h in range(2):
                            pe.wait_ge(hid_ready, 2 * e + h + 1)
                            for c in range(4 * h, 4 * h + 4):
                                i = m.transpose(p_ht[:, c * P:(c + 1) * P], hid[:, c * P:(c + 1) * P], ident[:])
                            i.then_inc(ht_full, 1)

                    def down(e, first):
                        if not first:
                            pe.wait_ge(y_copied, e)
                        for c in range(FC):
                            if c % 4 == 0:
                                pe.wait_ge(ht_lo_ready, 2 * e + c // 4 + 1)
                                pe.wait_ge(split_lo["d"], 2 * e + c // 4 + 1)
                            m.matmul(p_y[:], hs_hi[:, c], w_hi["d"][:, c], start=(c == 0), stop=False)
                            m.matmul(p_y[:], hs_hi[:, c], w_lo["d"][:, c], start=False, stop=False)
                            i = m.matmul(p_y[:], hs_lo[:, c], w_hi["d"][:, c], start=False, stop=(c == FC - 1))
                        i.then_inc(done["d"], 1)

                    turn_tokens(0)
                    pe.wait_ge(xt_lo_ready, 1)
                    wide_product("g", 0, p_gate)
                    wide_product("u", 0, p_up)
                    turn_tokens(1)

                    def body(e, first, last):
                        pe.wait_ge(xt_lo_ready, e + 1)
                        pe.wait_ge(silu_ready, 2 * e)
                        wide_product("g", e, p_gate)
                        turn_hidden(e - 1)
                        wide_product("u", e, p_up)
                        if not last:
                            turn_tokens(e + 1)
                        down(e - 1, first)

                    body(1, True, False)
                    with pe.Fori(2, NX - 1) as e:
                        body(e, False, False)
                    body(NX - 1, False, True)
                    turn_hidden(NX - 1)
                    down(NX - 1, False)

            with ExitStack() as f:
                x_whole = sb("x_whole", [P, KC, P], F32, f)
                h_whole = sb("h_whole", [P, FC, P], F32, f)
                p_gate = ps("p_gate2", [P, F], F32, f)
                p_up = ps("p_up2", [P, F], F32, f)
                p_ht = ps("p_ht2", [P, F], F32, f)
                p_x = ps("p_x2", [P, 512], F32, f)
                p_y = ps("p_y2", [P, 512], F32, f)
                tiles = nc.values_load(over[0:1, 2 * MAXOV:2 * MAXOV + 1], min_val=0, max_val=MAXOV)
                with nc.If(tiles > 0):
                    with nc.Fori(0, tiles) as nth:
                        with nc.Block() as block:
                            @block.sync
                            def _(sp):
                                e = sp.value_load(over[0:1, bass.ds(nth, 1)], min_val=0, max_val=NX - 1)
                                for k in "gud":
                                    for i in range(2):
                                        sp.dma_start(half(stage[k], k, i), w_piece(k, e, i)).then_inc(o_loaded[k], 16)
                                sp.wait_ge(o_y, 1)
                                sp.dma_start(y_dram[bass.ds((nth + NX) * P, P), :], y_sb[:]).then_inc(o_stored, 16)
                                sp.wait_ge(o_stored, 16)

                            @block.gpsimd
                            def _(pool):
                                e = pool.value_load(over[0:1, bass.ds(nth, 1)], min_val=0, max_val=NX - 1)
                                j = pool.value_load(over[0:1, bass.ds(nth + MAXOV, 1)], min_val=1, max_val=T - 1)
                                nc.gpsimd.tensor_copy(column[:], slot_token[:, bass.ds(T * e + j, 1)]).then_inc(o_column, 1)
                                pool.wait_ge(o_column, 1)
                                nc.gpsimd.indirect_dma_start(tokens[:], None, ln2_dram, bass.IndirectOffsetOnAxis(ap=column[:].bitcast(U32), axis=0)
                                                             ).then_inc(o_tokens, 16)

                            @block.vector
                            def _(dve):
                                dve.wait_ge(o_up, 1)
                                dve.wait_ge(o_silu, 1)
                                nc.vector.tensor_tensor(hid[:], silu[:], p_up[:], ALU.mult).then_inc(o_hid, 1)
                                dve.wait_ge(o_ht_full, 1)
                                nc.vector.tensor_copy(h_whole[:].rearrange("p c n -> p (c n)"), p_ht[:]).then_inc(o_ht, 1)

                            @block.scalar
                            def _(act):
                                act.wait_ge(o_xt_full, 1)
                                nc.scalar.copy(x_whole[:].rearrange("p c n -> p (c n)"), p_x[:]).then_inc(o_xt, 1)
                                act.wait_ge(o_gate, 1)
                                nc.scalar.activation(silu[:], p_gate[:], ACT.Silu).then_inc(o_silu, 1)
                                act.wait_ge(o_y_full, 1)
                                nc.scalar.copy(y_sb[:], p_y[:]).then_inc(o_y, 1)

                            @block.tensor
                            def _(pe):
                                m = nc.tensor
                                pe.wait_ge(o_tokens, 16 * nth + 16)
                                for c in range(KC):
                                    i = m.transpose(p_x[:, c * P:(c + 1) * P], tokens[:, c * P:(c + 1) * P], ident[:])
                                i.then_inc(o_xt_full, 1)
                                pe.wait_ge(o_xt, 1)
                                for k, into, signal in (("g", p_gate, o_gate), ("u", p_up, o_up)):
                                    pe.wait_ge(o_loaded[k], 32)
                                    for c in range(KC):
                                        for h in range(2):
                                            i = m.matmul(into[:, h * 512:(h + 1) * 512], x_whole[:, c], stage[k][:, c, h * 512:(h + 1) * 512],
                                                         start=(c == 0), stop=(c == KC - 1))
                                    i.then_inc(signal, 1)
                                pe.wait_ge(o_hid, 1)
                                for c in range(FC):
                                    i = m.transpose(p_ht[:, c * P:(c + 1) * P], hid[:, c * P:(c + 1) * P], ident[:])
                                i.then_inc(o_ht_full, 1)
                                pe.wait_ge(o_ht, 1)
                                pe.wait_ge(o_loaded["d"], 32)
                                for c in range(FC):
                                    i = m.matmul(p_y[:], h_whole[:, c], stage["d"][:, c], start=(c == 0), stop=(c == FC - 1))
                                i.then_inc(o_y_full, 1)

                        nc.all_engine_barrier(sems_to_clear=over_sems)

            with ExitStack() as f:
                rows = [stage["g"].rearrange("p c f -> p (c f)")[0:TP, 0:T * D].rearrange("p (t d) -> p t d", t=T),
                        stage["u"].rearrange("p c f -> p (c f)")[0:TP, 0:T * D].rearrange("p (t d) -> p t d", t=T)]
                block = f.enter_context(nc.Block())

                @block.gpsimd
                def _(pool):
                    for t in range(T):
                        for c, signal in enumerate((first_loaded, second_loaded)):
                            nc.gpsimd.indirect_dma_start(rows[c][:, t], None, y_dram,
                                                         bass.IndirectOffsetOnAxis(ap=y_at[:, c * T + t:c * T + t + 1].bitcast(U32), axis=0)
                                                         ).then_inc(signal[t], 16)

                @block.vector
                def _(dve):
                    v = nc.vector
                    for t in range(T):
                        dve.wait_ge(first_loaded[t], 16)
                        link("dve", dve, v.scalar_tensor_tensor(x_sb[:, t], rows[0][:, t], weight[:, 0, t:t + 1], x_sb[:, t], ALU.mult, ALU.add))
                        dve.wait_ge(second_loaded[t], 16)
                        v.scalar_tensor_tensor(x_sb[:, t], rows[1][:, t], weight[:, 1, t:t + 1], x_sb[:, t], ALU.mult, ALU.add).then_inc(combined, 1)

                @block.sync
                def _(sp):
                    for t in range(T):
                        sp.wait_ge(combined, t + 1)
                        sp.dma_start(out[t * TP:(t + 1) * TP, :], x_sb[:, t]).then_inc(out_stored, 16)
                    sp.wait_ge(out_stored, 16 * T)


def split_product(m, o, xt_hi, xt_lo, wt_hi_sb, wt_lo_sb, slot, t, start, stop):
    for dc in range(KC):
        x_hi, x_lo = xt_hi[:, dc, t * TP:(t + 1) * TP], xt_lo[:, dc, t * TP:(t + 1) * TP]
        m.matmul(o, x_hi, wt_hi_sb[:, slot, dc], start=start and dc == 0, stop=False)
        m.matmul(o, x_hi, wt_lo_sb[:, slot, dc], start=False, stop=False)
        i = m.matmul(o, x_lo, wt_hi_sb[:, slot, dc], start=False, stop=stop and dc == KC - 1)
    return i


NAMES = ["x", "src", "dst", "edge_type_8", "L0_gnn_W_self", "L0_gnn_b_self", "L0_gnn_W_rel", "L0_gnn_b_rel",
         "L0_ffn_router_w", "L0_ffn_gate_w", "L0_ffn_up_w", "L0_ffn_down_w"]


def kernel(**inputs):
    import numpy as np
    from concourse import bacc
    from concourse.bass_utils import run_bass_kernel_spmd

    nc = bacc.Bacc("TRN2", target_bir_lowering=False, num_devices=1)
    arrays = {f"in_{n}": np.ascontiguousarray(inputs[n]) for n in NAMES}
    args = [nc.dram_tensor(n, a.shape, mybir.dt.from_np(a.dtype), kind="ExternalInput").ap() for n, a in arrays.items()]
    out = nc.dram_tensor("out", (N, D), F32, kind="ExternalOutput").ap()
    build(nc, *args, out)
    result = run_bass_kernel_spmd(nc, [arrays], core_ids=[0])
    return result.results[0]["out"]
```

```python
from contextlib import ExitStack

import concourse.bass as bass
from concourse import mybir

F32 = mybir.dt.float32
F32R = mybir.dt.float32r
F16 = mybir.dt.float16
I32 = mybir.dt.int32
U32 = mybir.dt.uint32
ALU = mybir.AluOpType
ACT = mybir.ActivationFunctionType
AX = mybir.AxisListType

P = 128
N, D = 625, 512
TP, T = 125, 5
KC = D // P
R = 8
E = 10625
EP, EC = 125, 85
WIN = 16
NW = 40
NPAD = NW * WIN
CH = 3
CAP = CH * P
ROUNDS = -(-E // CAP)
EDGES = 87 * P
KEY = 1024
NX, F = 16, 1024
SLOTS = T * P
FC = F // P
MAXOV = (2 * N - NX) // P
TILES = NX + MAXOV
B_SELF = 32
LN_EPS = 1e-5


def build(nc, x, src, dst, edge_type, w_self, b_self, w_rel, b_rel, router_w, gate_w, up_w, down_w, out):
    ctx = ExitStack()
    with ctx:
        def sb(name, shape, dt, c=ctx):
            return c.enter_context(nc.sbuf_tensor(name, shape, dt))

        def ps(name, shape, dt, c):
            return c.enter_context(nc.psum_tensor(name, shape, dt))

        def sem(name):
            return ctx.enter_context(nc.semaphore(name))

        edges_dram = nc.dram_tensor("edges_dram", [EDGES, 2], F32).ap()
        ln2_dram = nc.dram_tensor("ln2_dram", [N, D], F32).ap()
        y_dram = nc.dram_tensor("y_dram", [TILES * P, D], F32).ap()

        ident = sb("ident", [P, P], F32)
        ident16 = sb("ident16", [P, P], F16)
        ones = sb("ones", [P, P], F32)
        x_sb = sb("x_sb", [TP, T, D], F32)
        agg_sb = sb("agg_sb", [TP, T, D], F32)
        stats = sb("stats", [TP, T, 6], F32)
        meanvar = sb("meanvar", [TP, T, 2], F32)
        rstd = sb("rstd", [TP, T], F32)
        stage_gate = sb("stage_gate", [P, KC, F], F32)
        before = sb("before", [TP, TP], F16)
        ones16 = sb("ones16", [TP, TP], F16)
        slot_iota = sb("slot_iota", [TP, P], F16)
        expert_iota = sb("expert_iota", [TP, NX], F32)
        token_id = sb("token_id", [TP, T], F32)
        router_sb = sb("router_sb", [NX, D], F32)

        chain = {e: sem(f"{e}_chain") for e in ("dve", "act", "pool")}
        consts_ready = sem("consts_ready")
        x_loaded = sem("x_loaded")
        edge_loaded = sem("edge_loaded")
        small_loaded = sem("small_loaded")
        first_w_loaded = sem("first_w_loaded")
        edges_packed, edges_stored = sem("edges_packed"), sem("edges_stored")
        var_ready, root_ready, ln_ready = sem("var_ready"), sem("root_ready"), sem("ln_ready")
        tr_full, tr_hi, tr_lo = sem("tr_full"), sem("tr_hi"), sem("tr_lo")
        count_ready, count_full = sem("count_ready"), sem("count_full")

        zero_ready = sem("zero_ready")
        next_w_loaded = sem("next_w_loaded")
        self_full, self_added = sem("self_full"), sem("self_added")
        win_loaded = [sem(f"win_loaded{i}") for i in range(4)]
        onehot_ready, a_full, a_stored = sem("onehot_ready"), sem("a_full"), sem("a_stored")
        wa_loaded, wb_loaded = sem("wa_loaded"), sem("wb_loaded")
        t_full, wt_hi, wt_lo = sem("t_full"), sem("wt_hi"), sem("wt_lo")
        a_ready, at_ready = sem("a_ready"), sem("at_ready")
        h_full, h_hi, h_lo = sem("h_full"), sem("h_hi"), sem("h_lo")
        deg_full, deg_copied, agg_full = sem("deg_full"), sem("deg_copied"), sem("agg_full")
        agg_added = sem("agg_added")
        round_sems = range(zero_ready.num, agg_added.num + 1)
        assert len(round_sems) == 25

        route_consts = sem("route_consts")
        later_cleared = sem("later_cleared")
        router_full, router_copied = sem("router_full"), sem("router_copied")
        x2_full, x2_copied, logits_full = sem("x2_full"), sem("x2_copied"), sem("logits_full")
        ln2_stored, gap_ready, exp_ready = sem("ln2_stored"), sem("gap_ready"), sem("exp_ready")
        mask_ready, rank_full, places_ready = sem("mask_ready"), sem("rank_full"), sem("places_ready")
        slots_full, slots_ready, list_ready = sem("slots_full"), sem("slots_ready"), sem("list_ready")
        loaded = {k: [sem(f"{k}{i}_loaded") for i in range(2)] for k in "gud"}
        split_hi = {k: sem(f"{k}_hi") for k in "gud"}
        split_lo = {k: sem(f"{k}_lo") for k in "gud"}
        done = {k: sem(f"{k}_done") for k in "gud"}
        column_copied, column_waited, tokens_loaded = sem("column_copied"), sem("column_waited"), sem("tokens_loaded")
        xt_full, xt_hi_ready, xt_lo_ready = sem("xt_full"), sem("xt_hi_ready"), sem("xt_lo_ready")
        silu_ready, hid_ready = sem("silu_ready"), sem("hid_ready")
        ht_full, ht_hi_ready, ht_lo_ready = sem("ht_full"), sem("ht_hi_ready"), sem("ht_lo_ready")
        y_copied, y_stored, all_stored = sem("y_copied"), sem("y_stored"), sem("all_stored")
        first_loaded = [sem(f"first_loaded{t}") for t in range(T)]
        second_loaded = [sem(f"second_loaded{t}") for t in range(T)]
        combined, out_stored = sem("combined"), sem("out_stored")

        steps_done = {"dve": 0, "act": 0, "pool": 0}

        def link(name, engine, instruction):
            steps_done[name] += 1
            instruction.then_inc(chain[name], 1)
            engine.wait_ge(chain[name], steps_done[name])

        def normalize(dve, xs, xn, nth):
            v = nc.vector
            for t in range(T):
                i = v.bn_stats(stats[:, t], xs[:, t])
            link("dve", dve, i)
            for t in range(T):
                i = v.bn_aggr(meanvar[:, t], stats[:, t])
            link("dve", dve, i)
            v.tensor_scalar(rstd[:], meanvar[:, :, 1], LN_EPS, None, ALU.add).then_inc(var_ready, 1)
            dve.wait_ge(root_ready, nth + 1)
            link("dve", dve, v.reciprocal(rstd[:], rstd[:]))
            for t in range(T):
                v.tensor_scalar(xn[:, t], xs[:, t], meanvar[:, t, 0:1], rstd[:, t:t + 1],
                                ALU.subtract, ALU.mult).then_inc(ln_ready, 1)

        def roots(act, nth):
            act.wait_ge(var_ready, nth + 1)
            nc.scalar.activation(rstd[:], rstd[:], ACT.Sqrt).then_inc(root_ready, 1)

        with ExitStack() as g:
            a16 = sb("a16", [TP, T, R, NPAD], F16, g)
            xt_hi = sb("xt_hi", [P, KC, N], F32R, g)
            xt_lo = sb("xt_lo", [P, KC, N], F32R, g)
            w_nat = sb("w_nat", [P, 2, 4, D], F32, g)
            wt_hi_sb = sb("wt_hi_sb", [P, 2, KC, D], F32R, g)
            wt_lo_sb = sb("wt_lo_sb", [P, 2, KC, D], F32R, g)
            iota_row = sb("iota_row", [P, NPAD], F16, g)
            win_key = sb("win_key", [P, NW], F32, g)
            offs = sb("offs", [1, NW + 1], I32, g)
            bias = sb("bias", [B_SELF + 1, D], F32, g)
            first = sb("first", [P, 1], F32, g)

            def load_first(sp, slot, signal):
                sp.dma_start(w_nat[:, slot], (w_self if slot else w_rel[R]).rearrange("(c p) d -> p c d", p=P)).then_inc(signal, 16)

            with ExitStack() as f:
                xn = sb("xn", [TP, T, D], F32, f)
                iota_i = sb("iota_i", [P, NPAD], I32, f)
                e_src = sb("e_src", [EP, EC], I32, f)
                e_dst = sb("e_dst", [EP, EC + 1], I32, f)
                e_type = sb("e_type", [EP, EC], I32, f)
                e_win = sb("e_win", [EP, EC], I32, f)
                e_winf = sb("e_winf", [EP, EC], F32, f)
                e_in = sb("e_in", [EP, EC], I32, f)
                e_key = sb("e_key", [EP, EC], F32, f)
                e_pack = sb("e_pack", [EP, EC, 2], F32, f)
                e_pad = sb("e_pad", [7, 73, 2], F32, f)
                below = sb("below", [EP, NW + 1, EC], F32, f)
                win_f = sb("win_f", [EP, NW + 1], F32, f)
                counts = sb("counts", [EP, NW + 2], F32, f)
                crow = sb("crow", [1, NW + 2], F32, f)
                cdiff = sb("cdiff", [1, NW], F32, f)
                flags = sb("flags", [1, 4], F32, f)
                zero_rows = sb("zero_rows", [P, D], F32, f)
                token_id_i = sb("token_id_i", [TP, T], I32, f)
                expert_iota_i = sb("expert_iota_i", [TP, NX], I32, f)
                p_t = ps("p_t", [P, T, 512], F32, f)
                p_count = ps("p_count", [P, 512], F32, f)


                def token_columns(a, t):
                    return a[:, :, t * TP:(t + 1) * TP]

                def turned(t):
                    return p_t[:, t, 0:KC * TP].rearrange("p (c n) -> p c n", c=KC)

                block = f.enter_context(nc.Block())

                @block.sync
                def _(sp):
                    sp.dma_start(e_src[:], src.rearrange("(p c) -> p c", p=EP)).then_inc(edge_loaded, 16)
                    sp.dma_start(e_type[:], edge_type.rearrange("(p c) -> p c", p=EP)).then_inc(edge_loaded, 16)
                    sp.wait_ge(consts_ready, 1)
                    sp.dma_start(e_dst[0:EP - 1, :], bass.AP(dst.tensor, 0, [[EC, EP - 1], [1, EC + 1]])).then_inc(edge_loaded, 16)
                    sp.dma_start(e_dst[EP - 1:EP, 0:EC], dst[(EP - 1) * EC:E].rearrange("(a b) -> a b", a=1)).then_inc(edge_loaded, 16)
                    sp.dma_start(x_sb[:], x.rearrange("(t p) d -> p t d", p=TP)).then_inc(x_loaded, 16)
                    sp.dma_start(router_sb[:], router_w).then_inc(small_loaded, 16)
                    sp.dma_start(bias[0:2 * R], b_rel).then_inc(small_loaded, 16)
                    sp.dma_start(bias[B_SELF:B_SELF + 1], b_self.rearrange("(a d) -> a d", a=1)).then_inc(small_loaded, 16)
                    load_first(sp, 1, first_w_loaded)
                    load_first(sp, 0, first_w_loaded)
                    sp.wait_ge(edges_packed, 1)
                    sp.wait_ge(consts_ready, 5)
                    sp.dma_start(edges_dram[0:E, :].rearrange("(p c) k -> p (c k)", p=EP),
                                 e_pack[:].rearrange("p c k -> p (c k)")).then_inc(edges_stored, 16)
                    sp.dma_start(edges_dram[E:EDGES, :].rearrange("(p c) k -> p (c k)", p=7),
                                 e_pad[:].rearrange("p c k -> p (c k)")).then_inc(edges_stored, 16)
                    sp.wait_ge(route_consts, 1)
                    sp.dma_start(y_dram[NX * P:TILES * P, :].rearrange("(c p) d -> p c d", p=P),
                                 zero_rows[:].unsqueeze(1).to_broadcast([P, MAXOV, D])).then_inc(later_cleared, 16)
                    for i in range(2):
                        sp.dma_start(stage_gate[:, 2 * i:2 * i + 2], gate_w[0].rearrange("(c p) f -> p c f", p=P)[:, 2 * i:2 * i + 2]
                                     ).then_inc(loaded["g"][i], 16)
                    sp.wait_ge(edges_stored, 32)
                    sp.wait_ge(later_cleared, 16)
                    sp.wait_ge(small_loaded, 48)
                    sp.wait_ge(first_w_loaded, 32)

                @block.gpsimd
                def _(pool):
                    nc.gpsimd.memset(e_dst[:], 1 << 20).then_inc(consts_ready, 1)
                    nc.gpsimd.iota(iota_i[:], [[1, NPAD]], base=0, channel_multiplier=0).then_inc(consts_ready, 1)
                    nc.gpsimd.memset(ones[:], 1.0).then_inc(consts_ready, 1)
                    pool.wait_ge(consts_ready, 3)
                    nc.gpsimd.affine_select(out=ident[:], in_=ones[:], compare_op=ALU.is_equal, fill=0.0, base=0,
                                            pattern=[[-1, P]], channel_multiplier=1).then_inc(consts_ready, 1)
                    nc.gpsimd.memset(e_pad[:], -1.0).then_inc(consts_ready, 1)
                    nc.gpsimd.memset(zero_rows[:], 0.0).then_inc(route_consts, 1)
                    nc.gpsimd.memset(agg_sb[:], 0.0)
                    nc.gpsimd.memset(first[:], 1.0)
                    nc.gpsimd.affine_select(out=before[:], in_=ones[0:TP, 0:TP], compare_op=ALU.is_gt, fill=0.0, base=0,
                                            pattern=[[1, TP]], channel_multiplier=-1)
                    nc.gpsimd.tensor_copy(ones16[:], ones[0:TP, 0:TP])
                    nc.gpsimd.iota(token_id_i[:], [[TP, T]], base=0, channel_multiplier=1)
                    link("pool", pool, nc.gpsimd.iota(expert_iota_i[:], [[1, NX]], base=0, channel_multiplier=0))
                    nc.gpsimd.tensor_copy(token_id[:], token_id_i[:])
                    nc.gpsimd.tensor_copy(expert_iota[:], expert_iota_i[:])
                    pool.wait_ge(consts_ready, 5)
                    nc.gpsimd.tensor_copy(slot_iota[:], iota_i[0:TP, 0:P])

                @block.vector
                def _(dve):
                    v = nc.vector
                    dve.wait_ge(edge_loaded, 64)
                    dve.wait_ge(consts_ready, 2)
                    v.tensor_scalar(e_win[:], e_dst[:, 0:EC], 4, None, ALU.arith_shift_right)
                    v.tensor_scalar(e_in[:], e_dst[:, 0:EC], WIN - 1, None, ALU.bitwise_and)
                    v.tensor_copy(iota_row[:], iota_i[:])
                    v.tensor_scalar(win_key[:], iota_i[:, 0:NW], float(KEY), None, ALU.mult)
                    v.tensor_copy(e_pack[:, :, 1], e_src[:])
                    v.tensor_tensor(below[:, 0, :], e_dst[:, 0:EC], e_dst[:, 1:EC + 1], ALU.is_gt)
                    link("dve", dve, v.tensor_copy(win_f[:], iota_i[0:EP, 0:NW + 1]))
                    v.tensor_copy(e_winf[:], e_win[:])
                    v.tensor_reduce(counts[:, NW + 1:NW + 2], below[:, 0, :], AX.X, ALU.add)
                    link("dve", dve, v.scalar_tensor_tensor(e_key[:], e_type[:], float(WIN), e_in[:], ALU.mult, ALU.add))
                    v.scalar_tensor_tensor(e_pack[:, :, 0], e_winf[:], float(KEY), e_key[:], ALU.mult, ALU.add).then_inc(edges_packed, 1)
                    link("dve", dve, v.tensor_tensor(below[:], e_winf[:].unsqueeze(1).to_broadcast([EP, NW + 1, EC]),
                                                    win_f[:].unsqueeze(2).to_broadcast([EP, NW + 1, EC]), ALU.is_lt))
                    v.tensor_reduce(counts[:, 0:NW + 1], below[:], AX.X, ALU.add).then_inc(count_ready, 1)
                    dve.wait_ge(x_loaded, 16)
                    normalize(dve, x_sb, xn, 0)
                    dve.wait_ge(count_full, 1)
                    link("dve", dve, v.tensor_copy(crow[:], p_count[0:1, 0:NW + 2]))
                    link("dve", dve, v.tensor_tensor(cdiff[:], crow[:, 1:NW + 1], crow[:, 0:NW], ALU.subtract))
                    link("dve", dve, v.tensor_reduce(flags[:, 0:1], cdiff[:], AX.X, ALU.max))
                    link("dve", dve, v.tensor_scalar(flags[:, 1:2], flags[:, 0:1], float(CAP), None, ALU.is_gt))
                    link("dve", dve, v.tensor_tensor(flags[:, 2:3], flags[:, 1:2], crow[:, NW + 1:NW + 2], ALU.add))
                    link("dve", dve, v.tensor_scalar(flags[:, 3:4], flags[:, 2:3], 0.0, None, ALU.is_equal))
                    v.tensor_scalar(offs[:, 0:NW], crow[:, 0:NW], flags[:, 3:4], None, ALU.mult)
                    v.tensor_scalar(offs[:, NW:NW + 1], flags[:, 3:4], float(1 - ROUNDS), float(ROUNDS), ALU.mult, ALU.add)
                    for t in range(T):
                        dve.wait_ge(tr_hi, t + 1)
                        v.tensor_tensor(token_columns(xt_lo, t), turned(t), token_columns(xt_hi, t).bitcast(F32),
                                        ALU.subtract)

                @block.scalar
                def _(act):
                    s = nc.scalar
                    roots(act, 0)
                    act.wait_ge(consts_ready, 4)
                    s.copy(ident16[:], ident[:])
                    for t in range(T):
                        act.wait_ge(tr_full, t + 1)
                        s.copy(token_columns(xt_hi, t), turned(t)).then_inc(tr_hi, 1)

                @block.tensor
                def _(pe):
                    m = nc.tensor
                    pe.wait_ge(count_ready, 1)
                    pe.wait_ge(consts_ready, 4)
                    m.matmul(p_count[0:1, 0:NW + 2], ones[0:EP, 0:1], counts[:], start=True, stop=True).then_inc(count_full, 1)
                    for t in range(T):
                        pe.wait_ge(ln_ready, t + 1)
                        for dc in range(KC):
                            i = m.transpose(p_t[:, t, dc * TP:(dc + 1) * TP], xn[:, t, dc * P:(dc + 1) * P], ident[0:TP, 0:TP])
                        i.then_inc(tr_full, 1)

            with ExitStack() as f:
                win_edges = sb("win_edges", [P, 4, CH, 2], F32, f)
                key_hot = sb("key_hot", [P, 2, CH, P], F16, f)
                src_hot = sb("src_hot", [P, 2, CH, NPAD], F16, f)
                lhs_a = sb("lhs_a", [TP, T, N], F32R, f)
                lhs_at = sb("lhs_at", [TP, T, N], F32R, f)
                h_hi_sb = sb("h_hi_sb", [TP, 2, D], F32R, f)
                h_lo_sb = sb("h_lo_sb", [TP, 2, D], F32R, f)
                degree = sb("degree", [TP, T, 2 * R], F32, f)
                degree_t = sb("degree_t", [2 * R, N], F32, f)
                zero_row = sb("zero_row", [1, D], F32R, f)
                p_agg = ps("p_agg", [P, T, 512], F32, f)
                p_h = ps("p_h", [P, 2, 512], F32, f)
                p_tr = ps("p_tr", [P, 512], F32, f)
                p_a = p_agg[:].rearrange("p t n -> p (t n)")
                p_first = [p_tr[:], p_agg[:, 4], p_h[:, 1], p_h[:, 0]]

                p_tr16 = p_tr[0:TP].bitcast(F16)[:, 0:T * (TP + 1)].rearrange("p (t n) -> p t n", t=T)

                rounds = nc.values_load(offs[0:1, NW:NW + 1], min_val=1, max_val=ROUNDS)
                with nc.Fori(0, rounds):
                    with nc.Block() as block:
                        @block.sync
                        def _(sp):
                            def w_load(slot, m, signal):
                                sp.dma_start(w_nat[:, slot], w_rel[m].rearrange("(c p) d -> p c d", p=P)
                                             if isinstance(m, int) else
                                             w_rel[bass.ds(m, 1)].rearrange("a (c p) d -> p (a c) d", p=P)).then_inc(signal, 16)

                            def window(q, k):
                                at = sp.value_load(offs[0:1, bass.ds(4 * q + k, 1)], min_val=0, max_val=EDGES - CAP)
                                sp.dma_start(win_edges[:, k], edges_dram[bass.ds(at, CAP), :].rearrange("(p c) k -> p c k", c=CH)
                                             ).then_inc(win_loaded[k], 16)

                            for k in range(4):
                                window(0, k)
                            sp.wait_ge(t_full, KC)
                            w_load(1, 0, wb_loaded)
                            with sp.Fori(1, NW // 4) as q:
                                for k in range(4):
                                    sp.wait_ge(onehot_ready, 4 * q + k - 3)
                                    window(q, k)
                            with sp.Fori(0, R - 1) as r:
                                sp.wait_ge(t_full, 13 * r + 8)
                                w_load(0, r + R + 1, wa_loaded)
                                sp.wait_ge(t_full, 13 * r + 15)
                                w_load(1, r + 1, wb_loaded)
                            sp.wait_ge(t_full, 13 * (R - 1) + 8)
                            load_first(sp, 0, next_w_loaded)
                            sp.wait_ge(t_full, 13 * (R - 1) + 15)
                            load_first(sp, 1, next_w_loaded)
                            sp.wait_ge(next_w_loaded, 32)

                        @block.vector
                        def _(dve):
                            v = nc.vector
                            v.memset(zero_row[:].bitcast(F32), 0.0).then_inc(zero_ready, 1)

                            def window(q, k):
                                dve.wait_ge(win_loaded[k], 16 * q + 16)
                                if not (isinstance(q, int) and q == 0 and k < 2):
                                    dve.wait_ge(a_full, 4 * q + k - 1)
                                for c in range(CH):
                                    v.tensor_scalar(key_hot[:, k % 2, c], iota_row[:, 0:P], win_key[:, bass.ds(4 * q + k, 1)],
                                                    win_edges[:, k, c, 0:1], ALU.add, ALU.is_equal)
                                for c in range(CH):
                                    i = v.tensor_scalar(src_hot[:, k % 2, c, 0:N], iota_row[:, 0:N], win_edges[:, k, c, 1:2], None, ALU.is_equal)
                                i.then_inc(onehot_ready, 1)

                            def w_low(slot, dc, hi, bank=p_tr[:]):
                                dve.wait_ge(wt_hi, hi)
                                v.tensor_tensor(wt_lo_sb[:, slot, dc], bank, wt_hi_sb[:, slot, dc].bitcast(F32),
                                                ALU.subtract).then_inc(wt_lo, 1)

                            def h_low(n, hi):
                                dve.wait_ge(h_hi, hi)
                                v.tensor_tensor(h_lo_sb[:, n % 2], p_h[0:TP, n % 2], h_hi_sb[:, n % 2].bitcast(F32),
                                                ALU.subtract).then_inc(h_lo, 1)

                            for dc in range(KC):
                                w_low(1, dc, dc + 1, p_first[dc])
                            for q in range(T + 1):
                                for k in range(4):
                                    window(q, k)
                                    if q > 0 and k == 1:
                                        dve.wait_ge(self_full, q)
                                        v.scalar_tensor_tensor(agg_sb[:, q - 1], p_h[0:TP, (q - 1) % 2], first[0:TP], agg_sb[:, q - 1],
                                                               ALU.mult, ALU.add).then_inc(self_added, 1)
                                    if q == T and k >= 2:
                                        for dc in (2 * k - 4, 2 * k - 3):
                                            w_low(0, dc, KC + dc + 1, p_first[dc])
                            with dve.Fori(T + 1, NW // 4) as q:
                                for k in range(4):
                                    window(q, k)
                            h_low(0, 1)
                            v.tensor_scalar(offs[:, 0:NW], offs[:, 0:NW], float(CAP), None, ALU.add)

                            def steps(r, last):
                                for n in range(2 * T):
                                    if n < 2 * T - 1 or not last:
                                        h_low(n + 1, 10 * r + n + 2)
                                    if n < KC:
                                        w_low(1, n, 8 * r + 8 + n + 1)
                                    if n >= T and n < T + KC and not last:
                                        w_low(0, n - T, 8 * r + 12 + n - T + 1)

                            with dve.Fori(0, R - 1) as r:
                                steps(r, False)
                            steps(R - 1, True)
                            dve.wait_ge(deg_full, 1)
                            v.tensor_copy(degree_t[:, 0:4 * TP], p_tr[0:2 * R, 0:4 * TP])
                            v.tensor_copy(degree_t[:, 4 * TP:N], p_h[0:2 * R, 0, 0:TP]).then_inc(deg_copied, 1)
                            for t in range(T):
                                dve.wait_ge(agg_full, t + 1)
                                v.tensor_tensor(agg_sb[:, t], agg_sb[:, t], p_agg[0:TP, t], ALU.add).then_inc(agg_added, 1)
                            v.memset(first[:], 0.0)

                        @block.scalar
                        def _(act):
                            s = nc.scalar

                            def w_high(slot, dc, full, bank=p_tr[:]):
                                act.wait_ge(t_full, full)
                                s.copy(wt_hi_sb[:, slot, dc], bank).then_inc(wt_hi, 1)

                            def h_high(n, full):
                                act.wait_ge(h_full, full)
                                s.copy(h_hi_sb[:, n % 2], p_h[0:TP, n % 2]).then_inc(h_hi, 1)

                            def a_direct(r, st):
                                s.activation(lhs_a[:, st], a16[:, st, r, 0:N] if isinstance(r, int) else a16[:, st, bass.ds(r, 1), 0:N].rearrange("p a n -> p (a n)"),
                                             ACT.Copy, accum_out=degree[:, st, bass.ds(r, 1)]).then_inc(a_ready, 1)

                            def a_turned(r, dt, full):
                                act.wait_ge(t_full, full)
                                s.activation(lhs_at[:, dt].rearrange("p (t n) -> p t n", t=T), p_tr16[:, :, 0:TP], ACT.Copy,
                                             accum_out=degree[:, dt, bass.ds(r + R, 1)]).then_inc(at_ready, 1)

                            def store_counts(q, k):
                                act.wait_ge(a_full, 4 * q + k + 1)
                                c = 1024 * (k % 2)
                                s.copy(a16[:, :, :, bass.ds((4 * q + k) * WIN, WIN)],
                                       p_a[0:TP, c:c + T * P].rearrange("p (t r d) -> p t r d", t=T, r=R)).then_inc(a_stored, 1)

                            for dc in range(KC):
                                w_high(1, dc, dc + 1, p_first[dc])
                            with act.Fori(0, T) as q:
                                for k in range(4):
                                    store_counts(q, k)
                            for k in range(4):
                                store_counts(T, k)
                                if k < 2:
                                    for dc in (2 * k, 2 * k + 1):
                                        w_high(0, dc, KC + dc + 1, p_first[dc])
                            h_high(0, 1)
                            with act.Fori(T + 1, NW // 4) as q:
                                for k in range(4):
                                    store_counts(q, k)
                            act.wait_ge(a_stored, NW)
                            for st in range(T):
                                a_direct(0, st)

                            def steps(r, last):
                                base = 13 * r + 8
                                g = 0
                                for n in range(2 * T):
                                    if n < 2 * T - 1 or not last:
                                        h_high(n + 1, 10 * r + n + 2)
                                    if n < KC:
                                        g += 1
                                        w_high(1, n, base + g)
                                    if n < T:
                                        g += 1
                                        a_turned(r, n, base + g)
                                    if n >= T and not last:
                                        if n < T + KC:
                                            g += 1
                                            w_high(0, n - T, base + g)
                                        a_direct(r + 1, n - T)

                            with act.Fori(0, R - 1) as r:
                                steps(r, False)
                            steps(R - 1, True)

                        @block.tensor
                        def _(pe):
                            m = nc.tensor

                            def w_turn(slot, dc, bank=p_tr[:]):
                                for oc in range(4):
                                    i = m.transpose(bank[:, oc * P:(oc + 1) * P], w_nat[:, slot, oc, dc * P:(dc + 1) * P], ident[:])
                                i.then_inc(t_full, 1)

                            def a_turn(r, dt):
                                for st in range(T):
                                    i = m.transpose(p_tr16[:, st, 0:TP],
                                                    a16[:, st, bass.ds(r, 1), dt * TP:(dt + 1) * TP].rearrange("p a n -> p (a n)"),
                                                    ident16[0:TP, 0:TP])
                                i.then_inc(t_full, 1)

                            def split_product(o, slot, t, dc, start, stop):
                                at = slice(t * TP, (t + 1) * TP)
                                m.matmul(o, xt_hi[:, dc, at], wt_hi_sb[:, slot, dc], start=start, stop=False)
                                m.matmul(o, xt_hi[:, dc, at], wt_lo_sb[:, slot, dc], start=False, stop=False)
                                return m.matmul(o, xt_lo[:, dc, at], wt_hi_sb[:, slot, dc], start=False, stop=stop)

                            def h_product(n):
                                for dc in range(KC):
                                    i = split_product(p_h[0:TP, n % 2], (n // T) % 2, n % T, dc, start=(dc == 0), stop=(dc == KC - 1))
                                i.then_inc(h_full, 1)

                            def add_messages(n):
                                lhs = lhs_a if n < T else lhs_at
                                for t in range(T):
                                    w = lhs[:, n % T, t * TP:(t + 1) * TP]
                                    m.matmul(p_agg[0:TP, t], w, h_hi_sb[:, n % 2], start=False, stop=False)
                                    i = m.matmul(p_agg[0:TP, t], w, h_lo_sb[:, n % 2], start=False, stop=False)

                            def window(q, k):
                                pe.wait_ge(onehot_ready, 4 * q + k + 1)
                                if not (isinstance(q, int) and q == 0 and k < 2):
                                    pe.wait_ge(a_stored, 4 * q + k - 1)
                                for st in range(T):
                                    for c in range(CH):
                                        o = 1024 * (k % 2) + st * P
                                        i = m.matmul(p_a[0:TP, o:o + P], src_hot[:, k % 2, c, st * TP:(st + 1) * TP],
                                                     key_hot[:, k % 2, c], start=(c == 0), stop=(c == CH - 1))
                                i.then_inc(a_full, 1)

                            for dc in range(KC):
                                w_turn(1, dc, p_first[dc])
                            for t in range(T):
                                for k in range(4):
                                    window(t, k)
                                    if k == 0:
                                        if t == 0:
                                            pe.wait_ge(wt_lo, KC)
                                        if t >= 2:
                                            pe.wait_ge(self_added, t - 1)
                                        m.matmul(p_h[0:TP, t % 2], ones[B_SELF:B_SELF + 1, 0:TP], bias[B_SELF:B_SELF + 1], start=True, stop=False)
                                    i = split_product(p_h[0:TP, t % 2], 1, t, k, start=False, stop=(k == KC - 1))
                                i.then_inc(self_full, 1)
                            for k in range(4):
                                window(T, k)
                                if k == 1:
                                    pe.wait_ge(self_added, T)
                                if k < 2:
                                    w_turn(0, 2 * k, p_first[2 * k])
                                    w_turn(0, 2 * k + 1, p_first[2 * k + 1])
                            pe.wait_ge(wt_lo, 2 * KC)
                            h_product(0)
                            with pe.Fori(T + 1, NW // 4) as q:
                                for k in range(4):
                                    window(q, k)
                            pe.wait_ge(a_stored, NW)
                            pe.wait_ge(zero_ready, 1)
                            for t in range(T):
                                m.matmul(p_agg[0:TP, t], zero_row[:, 0:TP], zero_row[:], start=True, stop=False)

                            def steps(r, last):
                                for n in range(2 * T):
                                    if n < 2 * T - 1 or not last:
                                        if n + 1 == T:
                                            pe.wait_ge(wt_lo, 8 * r + 12)
                                        if n + 1 == 2 * T:
                                            pe.wait_ge(wt_lo, 8 * r + 16)
                                        h_product((n + 1) % (2 * T))
                                    if n < KC:
                                        if n == 0:
                                            pe.wait_ge(wb_loaded, 16 * r + 16)
                                            pe.wait_ge(wt_lo, 8 * r + 8)
                                        else:
                                            pe.wait_ge(at_ready, 5 * r + n)
                                        w_turn(1, n)
                                    if T <= n < T + KC and not last:
                                        if n == T:
                                            pe.wait_ge(wa_loaded, 16 * r + 16)
                                            pe.wait_ge(at_ready, 5 * r + T)
                                        else:
                                            pe.wait_ge(wt_lo, 8 * r + 12 + n - T)
                                        w_turn(0, n - T)
                                    pe.wait_ge(h_lo, 10 * r + n + 1)
                                    if n < T:
                                        pe.wait_ge(a_ready, 5 * r + n + 1)
                                    else:
                                        pe.wait_ge(at_ready, 5 * r + n - T + 1)
                                    add_messages(n)
                                    if n < T:
                                        if n < KC:
                                            pe.wait_ge(wt_lo, 8 * r + 8 + n + 1)
                                        else:
                                            pe.wait_ge(at_ready, 5 * r + n)
                                        a_turn(r, n)

                            with pe.Fori(0, R - 1) as r:
                                steps(r, False)
                            steps(R - 1, True)
                            pe.wait_ge(at_ready, R * T)
                            pe.wait_ge(a_ready, R * T)
                            for t in range(T):
                                o = p_tr[0:2 * R, t * TP:(t + 1) * TP] if t < 4 else p_h[0:2 * R, 0, 0:TP]
                                i = m.transpose(o, degree[:, t], ident[0:TP, 0:TP])
                            i.then_inc(deg_full, 1)
                            pe.wait_ge(deg_copied, 1)
                            for t in range(T):
                                m.matmul(p_agg[0:TP, t], degree_t[:, t * TP:(t + 1) * TP], bias[0:2 * R],
                                         start=False, stop=True).then_inc(agg_full, 1)

                    nc.all_engine_barrier(sems_to_clear=round_sems)

        w_dram = {"g": gate_w, "u": up_w, "d": down_w}
        with ExitStack() as g:
            stage = {"g": stage_gate[:], "u": sb("stage_up", [P, KC, F], F32, g)[:],
                     "d": sb("stage_down", [P, FC, D], F32, g)[:]}
            shape = {"g": [P, KC, F], "u": [P, KC, F], "d": [P, FC, D]}
            w_hi = {k: sb(f"{k}_hi_sb", shape[k], F32R, g) for k in "gud"}
            w_lo = {k: sb(f"{k}_lo_sb", shape[k], F32R, g) for k in "gud"}
            tokens = sb("tokens", [P, D], F32, g)
            slot_token = sb("slot_token", [P, T * NX], I32, g)
            column = sb("column", [P, 1], I32, g)
            xs_hi = sb("xs_hi", [P, KC, P], F32R, g)
            xs_lo = sb("xs_lo", [P, KC, P], F32R, g)
            silu = sb("silu", [P, F], F32, g)
            hid = sb("hid", [P, F], F32, g)
            hs_hi = sb("hs_hi", [P, FC, P], F32R, g)
            hs_lo = sb("hs_lo", [P, FC, P], F32R, g)
            y_sb = sb("y_sb", [P, D], F32, g)
            router_t = sb("router_t", [P, KC, NX], F32, g)
            logits = sb("logits", [TP, T, NX], F32, g)
            rest = sb("rest", [TP, T, NX], F32, g)
            cand = sb("cand", [TP, T, NX], F32, g)
            hot = sb("hot", [TP, 2, T, NX], F32, g)
            mask = sb("mask", [TP, T + 1, NX], F16, g)
            xt2 = sb("xt2", [P, 2, KC, TP], F32, g)
            slot_hot = sb("slot_hot", [TP, 2 * T, P], F16, g)
            named = sb("named", [TP, 2, T, NX], F32, g)
            tag = sb("tag", [TP, 2 * T, T, NX], F16, g)
            best = sb("best", [TP, 2, T], F32, g)
            choice = sb("choice", [TP, 2, T], F32, g)
            rank = sb("rank", [TP, T + 1, NX], F32, g)
            picked = sb("picked", [TP, 2, T, NX], F32, g)
            place = sb("place", [TP, 2, T], F32, g)
            nth_tile = sb("nth_tile", [TP, 2, T], F32, g)
            later = sb("later", [TP, 2, T], F32, g)
            step = sb("step", [TP, 2, T], F32, g)
            y_at = sb("y_at", [TP, 2 * T], I32, g)
            weight = sb("weight", [TP, 2, T], F32, g)
            gap = sb("gap", [TP, T], F32, g)
            extra = sb("extra", [TP, NX], F32, g)
            upto = sb("upto", [TP, 2, NX], F32, g)
            le = sb("le", [1, 2, MAXOV, NX], F32, g)
            over_f = sb("over_f", [1, 3, MAXOV], F32, g)
            tile_expert = sb("tile_expert", [1, TILES], I32, g)
            tile_column = sb("tile_column", [1, TILES], I32, g)
            later_tiles = sb("later_tiles", [1, 1], I32, g)

            xn2 = agg_sb

            def w_piece(k, e, i):
                w = w_dram[k][e] if isinstance(e, int) else w_dram[k][bass.ds(e, 1)].rearrange("a r f -> (a r) f")
                rows = w.shape[0] // 2
                return w[i * rows:(i + 1) * rows, :].rearrange("(c p) f -> p c f", p=P)

            def half(ap, k, i):
                c = shape[k][1] // 2
                return ap[:, i * c:(i + 1) * c]

            with ExitStack() as f:
                p_gate = ps("p_gate", [P, F], F32, f)
                p_up = ps("p_up", [P, F], F32, f)
                p_ht = ps("p_ht", [P, F], F32, f)
                p_x = ps("p_x", [P, 512], F32, f)
                p_y = ps("p_y", [P, 512], F32, f)
                p_t = [p_gate[:, 0:KC * TP], p_gate[:, 512:512 + KC * TP]]
                p_router = p_y[:, 0:KC * NX].rearrange("p (c e) -> p c e", c=KC)
                p_logits = p_up[0:TP, 0:T * NX].rearrange("p (t e) -> p t e", t=T)
                p_rank = p_ht[0:TP, 0:(T + 1) * NX].rearrange("p (t e) -> p t e", t=T + 1)
                p_slots = p_up[:, 512:512 + T * NX]
                block = f.enter_context(nc.Block())

                @block.sync
                def _(sp):
                    def load(k, e, i):
                        sp.dma_start(half(stage[k], k, i), w_piece(k, e, i)).then_inc(loaded[k][i], 16)

                    load("u", 0, 0)
                    load("u", 0, 1)
                    sp.wait_ge(ln_ready, 2 * T)
                    sp.dma_start(ln2_dram.rearrange("(t p) d -> p t d", p=TP), xn2[:]).then_inc(ln2_stored, 16)
                    load("d", 0, 0)
                    load("d", 0, 1)

                    def reload(k, e, expert):
                        for i in range(2):
                            sp.wait_ge(split_lo[k], 2 * e - 1 + i)
                            load(k, expert, i)

                    def listed(e):
                        return sp.value_load(tile_expert[0:1, bass.ds(e, 1)], min_val=0, max_val=NX - 1)

                    reload("g", 1, 1)
                    reload("u", 1, 1)
                    reload("g", 2, 2)
                    reload("u", 2, 2)
                    sp.wait_ge(list_ready, 1)
                    n = sp.value_load(later_tiles[:], min_val=0, max_val=MAXOV) + NX
                    with sp.Fori(1, n - 2) as e:
                        reload("d", e, listed(e))
                        reload("g", e + 2, listed(e + 2))
                        reload("u", e + 2, listed(e + 2))
                    reload("d", n - 2, listed(n - 2))
                    reload("d", n - 1, listed(n - 1))

                @block.gpsimd
                def _(pool):
                    q = nc.gpsimd

                    def gather(e, at):
                        q.tensor_copy(column[:], slot_token[:, bass.ds(at, 1)]).then_inc(column_copied, 1)
                        pool.wait_ge(column_copied, e + 1)
                        pool.sem_inc(column_waited, 1)
                        q.indirect_dma_start(tokens[:], None, ln2_dram, bass.IndirectOffsetOnAxis(ap=column[:].bitcast(U32), axis=0)
                                             ).then_inc(tokens_loaded, 16)

                    pool.wait_ge(ln2_stored, 16)
                    pool.wait_ge(slots_ready, 1)
                    gather(0, 0)
                    pool.wait_ge(xt_full, 1)
                    gather(1, 1)
                    pool.wait_ge(list_ready, 1)
                    n = pool.value_load(later_tiles[:], min_val=0, max_val=MAXOV) + NX
                    with pool.Fori(2, n) as e:
                        pool.wait_ge(xt_full, e)
                        gather(e, pool.value_load(tile_column[0:1, bass.ds(e, 1)], min_val=0, max_val=T * NX - 1))

                @block.vector
                def _(dve):
                    v = nc.vector
                    for t in range(T):
                        i = v.scalar_tensor_tensor(x_sb[:, t], agg_sb[:, t], 0.0, x_sb[:, t], ALU.max, ALU.add)
                    link("dve", dve, i)
                    normalize(dve, x_sb, xn2, 1)
                    def low(k, e, i):
                        dve.wait_ge(split_hi[k], 2 * e + i + 1)
                        v.tensor_tensor(half(w_lo[k][:], k, i), half(stage[k], k, i), half(w_hi[k][:], k, i).bitcast(F32),
                                        ALU.subtract).then_inc(split_lo[k], 1)

                    def x_low(e):
                        dve.wait_ge(xt_hi_ready, e + 1)
                        v.tensor_tensor(xs_lo[:].rearrange("p c n -> p (c n)"), p_x[:], xs_hi[:].rearrange("p c n -> p (c n)").bitcast(F32),
                                        ALU.subtract).then_inc(xt_lo_ready, 1)

                    def hidden(e):
                        dve.wait_ge(done["u"], e + 1)
                        for i in range(2):
                            dve.wait_ge(silu_ready, 2 * e + i + 1)
                            v.tensor_tensor(hid[:, i * 512:(i + 1) * 512], silu[:, i * 512:(i + 1) * 512], p_up[:, i * 512:(i + 1) * 512],
                                            ALU.mult).then_inc(hid_ready, 1)

                    def h_low(e):
                        for i in range(2):
                            dve.wait_ge(ht_hi_ready, 2 * e + i + 1)
                            v.tensor_tensor(hs_lo[:, 4 * i:4 * i + 4].rearrange("p c n -> p (c n)"), p_ht[:, i * 512:(i + 1) * 512],
                                            hs_hi[:, 4 * i:4 * i + 4].rearrange("p c n -> p (c n)").bitcast(F32),
                                            ALU.subtract).then_inc(ht_lo_ready, 1)

                    dve.wait_ge(router_full, 1)
                    v.tensor_copy(router_t[:], p_router).then_inc(router_copied, 1)
                    v.memset(mask[:, T], 0.0)
                    low("g", 0, 0)
                    dve.wait_ge(logits_full, T)
                    link("dve", dve, v.tensor_copy(logits[:], p_logits))
                    iota = expert_iota[:].unsqueeze(1).to_broadcast([TP, T, NX])

                    def wide(a):
                        return a.unsqueeze(2).to_broadcast([TP, T, NX])

                    for c in range(2):
                        src_logits = logits if c == 0 else rest
                        link("dve", dve, v.tensor_reduce(best[:, c], src_logits[:], AX.X, ALU.max))
                        link("dve", dve, v.tensor_tensor(cand[:], src_logits[:], wide(best[:, c]), ALU.not_equal))
                        link("dve", dve, v.scalar_tensor_tensor(cand[:], cand[:], float(NX), iota, ALU.mult, ALU.add))
                        link("dve", dve, v.tensor_reduce(choice[:, c], cand[:], AX.X, ALU.min))
                        link("dve", dve, v.tensor_tensor(hot[:, c], iota, wide(choice[:, c]), ALU.is_equal))
                        if c == 0:
                            link("dve", dve, v.scalar_tensor_tensor(rest[:], hot[:, 0], -3.0e38, logits[:], ALU.mult, ALU.add))
                    v.tensor_tensor(mask[:, 0:T], hot[:, 0], hot[:, 1], ALU.add).then_inc(mask_ready, 1)
                    v.tensor_tensor(gap[:], best[:, 1], best[:, 0], ALU.subtract).then_inc(gap_ready, 1)
                    for c in range(2):
                        v.tensor_tensor(named[:, c], hot[:, c], wide(token_id[:]), ALU.mult)
                    dve.wait_ge(rank_full, 1)
                    link("dve", dve, v.tensor_copy(rank[:], p_rank))
                    for c in range(2):
                        i = v.tensor_tensor(picked[:, c], hot[:, c], rank[:, 0:T], ALU.mult)
                    link("dve", dve, i)
                    link("dve", dve, v.tensor_reduce(place[:], picked[:], AX.X, ALU.add))
                    link("dve", dve, v.tensor_scalar(nth_tile[:], place[:], float(P), None, ALU.is_ge))
                    for k in range(2, T):
                        link("dve", dve, v.scalar_tensor_tensor(nth_tile[:], place[:], float(k * P), nth_tile[:], ALU.is_ge, ALU.add))
                    link("dve", dve, v.scalar_tensor_tensor(step[:], nth_tile[:], -float(P), place[:], ALU.mult, ALU.add))
                    nths, names = nth_tile[:].rearrange("p c t -> p (c t)"), named[:].rearrange("p c t e -> p (c t) e")
                    steps = step[:].rearrange("p c t -> p (c t)")
                    for c in range(2 * T):
                        v.tensor_scalar(slot_hot[:, c], slot_iota[:], steps[:, c:c + 1], None, ALU.is_equal)
                    for j in range(T):
                        i = v.scalar_tensor_tensor(tag[:, :, j], nths.unsqueeze(2).to_broadcast([TP, 2 * T, NX]), float(j), names,
                                                   ALU.is_equal, ALU.mult)
                    i.then_inc(places_ready, 1)
                    low("g", 0, 1)
                    low("u", 0, 0)
                    low("u", 0, 1)
                    x_low(0)
                    n_tok, n_extra, cum = rank[:, T], extra[:], upto
                    link("dve", dve, v.tensor_scalar(n_extra, n_tok, float(P), None, ALU.is_gt))
                    for k in range(2, T):
                        link("dve", dve, v.scalar_tensor_tensor(n_extra, n_tok, float(k * P), n_extra, ALU.is_gt, ALU.add))
                    link("dve", dve, v.tensor_copy(cum[:, 0], n_extra))
                    for k, shift in enumerate((1, 2, 4, 8)):
                        a, b = cum[:, k % 2], cum[:, (k + 1) % 2]
                        v.tensor_copy(b[:, 0:shift], a[:, 0:shift])
                        link("dve", dve, v.tensor_tensor(b[:, shift:NX], a[:, shift:NX], a[:, 0:NX - shift], ALU.add))
                    ends = cum[0:1, 0].unsqueeze(1).to_broadcast([1, MAXOV, NX])
                    nth = expert_iota[0:1, 0:MAXOV].unsqueeze(2).to_broadcast([1, MAXOV, NX])
                    link("dve", dve, v.tensor_tensor(le[:, 0], ends, nth, ALU.is_le))
                    link("dve", dve, v.tensor_tensor(le[:, 1], le[:, 0], ends, ALU.mult))
                    v.tensor_reduce(over_f[:, 0], le[:, 0], AX.X, ALU.add)
                    link("dve", dve, v.tensor_reduce(over_f[:, 1], le[:, 1], AX.X, ALU.max))
                    v.tensor_scalar(over_f[:, 0], over_f[:, 0], float(NX - 1), None, ALU.min)
                    link("dve", dve, v.tensor_tensor(over_f[:, 2], expert_iota[0:1, 0:MAXOV], over_f[:, 1], ALU.subtract))
                    link("dve", dve, v.tensor_scalar(over_f[:, 2], over_f[:, 2], 1.0, float(T - 1), ALU.add, ALU.min))
                    v.tensor_copy(tile_expert[:, 0:NX], expert_iota[0:1])
                    v.tensor_copy(tile_column[:, 0:NX], expert_iota[0:1])
                    v.tensor_copy(tile_expert[:, NX:TILES], over_f[:, 0])
                    v.scalar_tensor_tensor(tile_column[:, NX:TILES], over_f[:, 2], float(NX), over_f[:, 0], ALU.mult, ALU.add)
                    v.tensor_copy(later_tiles[:], cum[0:1, 0, NX - 1:NX]).then_inc(list_ready, 1)
                    dve.wait_ge(list_ready, 1)
                    dve.wait_ge(exp_ready, 1)
                    link("dve", dve, v.tensor_scalar(best[:, 0], gap[:], 1.0, None, ALU.add))
                    link("dve", dve, v.reciprocal(weight[:, 0], best[:, 0]))
                    v.tensor_tensor(weight[:, 1], weight[:, 0], gap[:], ALU.mult)
                    link("dve", dve, v.tensor_tensor(n_extra, cum[:, 0], n_extra, ALU.subtract))
                    for c in range(2):
                        i = v.tensor_tensor(picked[:, c], hot[:, c], n_extra.unsqueeze(1).to_broadcast([TP, T, NX]), ALU.mult)
                    link("dve", dve, i)
                    link("dve", dve, v.tensor_reduce(later[:], picked[:], AX.X, ALU.add))
                    link("dve", dve, v.tensor_tensor(later[:], later[:], nth_tile[:], ALU.add))
                    link("dve", dve, v.scalar_tensor_tensor(later[:], later[:], float(NX - 1), choice[:], ALU.add, ALU.subtract))
                    link("dve", dve, v.scalar_tensor_tensor(later[:], nth_tile[:], 0.0, later[:], ALU.is_gt, ALU.mult))
                    link("dve", dve, v.tensor_tensor(later[:], later[:], choice[:], ALU.add))
                    v.scalar_tensor_tensor(y_at[:].rearrange("p (c t) -> p c t", c=2), later[:], float(P), step[:], ALU.mult, ALU.add)

                    def next_inputs(e):
                        low("g", e, 0)
                        low("g", e, 1)
                        x_low(e)

                    def down_inputs(e):
                        h_low(e)
                        low("d", e, 0)
                        low("d", e, 1)

                    def body(e):
                        down_inputs(e - 1)
                        next_inputs(e + 1)
                        hidden(e)
                        low("u", e + 1, 0)
                        low("u", e + 1, 1)

                    n = dve.value_load(later_tiles[:], min_val=0, max_val=MAXOV) + NX
                    next_inputs(1)
                    hidden(0)
                    low("u", 1, 0)
                    low("u", 1, 1)
                    with dve.Fori(1, n - 1) as e:
                        body(e)
                    down_inputs(n - 2)
                    hidden(n - 1)
                    down_inputs(n - 1)

                @block.scalar
                def _(act):
                    s = nc.scalar
                    def high(k, e, i):
                        act.wait_ge(loaded[k][i], 16 * e + 16)
                        s.copy(half(w_hi[k][:], k, i), half(stage[k], k, i)).then_inc(split_hi[k], 1)

                    def x_high(e):
                        act.wait_ge(xt_full, e + 1)
                        s.copy(xs_hi[:].rearrange("p c n -> p (c n)"), p_x[:]).then_inc(xt_hi_ready, 1)

                    def silus(e):
                        act.wait_ge(done["g"], e + 1)
                        if not (isinstance(e, int) and e == 0):
                            act.wait_ge(hid_ready, 2 * e)
                        for i in range(2):
                            s.activation(silu[:, i * 512:(i + 1) * 512], p_gate[:, i * 512:(i + 1) * 512], ACT.Silu).then_inc(silu_ready, 1)

                    def h_high(e):
                        for i in range(2):
                            act.wait_ge(ht_full, 2 * e + i + 1)
                            s.copy(hs_hi[:, 4 * i:4 * i + 4].rearrange("p c n -> p (c n)"), p_ht[:, i * 512:(i + 1) * 512]).then_inc(ht_hi_ready, 1)

                    def y_copy(e, first):
                        act.wait_ge(done["d"], e + 1)
                        if not first:
                            act.wait_ge(y_stored, 16 * e)
                        s.copy(y_sb[:], p_y[:]).then_inc(y_copied, 1)
                        act.wait_ge(y_copied, e + 1)
                        act.dma_start(y_dram[bass.ds(e * P, P), :], y_sb[:]).then_inc(y_stored, 16)

                    high("g", 0, 0)
                    high("g", 0, 1)
                    roots(act, 1)
                    for t in range(T):
                        act.wait_ge(x2_full, t + 1)
                        s.copy(xt2[:, t % 2].rearrange("p c n -> p (c n)"), p_t[t % 2]).then_inc(x2_copied, 1)
                    high("u", 0, 0)
                    high("u", 0, 1)
                    act.wait_ge(slots_full, 1)
                    s.copy(slot_token[:], p_slots).then_inc(slots_ready, 1)
                    act.wait_ge(gap_ready, 1)
                    s.activation(gap[:], gap[:], ACT.Exp).then_inc(exp_ready, 1)
                    x_high(0)

                    def next_inputs(e):
                        act.wait_ge(done["g"], e)
                        high("g", e, 0)
                        high("g", e, 1)
                        silus(e - 1)
                        x_high(e)
                        act.wait_ge(done["u"], e)
                        high("u", e, 0)
                        high("u", e, 1)

                    def body(e, nth):
                        h_high(e - 1)
                        if nth != 1:
                            y_copy(e - 2, nth == 2)
                        high("d", e - 1, 0)
                        high("d", e - 1, 1)
                        next_inputs(e + 1)

                    next_inputs(1)
                    act.wait_ge(list_ready, 1)
                    n = act.value_load(later_tiles[:], min_val=0, max_val=MAXOV) + NX
                    body(1, 1)
                    body(2, 2)
                    with act.Fori(3, n - 1) as e:
                        body(e, None)
                    h_high(n - 2)
                    y_copy(n - 3, False)
                    high("d", n - 2, 0)
                    high("d", n - 2, 1)
                    silus(n - 1)
                    h_high(n - 1)
                    y_copy(n - 2, False)
                    high("d", n - 1, 0)
                    high("d", n - 1, 1)
                    y_copy(n - 1, False)
                    act.wait_ge(y_stored, 16 * n)
                    act.sem_inc(all_stored, 1)

                @block.tensor
                def _(pe):
                    m = nc.tensor
                    for dc in range(KC):
                        i = m.transpose(p_router[:, dc], router_sb[:, dc * P:(dc + 1) * P], ident[0:NX, 0:NX])
                    i.then_inc(router_full, 1)
                    pe.wait_ge(router_copied, 1)

                    def token_logits(t):
                        pe.wait_ge(x2_copied, t + 1)
                        for dc in range(KC):
                            i = m.matmul(p_logits[:, t], xt2[:, t % 2, dc], router_t[:, dc], start=(dc == 0), stop=(dc == KC - 1))
                        i.then_inc(logits_full, 1)

                    for t in range(T):
                        pe.wait_ge(ln_ready, T + t + 1)
                        for dc in range(KC):
                            i = m.transpose(p_t[t % 2][:, dc * TP:(dc + 1) * TP], xn2[:, t, dc * P:(dc + 1) * P], ident[0:TP, 0:TP])
                        i.then_inc(x2_full, 1)
                        if t:
                            token_logits(t - 1)
                    token_logits(T - 1)
                    pe.wait_ge(mask_ready, 1)
                    m.matmul(p_rank, before[:], mask[:], start=True, stop=False)
                    for k in range(1, T + 1):
                        i = m.matmul(p_rank[:, k:T + 1], ones16[:], mask[:, 0:T + 1 - k], start=False, stop=(k == T))
                    i.then_inc(rank_full, 1)
                    pe.wait_ge(places_ready, 1)
                    for c in range(2 * T):
                        i = m.matmul(p_slots, slot_hot[:, c], tag[:, c].rearrange("p j e -> p (j e)"), start=(c == 0), stop=(c == 2 * T - 1))
                    i.then_inc(slots_full, 1)

                    def wide_product(k, e, into):
                        for c in range(KC):
                            if c % 2 == 0:
                                pe.wait_ge(split_lo[k], 2 * e + c // 2 + 1)
                            for x_part, w_part in ((xs_hi, w_hi), (xs_hi, w_lo), (xs_lo, w_hi)):
                                for h in range(2):
                                    i = m.matmul(into[:, h * 512:(h + 1) * 512], x_part[:, c], w_part[k][:, c, h * 512:(h + 1) * 512],
                                                 start=(c == 0 and x_part is xs_hi and w_part is w_hi),
                                                 stop=(c == KC - 1 and x_part is xs_lo))
                        i.then_inc(done[k], 1)

                    def turn_tokens(e):
                        pe.wait_ge(tokens_loaded, 16 * e + 16)
                        for c in range(KC):
                            i = m.transpose(p_x[:, c * P:(c + 1) * P], tokens[:, c * P:(c + 1) * P], ident[:])
                        i.then_inc(xt_full, 1)

                    def turn_hidden(e):
                        for h in range(2):
                            pe.wait_ge(hid_ready, 2 * e + h + 1)
                            for c in range(4 * h, 4 * h + 4):
                                i = m.transpose(p_ht[:, c * P:(c + 1) * P], hid[:, c * P:(c + 1) * P], ident[:])
                            i.then_inc(ht_full, 1)

                    def down(e, first):
                        if not first:
                            pe.wait_ge(y_copied, e)
                        for c in range(FC):
                            if c % 4 == 0:
                                pe.wait_ge(ht_lo_ready, 2 * e + c // 4 + 1)
                                pe.wait_ge(split_lo["d"], 2 * e + c // 4 + 1)
                            m.matmul(p_y[:], hs_hi[:, c], w_hi["d"][:, c], start=(c == 0), stop=False)
                            m.matmul(p_y[:], hs_hi[:, c], w_lo["d"][:, c], start=False, stop=False)
                            i = m.matmul(p_y[:], hs_lo[:, c], w_hi["d"][:, c], start=False, stop=(c == FC - 1))
                        i.then_inc(done["d"], 1)

                    def body(e, nth, last):
                        if nth != 0:
                            turn_hidden(e - 1)
                            pe.wait_ge(silu_ready, 2 * e)
                        pe.wait_ge(xt_lo_ready, e + 1)
                        wide_product("g", e, p_gate)
                        wide_product("u", e, p_up)
                        if not last:
                            turn_tokens(e + 1)
                        if nth != 0:
                            down(e - 1, nth == 1)

                    turn_tokens(0)
                    body(0, 0, False)
                    body(1, 1, False)
                    pe.wait_ge(list_ready, 1)
                    n = pe.value_load(later_tiles[:], min_val=0, max_val=MAXOV) + NX
                    with pe.Fori(2, n - 1) as e:
                        body(e, None, False)
                    body(n - 1, None, True)
                    turn_hidden(n - 1)
                    down(n - 1, False)

            with ExitStack() as f:
                rows = [stage["g"].rearrange("p c f -> p (c f)")[0:TP, 0:T * D].rearrange("p (t d) -> p t d", t=T),
                        stage["u"].rearrange("p c f -> p (c f)")[0:TP, 0:T * D].rearrange("p (t d) -> p t d", t=T)]
                block = f.enter_context(nc.Block())

                @block.gpsimd
                def _(pool):
                    for t in range(T):
                        for c, signal in enumerate((first_loaded, second_loaded)):
                            nc.gpsimd.indirect_dma_start(rows[c][:, t], None, y_dram,
                                                         bass.IndirectOffsetOnAxis(ap=y_at[:, c * T + t:c * T + t + 1].bitcast(U32), axis=0)
                                                         ).then_inc(signal[t], 16)

                @block.vector
                def _(dve):
                    v = nc.vector
                    for t in range(T):
                        dve.wait_ge(first_loaded[t], 16)
                        link("dve", dve, v.scalar_tensor_tensor(x_sb[:, t], rows[0][:, t], weight[:, 0, t:t + 1], x_sb[:, t], ALU.mult, ALU.add))
                        dve.wait_ge(second_loaded[t], 16)
                        v.scalar_tensor_tensor(x_sb[:, t], rows[1][:, t], weight[:, 1, t:t + 1], x_sb[:, t], ALU.mult, ALU.add).then_inc(combined, 1)

                @block.sync
                def _(sp):
                    for t in range(T):
                        sp.wait_ge(combined, t + 1)
                        sp.dma_start(out[t * TP:(t + 1) * TP, :], x_sb[:, t]).then_inc(out_stored, 16)
                    sp.wait_ge(out_stored, 16 * T)


NAMES = ["x", "src", "dst", "edge_type_8", "L0_gnn_W_self", "L0_gnn_b_self", "L0_gnn_W_rel", "L0_gnn_b_rel",
         "L0_ffn_router_w", "L0_ffn_gate_w", "L0_ffn_up_w", "L0_ffn_down_w"]


def kernel(**inputs):
    import numpy as np
    from concourse import bacc
    from concourse.bass_utils import run_bass_kernel_spmd

    nc = bacc.Bacc("TRN2", target_bir_lowering=False, num_devices=1)
    arrays = {f"in_{n}": np.ascontiguousarray(inputs[n]) for n in NAMES}
    args = [nc.dram_tensor(n, a.shape, mybir.dt.from_np(a.dtype), kind="ExternalInput").ap() for n, a in arrays.items()]
    out = nc.dram_tensor("out", (N, D), F32, kind="ExternalOutput").ap()
    build(nc, *args, out)
    result = run_bass_kernel_spmd(nc, [arrays], core_ids=[0])
    return result.results[0]["out"]
```

```python
from contextlib import ExitStack

import concourse.bass as bass
from concourse import mybir

F32 = mybir.dt.float32
F32R = mybir.dt.float32r
F16 = mybir.dt.float16
I32 = mybir.dt.int32
U32 = mybir.dt.uint32
ALU = mybir.AluOpType
ACT = mybir.ActivationFunctionType
AX = mybir.AxisListType

P = 128
N, D = 625, 512
TP, T = 125, 5
KC = D // P
R = 8
E = 10625
EP, EC = 125, 85
WIN = 18
NW = 36
NPAD = NW * WIN
KEYS = R * WIN
PAIR, PAIRS = 2 * TP, 3
ROUND = 3.0 * 2 ** 22
CH = 3
CAP = CH * P
ROUNDS = -(-E // CAP)
EDGES = 87 * P
KEY = 1024
NX, F = 16, 1024
FC = F // P
MAXOV = (2 * N - NX) // P
TILES = NX + MAXOV
FIXED = 1
AHEAD = 8
GROUPS = NX + FIXED
B_SELF = 32
LN_EPS = 1e-5


def build(nc, x, src, dst, edge_type, w_self, b_self, w_rel, b_rel, router_w, gate_w, up_w, down_w, out):
    ctx = ExitStack()
    with ctx:
        def sb(name, shape, dt, c=ctx):
            return c.enter_context(nc.sbuf_tensor(name, shape, dt))

        def ps(name, shape, dt, c):
            return c.enter_context(nc.psum_tensor(name, shape, dt))

        def sem(name):
            return ctx.enter_context(nc.semaphore(name))

        edges_dram = nc.dram_tensor("edges_dram", [EDGES, 2], F32).ap()
        ln2_dram = nc.dram_tensor("ln2_dram", [N, D], F32).ap()
        y_dram = nc.dram_tensor("y_dram", [TILES * P, D], F32).ap()

        ident = sb("ident", [P, P], F32)
        ident16 = sb("ident16", [P, P], F16)
        ones = sb("ones", [P, P], F32)
        x_sb = sb("x_sb", [TP, T, D], F32)
        agg_whole = sb("agg_whole", [P, T, D], F32)
        agg_sb = agg_whole[0:TP]
        stats = sb("stats", [TP, T, 6], F32)
        meanvar = sb("meanvar", [TP, T, 2], F32)
        rstd = sb("rstd", [TP, T], F32)
        stage_gate = sb("stage_gate", [P, KC, F], F32)
        before = sb("before", [TP, TP], F16)
        ones16 = sb("ones16", [TP, TP], F16)
        slot_iota = sb("slot_iota", [TP, P], F16)
        expert_iota = sb("expert_iota", [TP, NX], F32)
        tile_iota = sb("tile_iota", [1, TILES], F32)
        token_id = sb("token_id", [TP, T], F32)
        router_sb = sb("router_sb", [NX, D], F32)

        chain = {e: sem(f"{e}_chain") for e in ("dve", "act", "pool")}
        consts_ready = sem("consts_ready")
        x_loaded = sem("x_loaded")
        edge_loaded = sem("edge_loaded")
        small_loaded = sem("small_loaded")
        first_w_loaded = sem("first_w_loaded")
        edges_packed, edges_stored = sem("edges_packed"), sem("edges_stored")
        var_ready, root_ready, ln_ready = sem("var_ready"), sem("root_ready"), sem("ln_ready")
        tr_full, tr_hi = sem("tr_full"), sem("tr_hi")
        count_ready, count_full = sem("count_ready"), sem("count_full")

        zero_ready = sem("zero_ready")
        next_w_loaded = sem("next_w_loaded")
        self_full, self_added = sem("self_full"), sem("self_added")
        win_loaded = [sem(f"win_loaded{i}") for i in range(4)]
        onehot_ready, a_full, a_stored = sem("onehot_ready"), sem("a_full"), sem("a_stored")
        wa_loaded, wb_loaded = sem("wa_loaded"), sem("wb_loaded")
        t_full, wt_hi, wt_lo = sem("t_full"), sem("wt_hi"), sem("wt_lo")
        a_ready, at_ready = sem("a_ready"), sem("at_ready")
        h_full, h_hi, h_lo = sem("h_full"), sem("h_hi"), sem("h_lo")
        deg_full, deg_copied, agg_full = sem("deg_full"), sem("deg_copied"), sem("agg_full")
        agg_added = sem("agg_added")
        round_sems = range(zero_ready.num, agg_added.num + 1)
        assert len(round_sems) == 25

        route_consts = sem("route_consts")
        later_cleared = sem("later_cleared")
        router_full, router_copied = sem("router_full"), sem("router_copied")
        x2_full, x2_copied, logits_full = sem("x2_full"), sem("x2_copied"), sem("logits_full")
        ln2_stored, gap_ready, exp_ready = sem("ln2_stored"), sem("gap_ready"), sem("exp_ready")
        mask_ready, rank_full, places_ready = sem("mask_ready"), sem("rank_full"), sem("places_ready")
        slots_full, slots_ready, list_ready = sem("slots_full"), sem("slots_ready"), sem("list_ready")
        loaded = {k: [sem(f"{k}{i}_loaded") for i in range(2)] for k in "gud"}
        split_seen = sem("split_seen")
        split_hi = {k: sem(f"{k}_hi") for k in "gud"}
        split_lo = {k: sem(f"{k}_lo") for k in "gud"}
        done = {k: sem(f"{k}_done") for k in "gud"}
        ahead_loaded = [sem(f"ahead_loaded{i}") for i in range(2)]
        column_copied, column_waited, tokens_loaded = sem("column_copied"), sem("column_waited"), sem("tokens_loaded")
        xt_full, xt_hi_ready, xt_lo_ready = sem("xt_full"), sem("xt_hi_ready"), sem("xt_lo_ready")
        silu_ready, hid_ready = sem("silu_ready"), sem("hid_ready")
        ht_full, ht_hi_ready, ht_lo_ready = sem("ht_full"), sem("ht_hi_ready"), sem("ht_lo_ready")
        y_copied, y_stored, all_stored = sem("y_copied"), sem("y_stored"), sem("all_stored")
        first_loaded = [sem(f"first_loaded{t}") for t in range(T)]
        second_loaded = [sem(f"second_loaded{t}") for t in range(T)]
        combined, out_stored = sem("combined"), sem("out_stored")

        steps_done = {"dve": 0, "act": 0, "pool": 0}

        def link(name, engine, instruction):
            steps_done[name] += 1
            instruction.then_inc(chain[name], 1)
            engine.wait_ge(chain[name], steps_done[name])

        def variance(dve, xs, t):
            v = nc.vector
            link("dve", dve, v.bn_stats(stats[:, t], xs[:, t]))
            link("dve", dve, v.bn_aggr(meanvar[:, t], stats[:, t]))
            v.tensor_scalar(rstd[:, t:t + 1], meanvar[:, t, 1:2], LN_EPS, None, ALU.add).then_inc(var_ready, 1)

        def normalize(dve, xs, xn, nth, t):
            v = nc.vector
            dve.wait_ge(root_ready, T * nth + t + 1)
            link("dve", dve, v.reciprocal(rstd[:, t:t + 1], rstd[:, t:t + 1]))
            v.tensor_scalar(xn[:, t], xs[:, t], meanvar[:, t, 0:1], rstd[:, t:t + 1],
                            ALU.subtract, ALU.mult).then_inc(ln_ready, 1)

        def root(act, nth, t):
            act.wait_ge(var_ready, T * nth + t + 1)
            nc.scalar.activation(rstd[:, t:t + 1], rstd[:, t:t + 1], ACT.Sqrt).then_inc(root_ready, 1)

        with ExitStack() as g:
            a16 = sb("a16", [TP, T, R, NPAD], F16, g)
            xt_hi = sb("xt_hi", [P, KC, N], F32R, g)
            xt_lo = sb("xt_lo", [P, KC, N], F32R, g)
            w_nat = sb("w_nat", [P, 2, 4, D], F32, g)
            wt_hi_sb = sb("wt_hi_sb", [P, 2, KC, D], F32R, g)
            wt_lo_sb = sb("wt_lo_sb", [P, 2, KC, D], F32R, g)
            iota_row = sb("iota_row", [P, PAIRS * KEYS], F16, g)
            win_key = sb("win_key", [P, NW], F32, g)
            offs = sb("offs", [1, NW + 1], I32, g)
            bias = sb("bias", [B_SELF + 1, D], F32, g)
            first = sb("first", [P, 1], F32, g)

            def load_first(sp, slot, signal):
                sp.dma_start(w_nat[:, slot], (w_self if slot else w_rel[R]).rearrange("(c p) d -> p c d", p=P)).then_inc(signal, 16)

            with ExitStack() as f:
                xn = sb("xn", [TP, T, D], F32, f)
                iota_i = sb("iota_i", [P, PAIRS * KEYS], I32, f)
                e_src = sb("e_src", [EP, EC], I32, f)
                e_dst = sb("e_dst", [EP, EC + 1], I32, f)
                e_type = sb("e_type", [EP, EC], I32, f)
                e_winf = sb("e_winf", [EP, EC], F32, f)
                e_in = sb("e_in", [EP, EC], F32, f)
                e_pair = sb("e_pair", [EP, EC], F32, f)
                e_key = sb("e_key", [EP, EC], F32, f)
                e_pack = sb("e_pack", [EP, EC, 2], F32, f)
                e_pad = sb("e_pad", [7, 73, 2], F32, f)
                below = sb("below", [EP, NW + 1, EC], F32, f)
                win_f = sb("win_f", [EP, NW + 1], F32, f)
                counts = sb("counts", [EP, NW + 2], F32, f)
                crow = sb("crow", [1, NW + 2], F32, f)
                cdiff = sb("cdiff", [1, NW], F32, f)
                flags = sb("flags", [1, 4], F32, f)
                zero_rows = sb("zero_rows", [P, D], F32, f)
                token_id_i = sb("token_id_i", [TP, T], I32, f)
                expert_iota_i = sb("expert_iota_i", [TP, NX], I32, f)
                p_t = ps("p_t", [P, T, 512], F32, f)
                p_count = ps("p_count", [P, 512], F32, f)


                def token_columns(a, t):
                    return a[:, :, t * TP:(t + 1) * TP]

                def turned(t):
                    return p_t[:, t, 0:KC * TP].rearrange("p (c n) -> p c n", c=KC)

                block = f.enter_context(nc.Block())

                @block.sync
                def _(sp):
                    sp.dma_start(e_src[:], src.rearrange("(p c) -> p c", p=EP)).then_inc(edge_loaded, 16)
                    sp.dma_start(e_type[:], edge_type.rearrange("(p c) -> p c", p=EP)).then_inc(edge_loaded, 16)
                    sp.wait_ge(consts_ready, 1)
                    sp.dma_start(e_dst[0:EP - 1, :], bass.AP(dst.tensor, 0, [[EC, EP - 1], [1, EC + 1]])).then_inc(edge_loaded, 16)
                    sp.dma_start(e_dst[EP - 1:EP, 0:EC], dst[(EP - 1) * EC:E].rearrange("(a b) -> a b", a=1)).then_inc(edge_loaded, 16)
                    sp.dma_start(x_sb[:], x.rearrange("(t p) d -> p t d", p=TP)).then_inc(x_loaded, 16)
                    sp.dma_start(router_sb[:], router_w).then_inc(small_loaded, 16)
                    sp.dma_start(bias[0:2 * R], b_rel).then_inc(small_loaded, 16)
                    sp.dma_start(bias[B_SELF:B_SELF + 1], b_self.rearrange("(a d) -> a d", a=1)).then_inc(small_loaded, 16)
                    load_first(sp, 1, first_w_loaded)
                    load_first(sp, 0, first_w_loaded)
                    sp.wait_ge(edges_packed, 1)
                    sp.wait_ge(consts_ready, 5)
                    sp.dma_start(edges_dram[0:E, :].rearrange("(p c) k -> p (c k)", p=EP),
                                 e_pack[:].rearrange("p c k -> p (c k)")).then_inc(edges_stored, 16)
                    sp.dma_start(edges_dram[E:EDGES, :].rearrange("(p c) k -> p (c k)", p=7),
                                 e_pad[:].rearrange("p c k -> p (c k)")).then_inc(edges_stored, 16)
                    sp.wait_ge(route_consts, 1)
                    sp.dma_start(y_dram[NX * P:TILES * P, :].rearrange("(c p) d -> p c d", p=P),
                                 zero_rows[:].unsqueeze(1).to_broadcast([P, MAXOV, D])).then_inc(later_cleared, 16)
                    for i in range(2):
                        sp.dma_start(stage_gate[:, 2 * i:2 * i + 2], gate_w[0].rearrange("(c p) f -> p c f", p=P)[:, 2 * i:2 * i + 2]
                                     ).then_inc(loaded["g"][i], 16)
                    sp.wait_ge(edges_stored, 32)
                    sp.wait_ge(later_cleared, 16)
                    sp.wait_ge(small_loaded, 48)
                    sp.wait_ge(first_w_loaded, 32)

                @block.gpsimd
                def _(pool):
                    nc.gpsimd.memset(e_dst[:], 1 << 20).then_inc(consts_ready, 1)
                    nc.gpsimd.iota(iota_i[:], [[1, PAIRS * KEYS]], base=0, channel_multiplier=0).then_inc(consts_ready, 1)
                    nc.gpsimd.memset(ones[:], 1.0).then_inc(consts_ready, 1)
                    pool.wait_ge(consts_ready, 3)
                    nc.gpsimd.affine_select(out=ident[:], in_=ones[:], compare_op=ALU.is_equal, fill=0.0, base=0,
                                            pattern=[[-1, P]], channel_multiplier=1).then_inc(consts_ready, 1)
                    nc.gpsimd.memset(e_pad[:], -1.0).then_inc(consts_ready, 1)
                    nc.gpsimd.memset(zero_rows[:], 0.0).then_inc(route_consts, 1)
                    nc.gpsimd.memset(agg_sb[:], 0.0)
                    nc.gpsimd.memset(first[:], 1.0)
                    nc.gpsimd.affine_select(out=before[:], in_=ones[0:TP, 0:TP], compare_op=ALU.is_gt, fill=0.0, base=0,
                                            pattern=[[1, TP]], channel_multiplier=-1)
                    nc.gpsimd.tensor_copy(ones16[:], ones[0:TP, 0:TP])
                    nc.gpsimd.iota(token_id_i[:], [[TP, T]], base=0, channel_multiplier=1)
                    link("pool", pool, nc.gpsimd.iota(expert_iota_i[:], [[1, NX]], base=0, channel_multiplier=0))
                    nc.gpsimd.tensor_copy(token_id[:], token_id_i[:])
                    nc.gpsimd.tensor_copy(expert_iota[:], expert_iota_i[:])
                    pool.wait_ge(consts_ready, 5)
                    nc.gpsimd.tensor_copy(slot_iota[:], iota_i[0:TP, 0:P])
                    nc.gpsimd.tensor_copy(tile_iota[:], iota_i[0:1, 0:TILES])

                @block.vector
                def _(dve):
                    v = nc.vector
                    dve.wait_ge(edge_loaded, 64)
                    dve.wait_ge(consts_ready, 2)
                    link("dve", dve, v.tensor_scalar(e_winf[:], e_dst[:, 0:EC], (WIN - 1) / 2, 1 / WIN, ALU.subtract, ALU.mult))
                    link("dve", dve, v.tensor_scalar(e_winf[:], e_winf[:], ROUND, None, ALU.add))
                    v.tensor_scalar(e_winf[:], e_winf[:], ROUND, None, ALU.subtract)
                    v.tensor_scalar(e_pair[:], e_src[:], float(PAIR), None, ALU.is_ge)
                    v.tensor_copy(iota_row[:], iota_i[:])
                    v.tensor_scalar(win_key[:], iota_i[:, 0:NW], float(KEY), None, ALU.mult)
                    link("dve", dve, v.tensor_tensor(below[:, 0, :], e_dst[:, 0:EC], e_dst[:, 1:EC + 1], ALU.is_gt))
                    v.scalar_tensor_tensor(e_in[:], e_winf[:], -float(WIN), e_dst[:, 0:EC], ALU.mult, ALU.add)
                    link("dve", dve, v.scalar_tensor_tensor(e_pair[:], e_src[:], 2.0 * PAIR, e_pair[:], ALU.is_ge, ALU.add))
                    v.tensor_copy(win_f[:], iota_i[0:EP, 0:NW + 1])
                    v.tensor_reduce(counts[:, NW + 1:NW + 2], below[:, 0, :], AX.X, ALU.add)
                    v.scalar_tensor_tensor(e_pack[:, :, 1], e_pair[:], -float(PAIR), e_src[:], ALU.mult, ALU.add)
                    link("dve", dve, v.scalar_tensor_tensor(e_key[:], e_type[:], float(WIN), e_in[:], ALU.mult, ALU.add))
                    link("dve", dve, v.scalar_tensor_tensor(e_key[:], e_pair[:], float(KEYS), e_key[:], ALU.mult, ALU.add))
                    v.scalar_tensor_tensor(e_pack[:, :, 0], e_winf[:], float(KEY), e_key[:], ALU.mult, ALU.add).then_inc(edges_packed, 1)
                    link("dve", dve, v.tensor_tensor(below[:], e_winf[:].unsqueeze(1).to_broadcast([EP, NW + 1, EC]),
                                                    win_f[:].unsqueeze(2).to_broadcast([EP, NW + 1, EC]), ALU.is_lt))
                    v.tensor_reduce(counts[:, 0:NW + 1], below[:], AX.X, ALU.add).then_inc(count_ready, 1)
                    dve.wait_ge(x_loaded, 16)
                    for t in range(T + 1):
                        if t < T:
                            variance(dve, x_sb, t)
                        if t > 0:
                            normalize(dve, x_sb, xn, 0, t - 1)
                    dve.wait_ge(count_full, 1)
                    link("dve", dve, v.tensor_copy(crow[:], p_count[0:1, 0:NW + 2]))
                    link("dve", dve, v.tensor_tensor(cdiff[:], crow[:, 1:NW + 1], crow[:, 0:NW], ALU.subtract))
                    link("dve", dve, v.tensor_reduce(flags[:, 0:1], cdiff[:], AX.X, ALU.max))
                    link("dve", dve, v.tensor_scalar(flags[:, 1:2], flags[:, 0:1], float(CAP), None, ALU.is_gt))
                    link("dve", dve, v.tensor_tensor(flags[:, 2:3], flags[:, 1:2], crow[:, NW + 1:NW + 2], ALU.add))
                    link("dve", dve, v.tensor_scalar(flags[:, 3:4], flags[:, 2:3], 0.0, None, ALU.is_equal))
                    v.tensor_scalar(offs[:, 0:NW], crow[:, 0:NW], flags[:, 3:4], None, ALU.mult)
                    v.tensor_scalar(offs[:, NW:NW + 1], flags[:, 3:4], float(1 - ROUNDS), float(ROUNDS), ALU.mult, ALU.add)
                    for t in range(T):
                        dve.wait_ge(tr_hi, t + 1)
                        v.tensor_tensor(token_columns(xt_lo, t), turned(t), token_columns(xt_hi, t).bitcast(F32),
                                        ALU.subtract)

                @block.scalar
                def _(act):
                    s = nc.scalar
                    for t in range(T):
                        root(act, 0, t)
                    act.wait_ge(consts_ready, 4)
                    s.copy(ident16[:], ident[:])
                    for t in range(T):
                        act.wait_ge(tr_full, t + 1)
                        s.copy(token_columns(xt_hi, t), turned(t)).then_inc(tr_hi, 1)

                @block.tensor
                def _(pe):
                    m = nc.tensor
                    pe.wait_ge(count_ready, 1)
                    pe.wait_ge(consts_ready, 4)
                    m.matmul(p_count[0:1, 0:NW + 2], ones[0:EP, 0:1], counts[:], start=True, stop=True).then_inc(count_full, 1)
                    for t in range(T):
                        pe.wait_ge(ln_ready, t + 1)
                        for dc in range(KC):
                            i = m.transpose(p_t[:, t, dc * TP:(dc + 1) * TP], xn[:, t, dc * P:(dc + 1) * P], ident[0:TP, 0:TP])
                        i.then_inc(tr_full, 1)

            with ExitStack() as f:
                win_edges = sb("win_edges", [P, 4, CH, 2], F32, f)
                key_hot = sb("key_hot", [P, 2, CH, PAIRS * KEYS], F16, f)
                src_hot = sb("src_hot", [P, 2, CH, PAIR], F16, f)
                lhs_a = sb("lhs_a", [TP, T, N], F32R, f)
                lhs_at = sb("lhs_at", [TP, T, N], F32R, f)
                h_hi_sb = sb("h_hi_sb", [TP, 2, D], F32R, f)
                h_lo_sb = sb("h_lo_sb", [TP, 2, D], F32R, f)
                degree = sb("degree", [TP, T, 2 * R], F32, f)
                degree_t = sb("degree_t", [2 * R, N], F32, f)
                zero_row = sb("zero_row", [1, D], F32R, f)
                p_agg = ps("p_agg", [P, T, 512], F32, f)
                p_h = ps("p_h", [P, 2, 512], F32, f)
                p_tr = ps("p_tr", [P, 512], F32, f)
                p_first = [p_tr[:], p_agg[:, 4], p_h[:, 1], p_h[:, 0]]

                p_tr16 = p_tr[0:TP].bitcast(F16)[:, 0:T * (TP + 1)].rearrange("p (t n) -> p t n", t=T)

                rounds = nc.values_load(offs[0:1, NW:NW + 1], min_val=1, max_val=ROUNDS)
                with nc.Fori(0, rounds):
                    with nc.Block() as block:
                        @block.sync
                        def _(sp):
                            def w_load(slot, m, signal):
                                sp.dma_start(w_nat[:, slot], w_rel[m].rearrange("(c p) d -> p c d", p=P)
                                             if isinstance(m, int) else
                                             w_rel[bass.ds(m, 1)].rearrange("a (c p) d -> p (a c) d", p=P)).then_inc(signal, 16)

                            def window(q, k):
                                at = sp.value_load(offs[0:1, bass.ds(4 * q + k, 1)], min_val=0, max_val=EDGES - CAP)
                                sp.dma_start(win_edges[:, k], edges_dram[bass.ds(at, CAP), :].rearrange("(p c) k -> p c k", c=CH)
                                             ).then_inc(win_loaded[k], 16)

                            for k in range(4):
                                window(0, k)
                            sp.wait_ge(t_full, KC)
                            w_load(1, 0, wb_loaded)
                            with sp.Fori(1, NW // 4) as q:
                                for k in range(4):
                                    sp.wait_ge(onehot_ready, 4 * q + k - 3)
                                    window(q, k)
                            with sp.Fori(0, R - 1) as r:
                                sp.wait_ge(t_full, 13 * r + 8)
                                w_load(0, r + R + 1, wa_loaded)
                                sp.wait_ge(t_full, 13 * r + 15)
                                w_load(1, r + 1, wb_loaded)
                            sp.wait_ge(t_full, 13 * (R - 1) + 8)
                            load_first(sp, 0, next_w_loaded)
                            sp.wait_ge(t_full, 13 * (R - 1) + 15)
                            load_first(sp, 1, next_w_loaded)
                            sp.wait_ge(next_w_loaded, 32)

                        @block.vector
                        def _(dve):
                            v = nc.vector
                            v.memset(zero_row[:].bitcast(F32), 0.0).then_inc(zero_ready, 1)

                            def window(q, k):
                                dve.wait_ge(win_loaded[k], 16 * q + 16)
                                if not (isinstance(q, int) and q == 0 and k < 2):
                                    dve.wait_ge(a_full, 4 * q + k - 1)
                                for c in range(CH):
                                    v.tensor_scalar(key_hot[:, k % 2, c], iota_row[:], win_key[:, bass.ds(4 * q + k, 1)],
                                                    win_edges[:, k, c, 0:1], ALU.add, ALU.is_equal)
                                for c in range(CH):
                                    i = v.tensor_scalar(src_hot[:, k % 2, c], iota_row[:, 0:PAIR], win_edges[:, k, c, 1:2], None, ALU.is_equal)
                                i.then_inc(onehot_ready, 1)

                            def w_low(slot, dc, hi, bank=p_tr[:]):
                                dve.wait_ge(wt_hi, hi)
                                v.tensor_tensor(wt_lo_sb[:, slot, dc], bank, wt_hi_sb[:, slot, dc].bitcast(F32),
                                                ALU.subtract).then_inc(wt_lo, 1)

                            def h_low(n, hi):
                                dve.wait_ge(h_hi, hi)
                                v.tensor_tensor(h_lo_sb[:, n % 2], p_h[0:TP, n % 2], h_hi_sb[:, n % 2].bitcast(F32),
                                                ALU.subtract).then_inc(h_lo, 1)

                            for dc in range(KC):
                                w_low(1, dc, dc + 1, p_first[dc])
                            for q in range(T + 1):
                                for k in range(4):
                                    window(q, k)
                                    if q > 0 and k == 1:
                                        dve.wait_ge(self_full, q)
                                        v.scalar_tensor_tensor(agg_sb[:, q - 1], p_h[0:TP, (q - 1) % 2], first[0:TP], agg_sb[:, q - 1],
                                                               ALU.mult, ALU.add).then_inc(self_added, 1)
                                    if q == T and k >= 2:
                                        for dc in (2 * k - 4, 2 * k - 3):
                                            w_low(0, dc, KC + dc + 1, p_first[dc])
                            with dve.Fori(T + 1, NW // 4) as q:
                                for k in range(4):
                                    window(q, k)
                            h_low(0, 1)
                            v.tensor_scalar(offs[:, 0:NW], offs[:, 0:NW], float(CAP), None, ALU.add)

                            def steps(r, last):
                                for n in range(2 * T):
                                    if n < 2 * T - 1 or not last:
                                        h_low(n + 1, 10 * r + n + 2)
                                    if n < KC:
                                        w_low(1, n, 8 * r + 8 + n + 1)
                                    if n >= T and n < T + KC and not last:
                                        w_low(0, n - T, 8 * r + 12 + n - T + 1)

                            with dve.Fori(0, R - 1) as r:
                                steps(r, False)
                            steps(R - 1, True)
                            dve.wait_ge(deg_full, 1)
                            v.tensor_copy(degree_t[:, 0:4 * TP], p_tr[0:2 * R, 0:4 * TP])
                            v.tensor_copy(degree_t[:, 4 * TP:N], p_h[0:2 * R, 0, 0:TP]).then_inc(deg_copied, 1)
                            for t in range(T):
                                dve.wait_ge(agg_full, t + 1)
                                v.tensor_tensor(agg_sb[:, t], agg_sb[:, t], p_agg[0:TP, t], ALU.add).then_inc(agg_added, 1)
                            v.memset(first[:], 0.0)

                        @block.scalar
                        def _(act):
                            s = nc.scalar

                            def w_high(slot, dc, full, bank=p_tr[:]):
                                act.wait_ge(t_full, full)
                                s.copy(wt_hi_sb[:, slot, dc], bank).then_inc(wt_hi, 1)

                            def h_high(n, full):
                                act.wait_ge(h_full, full)
                                s.copy(h_hi_sb[:, n % 2], p_h[0:TP, n % 2]).then_inc(h_hi, 1)

                            def a_direct(r, st):
                                s.activation(lhs_a[:, st], a16[:, st, r, 0:N] if isinstance(r, int) else a16[:, st, bass.ds(r, 1), 0:N].rearrange("p a n -> p (a n)"),
                                             ACT.Copy, accum_out=degree[:, st, bass.ds(r, 1)]).then_inc(a_ready, 1)

                            def a_turned(r, dt, full):
                                act.wait_ge(t_full, full)
                                s.activation(lhs_at[:, dt].rearrange("p (t n) -> p t n", t=T), p_tr16[:, :, 0:TP], ACT.Copy,
                                             accum_out=degree[:, dt, bass.ds(r + R, 1)]).then_inc(at_ready, 1)

                            def store_counts(q, k):
                                act.wait_ge(a_full, 4 * q + k + 1)
                                for x in range(2):
                                    tiles = (T + 1 - x) // 2
                                    i = s.copy(a16[:, x::2, :, bass.ds((4 * q + k) * WIN, WIN)],
                                               p_agg[0:TP, 2 * (k % 2) + x, 0:tiles * KEYS].rearrange("p (t r d) -> p t r d", t=tiles, r=R))
                                i.then_inc(a_stored, 1)

                            for dc in range(KC):
                                w_high(1, dc, dc + 1, p_first[dc])
                            with act.Fori(0, T) as q:
                                for k in range(4):
                                    store_counts(q, k)
                            for k in range(4):
                                store_counts(T, k)
                                if k < 2:
                                    for dc in (2 * k, 2 * k + 1):
                                        w_high(0, dc, KC + dc + 1, p_first[dc])
                            h_high(0, 1)
                            with act.Fori(T + 1, NW // 4) as q:
                                for k in range(4):
                                    store_counts(q, k)
                            act.wait_ge(a_stored, NW)
                            for st in range(T):
                                a_direct(0, st)

                            def steps(r, last):
                                base = 13 * r + 8
                                g = 0
                                for n in range(2 * T):
                                    if n < 2 * T - 1 or not last:
                                        h_high(n + 1, 10 * r + n + 2)
                                    if n < KC:
                                        g += 1
                                        w_high(1, n, base + g)
                                    if n < T:
                                        g += 1
                                        a_turned(r, n, base + g)
                                    if n >= T and not last:
                                        if n < T + KC:
                                            g += 1
                                            w_high(0, n - T, base + g)
                                        a_direct(r + 1, n - T)

                            with act.Fori(0, R - 1) as r:
                                steps(r, False)
                            steps(R - 1, True)

                        @block.tensor
                        def _(pe):
                            m = nc.tensor

                            def w_turn(slot, dc, bank=p_tr[:]):
                                for oc in range(4):
                                    i = m.transpose(bank[:, oc * P:(oc + 1) * P], w_nat[:, slot, oc, dc * P:(dc + 1) * P], ident[:])
                                i.then_inc(t_full, 1)

                            def a_turn(r, dt):
                                for st in range(T):
                                    i = m.transpose(p_tr16[:, st, 0:TP],
                                                    a16[:, st, bass.ds(r, 1), dt * TP:(dt + 1) * TP].rearrange("p a n -> p (a n)"),
                                                    ident16[0:TP, 0:TP])
                                i.then_inc(t_full, 1)

                            def split_product(o, slot, t, dc, start, stop):
                                at = slice(t * TP, (t + 1) * TP)
                                m.matmul(o, xt_hi[:, dc, at], wt_hi_sb[:, slot, dc], start=start, stop=False)
                                m.matmul(o, xt_hi[:, dc, at], wt_lo_sb[:, slot, dc], start=False, stop=False)
                                return m.matmul(o, xt_lo[:, dc, at], wt_hi_sb[:, slot, dc], start=False, stop=stop)

                            def h_product(n):
                                for dc in range(KC):
                                    i = split_product(p_h[0:TP, n % 2], (n // T) % 2, n % T, dc, start=(dc == 0), stop=(dc == KC - 1))
                                i.then_inc(h_full, 1)

                            def add_messages(n):
                                lhs = lhs_a if n < T else lhs_at
                                for t in range(T):
                                    w = lhs[:, n % T, t * TP:(t + 1) * TP]
                                    m.matmul(p_agg[0:TP, t], w, h_hi_sb[:, n % 2], start=False, stop=False)
                                    i = m.matmul(p_agg[0:TP, t], w, h_lo_sb[:, n % 2], start=False, stop=False)

                            def window(q, k):
                                pe.wait_ge(onehot_ready, 4 * q + k + 1)
                                if not (isinstance(q, int) and q == 0 and k < 2):
                                    pe.wait_ge(a_stored, 4 * q + k - 1)
                                for x in range(2):
                                    wide = (T + 1 - x) // 2 * KEYS
                                    for c in range(CH):
                                        i = m.matmul(p_agg[0:TP, 2 * (k % 2) + x, 0:wide], src_hot[:, k % 2, c, x * TP:(x + 1) * TP],
                                                     key_hot[:, k % 2, c, 0:wide], start=(c == 0), stop=(c == CH - 1))
                                i.then_inc(a_full, 1)

                            for dc in range(KC):
                                w_turn(1, dc, p_first[dc])
                            for t in range(T):
                                if t >= 2:
                                    pe.wait_ge(self_added, t - 1)
                                if t == 0:
                                    pe.wait_ge(wt_lo, KC)
                                m.matmul(p_h[0:TP, t % 2], ones[B_SELF:B_SELF + 1, 0:TP], bias[B_SELF:B_SELF + 1], start=True, stop=False)
                                for k in range(4):
                                    i = split_product(p_h[0:TP, t % 2], 1, t, k, start=False, stop=(k == KC - 1))
                                    if k == KC - 1:
                                        i.then_inc(self_full, 1)
                                    window(t, k)
                            for k in range(4):
                                window(T, k)
                                if k == 1:
                                    pe.wait_ge(self_added, T)
                                if k < 2:
                                    w_turn(0, 2 * k, p_first[2 * k])
                                    w_turn(0, 2 * k + 1, p_first[2 * k + 1])
                            pe.wait_ge(wt_lo, 2 * KC)
                            h_product(0)
                            with pe.Fori(T + 1, NW // 4) as q:
                                for k in range(4):
                                    window(q, k)
                            pe.wait_ge(a_stored, NW)
                            pe.wait_ge(zero_ready, 1)
                            for t in range(T):
                                m.matmul(p_agg[0:TP, t], zero_row[:, 0:TP], zero_row[:], start=True, stop=False)

                            def steps(r, last):
                                for n in range(2 * T):
                                    if n < 2 * T - 1 or not last:
                                        if n + 1 == T:
                                            pe.wait_ge(wt_lo, 8 * r + 12)
                                        if n + 1 == 2 * T:
                                            pe.wait_ge(wt_lo, 8 * r + 16)
                                        h_product((n + 1) % (2 * T))
                                    if n < KC:
                                        if n == 0:
                                            pe.wait_ge(wb_loaded, 16 * r + 16)
                                            pe.wait_ge(wt_lo, 8 * r + 8)
                                        else:
                                            pe.wait_ge(at_ready, 5 * r + n)
                                        w_turn(1, n)
                                    if T <= n < T + KC and not last:
                                        if n == T:
                                            pe.wait_ge(wa_loaded, 16 * r + 16)
                                            pe.wait_ge(at_ready, 5 * r + T)
                                        else:
                                            pe.wait_ge(wt_lo, 8 * r + 12 + n - T)
                                        w_turn(0, n - T)
                                    pe.wait_ge(h_lo, 10 * r + n + 1)
                                    if n < T:
                                        pe.wait_ge(a_ready, 5 * r + n + 1)
                                    else:
                                        pe.wait_ge(at_ready, 5 * r + n - T + 1)
                                    add_messages(n)
                                    if n < T:
                                        if n < KC:
                                            pe.wait_ge(wt_lo, 8 * r + 8 + n + 1)
                                        else:
                                            pe.wait_ge(at_ready, 5 * r + n)
                                        a_turn(r, n)

                            with pe.Fori(0, R - 1) as r:
                                steps(r, False)
                            steps(R - 1, True)
                            pe.wait_ge(at_ready, R * T)
                            pe.wait_ge(a_ready, R * T)
                            for t in range(T):
                                o = p_tr[0:2 * R, t * TP:(t + 1) * TP] if t < 4 else p_h[0:2 * R, 0, 0:TP]
                                i = m.transpose(o, degree[:, t], ident[0:TP, 0:TP])
                            i.then_inc(deg_full, 1)
                            pe.wait_ge(deg_copied, 1)
                            for t in range(T):
                                m.matmul(p_agg[0:TP, t], degree_t[:, t * TP:(t + 1) * TP], bias[0:2 * R],
                                         start=False, stop=True).then_inc(agg_full, 1)

                    nc.all_engine_barrier(sems_to_clear=round_sems)

        w_dram = {"g": gate_w, "u": up_w, "d": down_w}
        with ExitStack() as g:
            stage = {"g": stage_gate[:], "u": sb("stage_up", [P, KC, F], F32, g)[:],
                     "d": sb("stage_down", [P, FC, D], F32, g)[:]}
            shape = {"g": [P, KC, F], "u": [P, KC, F], "d": [P, FC, D]}
            w_hi = {k: sb(f"{k}_hi_sb", shape[k], F32R, g) for k in "gud"}
            w_lo = {k: sb(f"{k}_lo_sb", shape[k], F32R, g) for k in "gud"}
            tokens = sb("tokens", [P, D], F32, g)
            slot_token = sb("slot_token", [P, T * NX], I32, g)
            column = sb("column", [P, 1], I32, g)
            xs_hi = sb("xs_hi", [P, KC, P], F32R, g)
            xs_lo = sb("xs_lo", [P, KC, P], F32R, g)
            silu = sb("silu", [P, F], F32, g)
            hid = sb("hid", [P, F], F32, g)
            gate_ahead = sb("gate_ahead", [P, 2 * F], F32, g)
            hs_hi = sb("hs_hi", [P, FC, P], F32R, g)
            hs_lo = sb("hs_lo", [P, FC, P], F32R, g)
            y_sb = sb("y_sb", [P, D], F32, g)
            ahead = [a.rearrange("p (c f) -> p c f", f=F)
                     for a in (agg_whole[:].rearrange("p t d -> p (t d)")[:, 0:2 * F], gate_ahead[:])]
            router_t = sb("router_t", [P, KC, NX], F32, g)
            logits = sb("logits", [TP, T, NX], F32, g)
            rest = sb("rest", [TP, T, NX], F32, g)
            cand = sb("cand", [TP, T, NX], F32, g)
            hot = sb("hot", [TP, 2, T, NX], F32, g)
            mask = sb("mask", [TP, T + 1, NX], F16, g)
            xt2 = hid[:, 0:2 * KC * TP].rearrange("p (b c n) -> p b c n", b=2, c=KC)
            slot_hot = silu[0:TP].bitcast(F16)[:, 0:2 * T * P].rearrange("p (c n) -> p c n", c=2 * T)
            named = sb("named", [TP, 2, T, NX], F32, g)
            tag = sb("tag", [TP, 2 * T, T, NX], F16, g)
            best = sb("best", [TP, 2, T], F32, g)
            choice = sb("choice", [TP, 2, T], F32, g)
            rank = sb("rank", [TP, T + 1, NX], F32, g)
            picked = sb("picked", [TP, 2, T, NX], F32, g)
            place = sb("place", [TP, 2, T], F32, g)
            nth_tile = sb("nth_tile", [TP, 2, T], F32, g)
            later = sb("later", [TP, 2, T], F32, g)
            step = sb("step", [TP, 2, T], F32, g)
            y_at = sb("y_at", [TP, 2 * T], I32, g)
            weight = sb("weight", [TP, 2, T], F32, g)
            gap = sb("gap", [TP, T], F32, g)
            extra = sb("extra", [TP, NX], F32, g)
            in_group = sb("in_group", [TP, GROUPS], F32, g)
            upto = sb("upto", [TP, 2, GROUPS], F32, g)
            moved = sb("moved", [TP, NX], F32, g)
            moved_by = sb("moved_by", [TP, 2, T], F32, g)
            le = hid[0:1, 0:2 * TILES * GROUPS].rearrange("p (a i g) -> p a i g", a=2, i=TILES)
            list_f = sb("list_f", [1, 4, TILES], F32, g)
            tile_kept = sb("tile_kept", [1, TILES], I32, g)
            tile_expert = sb("tile_expert", [1, TILES], I32, g)
            tile_column = sb("tile_column", [1, TILES], I32, g)
            later_tiles = sb("later_tiles", [1, 1], I32, g)

            xn2 = agg_sb

            def w_piece(k, e, i):
                w = w_dram[k][e] if isinstance(e, int) else w_dram[k][bass.ds(e, 1)].rearrange("a r f -> (a r) f")
                rows = w.shape[0] // 2
                return w[i * rows:(i + 1) * rows, :].rearrange("(c p) f -> p c f", p=P)

            def half(ap, k, i):
                c = shape[k][1] // 2
                return ap[:, i * c:(i + 1) * c]

            def is_ahead(k, e):
                return k == "g" and isinstance(e, int) and e == AHEAD

            def staged(k, e, i):
                return ahead[i] if is_ahead(k, e) else half(stage[k], k, i)

            def as_down(ap):
                return ap.rearrange("p c f -> p (c f)").rearrange("p (c f) -> p c f", f=D)

            with ExitStack() as f:
                p_gate = ps("p_gate", [P, F], F32, f)
                p_up = ps("p_up", [P, F], F32, f)
                p_ht = ps("p_ht", [P, F], F32, f)
                p_x = ps("p_x", [P, 512], F32, f)
                p_y = ps("p_y", [P, 512], F32, f)
                p_t = [p_gate[:, 0:KC * TP], p_gate[:, 512:512 + KC * TP]]
                p_router = p_y[:, 0:KC * NX].rearrange("p (c e) -> p c e", c=KC)
                p_logits = p_up[0:TP, 0:T * NX].rearrange("p (t e) -> p t e", t=T)
                p_rank = p_ht[0:TP, 0:(T + 1) * NX].rearrange("p (t e) -> p t e", t=T + 1)
                p_slots = p_up[:, 512:512 + T * NX]
                block = f.enter_context(nc.Block())

                @block.sync
                def _(sp):
                    def load(k, e, i):
                        sp.dma_start(half(stage[k], k, i), w_piece(k, e, i)).then_inc(loaded[k][i], 16)

                    load("u", 0, 0)
                    load("u", 0, 1)
                    load("d", 0, 0)
                    load("d", 0, 1)
                    sp.wait_ge(ln_ready, 2 * T)
                    sp.dma_start(ln2_dram.rearrange("(t p) d -> p t d", p=TP), xn2[:]).then_inc(ln2_stored, 16)

                    def reload(k, e, expert):
                        for i in range(2):
                            sp.wait_ge(split_lo[k], 2 * e - 1 + i)
                            load(k, expert, i)

                    def listed(e):
                        return sp.value_load(tile_expert[0:1, bass.ds(e, 1)], min_val=0, max_val=NX - 1)

                    for k in "gud":
                        reload(k, 1, 1)
                    sp.wait_ge(list_ready, 1)
                    n = sp.value_load(later_tiles[:], min_val=0, max_val=MAXOV) + NX

                    def reload_or_keep(k, e):
                        expert, kept = listed(e), sp.value_load(tile_kept[0:1, bass.ds(e, 1)], min_val=0, max_val=1)
                        for i in range(2):
                            sp.wait_ge(split_lo[k], 2 * e - 1 + i)
                            sp.sem_inc(split_seen, 1)
                            with sp.If(kept < 1):
                                load(k, expert, i)
                            with sp.If(kept > 0):
                                sp.sem_inc(loaded[k][i], 16)

                    for e in (2, 3):
                        reload_or_keep("g", e)
                        reload_or_keep("u", e)
                    def next_tiles(e):
                        reload_or_keep("d", e)
                        reload_or_keep("g", e + 2)
                        reload_or_keep("u", e + 2)

                    expert = listed(AHEAD)
                    sp.wait_ge(ln2_stored, 16)
                    sp.wait_ge(x2_full, T)
                    for i in range(2):
                        sp.dma_start(ahead[i], w_piece("g", expert, i)).then_inc(ahead_loaded[i], 16)
                    with sp.Fori(2, AHEAD - 2) as e:
                        next_tiles(e)
                    reload_or_keep("d", AHEAD - 2)
                    reload_or_keep("u", AHEAD)
                    reload_or_keep("d", AHEAD - 1)
                    expert = listed(AHEAD + 1)
                    for i in range(2):
                        sp.wait_ge(split_lo["g"], 2 * (AHEAD - 1) + i + 1)
                        load("g", expert, i)
                    reload_or_keep("u", AHEAD + 1)
                    with sp.Fori(AHEAD, n - 2) as e:
                        next_tiles(e)
                    reload_or_keep("d", n - 2)
                    last = listed(n - 1)
                    for i in range(2):
                        sp.wait_ge(split_lo["g"], 2 * n - 1 + i)
                        sp.dma_start(as_down(half(stage["g"], "g", i)), w_piece("d", last, i)).then_inc(loaded["g"][i], 16)

                @block.gpsimd
                def _(pool):
                    q = nc.gpsimd

                    def gather(e, at):
                        q.tensor_copy(column[:], slot_token[:, bass.ds(at, 1)]).then_inc(column_copied, 1)
                        pool.wait_ge(column_copied, e + 1)
                        pool.sem_inc(column_waited, 1)
                        q.indirect_dma_start(tokens[:], None, ln2_dram, bass.IndirectOffsetOnAxis(ap=column[:].bitcast(U32), axis=0)
                                             ).then_inc(tokens_loaded, 16)

                    pool.wait_ge(ln2_stored, 16)
                    pool.wait_ge(slots_ready, 1)
                    gather(0, 0)
                    pool.wait_ge(xt_full, 1)
                    gather(1, 1)
                    pool.wait_ge(list_ready, 1)
                    n = pool.value_load(later_tiles[:], min_val=0, max_val=MAXOV) + NX
                    with pool.Fori(2, n) as e:
                        pool.wait_ge(xt_full, e)
                        gather(e, pool.value_load(tile_column[0:1, bass.ds(e, 1)], min_val=0, max_val=T * NX - 1))

                @block.vector
                def _(dve):
                    v = nc.vector

                    dve.wait_ge(router_full, 1)
                    v.tensor_copy(router_t[:], p_router).then_inc(router_copied, 1)
                    v.memset(mask[:, T], 0.0)
                    for t in range(T + 1):
                        if t < T:
                            link("dve", dve, v.scalar_tensor_tensor(x_sb[:, t], agg_sb[:, t], 0.0, x_sb[:, t], ALU.max, ALU.add))
                            variance(dve, x_sb, t)
                        if t > 0:
                            normalize(dve, x_sb, xn2, 1, t - 1)

                    def low(k, e, i):
                        dve.wait_ge(split_hi[k], 2 * e + i + 1)
                        v.tensor_tensor(half(w_lo[k][:], k, i), staged(k, e, i), half(w_hi[k][:], k, i).bitcast(F32),
                                        ALU.subtract).then_inc(split_lo[k], 1)

                    def x_low(e):
                        dve.wait_ge(xt_hi_ready, e + 1)
                        v.tensor_tensor(xs_lo[:].rearrange("p c n -> p (c n)"), p_x[:], xs_hi[:].rearrange("p c n -> p (c n)").bitcast(F32),
                                        ALU.subtract).then_inc(xt_lo_ready, 1)

                    def hidden(e):
                        dve.wait_ge(done["u"], e + 1)
                        for i in range(2):
                            dve.wait_ge(silu_ready, 2 * e + i + 1)
                            v.tensor_tensor(hid[:, i * 512:(i + 1) * 512], silu[:, i * 512:(i + 1) * 512], p_up[:, i * 512:(i + 1) * 512],
                                            ALU.mult).then_inc(hid_ready, 1)

                    def h_low(e):
                        for i in range(2):
                            dve.wait_ge(ht_hi_ready, 2 * e + i + 1)
                            v.tensor_tensor(hs_lo[:, 4 * i:4 * i + 4].rearrange("p c n -> p (c n)"), p_ht[:, i * 512:(i + 1) * 512],
                                            hs_hi[:, 4 * i:4 * i + 4].rearrange("p c n -> p (c n)").bitcast(F32),
                                            ALU.subtract).then_inc(ht_lo_ready, 1)

                    low("g", 0, 0)
                    low("g", 0, 1)
                    dve.wait_ge(logits_full, T)
                    link("dve", dve, v.tensor_copy(logits[:], p_logits))
                    iota = expert_iota[:].unsqueeze(1).to_broadcast([TP, T, NX])

                    def wide(a):
                        return a.unsqueeze(2).to_broadcast([TP, T, NX])

                    for c in range(2):
                        src_logits = logits if c == 0 else rest
                        link("dve", dve, v.tensor_reduce(best[:, c], src_logits[:], AX.X, ALU.max))
                        link("dve", dve, v.tensor_tensor(cand[:], src_logits[:], wide(best[:, c]), ALU.not_equal))
                        link("dve", dve, v.scalar_tensor_tensor(cand[:], cand[:], float(NX), iota, ALU.mult, ALU.add))
                        link("dve", dve, v.tensor_reduce(choice[:, c], cand[:], AX.X, ALU.min))
                        link("dve", dve, v.tensor_tensor(hot[:, c], iota, wide(choice[:, c]), ALU.is_equal))
                        if c == 0:
                            link("dve", dve, v.scalar_tensor_tensor(rest[:], hot[:, 0], -3.0e38, logits[:], ALU.mult, ALU.add))
                    v.tensor_tensor(mask[:, 0:T], hot[:, 0], hot[:, 1], ALU.add).then_inc(mask_ready, 1)
                    v.tensor_tensor(gap[:], best[:, 1], best[:, 0], ALU.subtract).then_inc(gap_ready, 1)
                    for c in range(2):
                        v.tensor_tensor(named[:, c], hot[:, c], wide(token_id[:]), ALU.mult)
                    dve.wait_ge(rank_full, 1)
                    link("dve", dve, v.tensor_copy(rank[:], p_rank))
                    for c in range(2):
                        i = v.tensor_tensor(picked[:, c], hot[:, c], rank[:, 0:T], ALU.mult)
                    link("dve", dve, i)
                    link("dve", dve, v.tensor_reduce(place[:], picked[:], AX.X, ALU.add))
                    link("dve", dve, v.tensor_scalar(nth_tile[:], place[:], float(P), None, ALU.is_ge))
                    for k in range(2, T):
                        link("dve", dve, v.scalar_tensor_tensor(nth_tile[:], place[:], float(k * P), nth_tile[:], ALU.is_ge, ALU.add))
                    link("dve", dve, v.scalar_tensor_tensor(step[:], nth_tile[:], -float(P), place[:], ALU.mult, ALU.add))
                    nths, names = nth_tile[:].rearrange("p c t -> p (c t)"), named[:].rearrange("p c t e -> p (c t) e")
                    steps = step[:].rearrange("p c t -> p (c t)")
                    for c in range(2 * T):
                        v.tensor_scalar(slot_hot[:, c], slot_iota[:], steps[:, c:c + 1], None, ALU.is_equal)
                    for j in range(T):
                        i = v.scalar_tensor_tensor(tag[:, :, j], nths.unsqueeze(2).to_broadcast([TP, 2 * T, NX]), float(j), names,
                                                   ALU.is_equal, ALU.mult)
                    i.then_inc(places_ready, 1)
                    low("u", 0, 0)
                    low("u", 0, 1)
                    low("d", 0, 0)
                    x_low(0)
                    n_tok, n_extra, cum = rank[:, T], extra[:], upto
                    v.memset(in_group[:, 0:FIXED], 1.0)
                    link("dve", dve, v.tensor_scalar(n_extra, n_tok, float(P), None, ALU.is_gt))
                    for k in range(2, T):
                        link("dve", dve, v.scalar_tensor_tensor(n_extra, n_tok, float(k * P), n_extra, ALU.is_gt, ALU.add))
                    v.tensor_scalar(in_group[:, FIXED:NX], n_extra[:, FIXED:NX], 1.0, None, ALU.add)
                    link("dve", dve, v.tensor_copy(in_group[:, NX:GROUPS], n_extra[:, 0:FIXED]))
                    link("dve", dve, v.tensor_copy(cum[:, 0], in_group[:]))
                    shifts = (1, 2, 4, 8, 16)
                    for k, shift in enumerate(shifts):
                        a, b = cum[:, k % 2], cum[:, (k + 1) % 2]
                        v.tensor_copy(b[:, 0:shift], a[:, 0:shift])
                        link("dve", dve, v.tensor_tensor(b[:, shift:GROUPS], a[:, shift:GROUPS], a[:, 0:GROUPS - shift], ALU.add))
                    end, start = cum[:, len(shifts) % 2], cum[:, (len(shifts) + 1) % 2]
                    ends = end[0:1].unsqueeze(1).to_broadcast([1, TILES, GROUPS])
                    nth = tile_iota[:].unsqueeze(2).to_broadcast([1, TILES, GROUPS])
                    group, begin, within, beyond = [list_f[:, k] for k in range(4)]
                    v.tensor_tensor(start, end, in_group[:], ALU.subtract)
                    link("dve", dve, v.tensor_tensor(le[:, 0], ends, nth, ALU.is_le))
                    link("dve", dve, v.tensor_tensor(le[:, 1], le[:, 0], ends, ALU.mult))
                    v.tensor_reduce(group, le[:, 0], AX.X, ALU.add)
                    link("dve", dve, v.tensor_reduce(begin, le[:, 1], AX.X, ALU.max))
                    v.tensor_scalar(beyond, group, float(NX), None, ALU.is_ge)
                    link("dve", dve, v.tensor_tensor(within, tile_iota[:], begin, ALU.subtract))
                    v.tensor_scalar(tile_kept[:], within, 0.0, None, ALU.is_gt)
                    link("dve", dve, v.scalar_tensor_tensor(group, beyond, -float(NX), group, ALU.mult, ALU.add))
                    link("dve", dve, v.tensor_tensor(within, within, beyond, ALU.add))
                    link("dve", dve, v.tensor_scalar(within, within, float(T - 1), None, ALU.min))
                    v.tensor_copy(tile_expert[:], group)
                    v.scalar_tensor_tensor(tile_column[:], within, float(NX), group, ALU.mult, ALU.add)
                    v.tensor_scalar(later_tiles[:], end[0:1, GROUPS - 1:GROUPS], float(NX), None, ALU.subtract).then_inc(list_ready, 1)
                    dve.wait_ge(list_ready, 1)
                    low("d", 0, 1)

                    def next_inputs(e):
                        low("g", e, 0)
                        low("g", e, 1)
                        x_low(e)

                    def down_inputs(e):
                        h_low(e)
                        low("d", e, 0)
                        low("d", e, 1)

                    def body(e, nth):
                        if nth == 1:
                            h_low(0)
                        else:
                            down_inputs(e - 1)
                        next_inputs(e + 1)
                        hidden(e)
                        low("u", e + 1, 0)
                        low("u", e + 1, 1)

                    n = dve.value_load(later_tiles[:], min_val=0, max_val=MAXOV) + NX
                    next_inputs(1)
                    hidden(0)
                    low("u", 1, 0)
                    low("u", 1, 1)
                    dve.wait_ge(exp_ready, 1)
                    link("dve", dve, v.tensor_scalar(best[:, 0], gap[:], 1.0, None, ALU.add))
                    link("dve", dve, v.reciprocal(weight[:, 0], best[:, 0]))
                    v.tensor_tensor(weight[:, 1], weight[:, 0], gap[:], ALU.mult)
                    v.memset(moved[:, FIXED:NX], 0.0)
                    link("dve", dve, v.scalar_tensor_tensor(moved[:, 0:FIXED], start[:, NX:GROUPS], -1.0, start[:, 0:FIXED], ALU.add, ALU.subtract))
                    for table, into in ((start[:, 0:NX], later), (moved[:], moved_by)):
                        for c in range(2):
                            i = v.tensor_tensor(picked[:, c], hot[:, c], table.unsqueeze(1).to_broadcast([TP, T, NX]), ALU.mult)
                        link("dve", dve, i)
                        link("dve", dve, v.tensor_reduce(into[:], picked[:], AX.X, ALU.add))
                    link("dve", dve, v.scalar_tensor_tensor(moved_by[:], nth_tile[:], 0.0, moved_by[:], ALU.is_gt, ALU.mult))
                    link("dve", dve, v.tensor_tensor(later[:], later[:], nth_tile[:], ALU.add))
                    link("dve", dve, v.tensor_tensor(later[:], later[:], moved_by[:], ALU.add))
                    v.scalar_tensor_tensor(y_at[:].rearrange("p (c t) -> p c t", c=2), later[:], float(P), step[:], ALU.mult, ALU.add)
                    body(1, 1)
                    with dve.Fori(2, AHEAD - 1) as e:
                        body(e, None)
                    body(AHEAD - 1, None)
                    with dve.Fori(AHEAD, n - 1) as e:
                        body(e, None)
                    down_inputs(n - 2)
                    low("g", n, 0)
                    low("g", n, 1)
                    hidden(n - 1)
                    h_low(n - 1)

                @block.scalar
                def _(act):
                    s = nc.scalar
                    def high(k, e, i, past=False):
                        if is_ahead(k, e):
                            act.wait_ge(ahead_loaded[i], 16)
                        elif k == "g" and past:
                            act.wait_ge(loaded[k][i], 16 * e)
                        else:
                            act.wait_ge(loaded[k][i], 16 * e + 16)
                        s.copy(half(w_hi[k][:], k, i), staged(k, e, i)).then_inc(split_hi[k], 1)

                    def x_high(e):
                        act.wait_ge(xt_full, e + 1)
                        s.copy(xs_hi[:].rearrange("p c n -> p (c n)"), p_x[:]).then_inc(xt_hi_ready, 1)

                    def silus(e):
                        act.wait_ge(done["g"], e + 1)
                        if not (isinstance(e, int) and e == 0):
                            act.wait_ge(hid_ready, 2 * e)
                        for i in range(2):
                            s.activation(silu[:, i * 512:(i + 1) * 512], p_gate[:, i * 512:(i + 1) * 512], ACT.Silu).then_inc(silu_ready, 1)

                    def h_high(e):
                        for i in range(2):
                            act.wait_ge(ht_full, 2 * e + i + 1)
                            s.copy(hs_hi[:, 4 * i:4 * i + 4].rearrange("p c n -> p (c n)"), p_ht[:, i * 512:(i + 1) * 512]).then_inc(ht_hi_ready, 1)

                    def y_copy(e, first):
                        act.wait_ge(done["d"], e + 1)
                        if not first:
                            act.wait_ge(y_stored, 16 * e)
                        s.copy(y_sb[:], p_y[:]).then_inc(y_copied, 1)
                        act.wait_ge(y_copied, e + 1)
                        act.dma_start(y_dram[bass.ds(e * P, P), :], y_sb[:]).then_inc(y_stored, 16)

                    def x2_copy(t):
                        act.wait_ge(x2_full, t + 1)
                        s.copy(xt2[:, t % 2].rearrange("p c n -> p (c n)"), p_t[t % 2]).then_inc(x2_copied, 1)

                    high("g", 0, 0)
                    root(act, 1, 0)
                    for t in range(1, T):
                        root(act, 1, t)
                        if t < 4:
                            x2_copy(t - 1)
                    high("g", 0, 1)
                    x2_copy(3)
                    high("u", 0, 0)
                    x2_copy(4)
                    high("u", 0, 1)
                    high("d", 0, 0)
                    high("d", 0, 1)
                    act.wait_ge(slots_full, 1)
                    s.copy(slot_token[:], p_slots).then_inc(slots_ready, 1)
                    act.wait_ge(gap_ready, 1)
                    s.activation(gap[:], gap[:], ACT.Exp).then_inc(exp_ready, 1)
                    x_high(0)

                    def next_inputs(e, past=False):
                        act.wait_ge(done["g"], e)
                        high("g", e, 0, past)
                        high("g", e, 1, past)
                        silus(e - 1)
                        x_high(e)
                        act.wait_ge(done["u"], e)
                        high("u", e, 0)
                        high("u", e, 1)

                    def body(e, nth, past=False):
                        h_high(e - 1)
                        if nth != 1:
                            y_copy(e - 2, nth == 2)
                            high("d", e - 1, 0)
                            high("d", e - 1, 1)
                        next_inputs(e + 1, past)

                    next_inputs(1)
                    act.wait_ge(list_ready, 1)
                    n = act.value_load(later_tiles[:], min_val=0, max_val=MAXOV) + NX
                    body(1, 1)
                    body(2, 2)
                    with act.Fori(3, AHEAD - 1) as e:
                        body(e, None)
                    body(AHEAD - 1, None)
                    with act.Fori(AHEAD, n - 1) as e:
                        body(e, None, past=True)
                    h_high(n - 2)
                    y_copy(n - 3, False)
                    high("d", n - 2, 0)
                    high("d", n - 2, 1)
                    silus(n - 1)
                    high("g", n, 0, past=True)
                    high("g", n, 1, past=True)
                    h_high(n - 1)
                    y_copy(n - 2, False)
                    y_copy(n - 1, False)
                    act.wait_ge(y_stored, 16 * n)
                    act.sem_inc(all_stored, 1)

                @block.tensor
                def _(pe):
                    m = nc.tensor
                    for dc in range(KC):
                        i = m.transpose(p_router[:, dc], router_sb[:, dc * P:(dc + 1) * P], ident[0:NX, 0:NX])
                    i.then_inc(router_full, 1)
                    pe.wait_ge(router_copied, 1)

                    def token_logits(t):
                        pe.wait_ge(x2_copied, t + 1)
                        for dc in range(KC):
                            i = m.matmul(p_logits[:, t], xt2[:, t % 2, dc], router_t[:, dc], start=(dc == 0), stop=(dc == KC - 1))
                        i.then_inc(logits_full, 1)

                    for t in range(T):
                        pe.wait_ge(ln_ready, T + t + 1)
                        for dc in range(KC):
                            i = m.transpose(p_t[t % 2][:, dc * TP:(dc + 1) * TP], xn2[:, t, dc * P:(dc + 1) * P], ident[0:TP, 0:TP])
                        i.then_inc(x2_full, 1)
                        if t:
                            token_logits(t - 1)
                    token_logits(T - 1)
                    pe.wait_ge(mask_ready, 1)
                    m.matmul(p_rank, before[:], mask[:], start=True, stop=False)
                    for k in range(1, T + 1):
                        i = m.matmul(p_rank[:, k:T + 1], ones16[:], mask[:, 0:T + 1 - k], start=False, stop=(k == T))
                    i.then_inc(rank_full, 1)
                    pe.wait_ge(places_ready, 1)
                    for c in range(2 * T):
                        i = m.matmul(p_slots, slot_hot[:, c], tag[:, c].rearrange("p j e -> p (j e)"), start=(c == 0), stop=(c == 2 * T - 1))
                    i.then_inc(slots_full, 1)

                    def wide_product(k, e, into):
                        for c in range(KC):
                            if c % 2 == 0:
                                pe.wait_ge(split_lo[k], 2 * e + c // 2 + 1)
                            for x_part, w_part in ((xs_hi, w_hi), (xs_hi, w_lo), (xs_lo, w_hi)):
                                for h in range(2):
                                    i = m.matmul(into[:, h * 512:(h + 1) * 512], x_part[:, c], w_part[k][:, c, h * 512:(h + 1) * 512],
                                                 start=(c == 0 and x_part is xs_hi and w_part is w_hi),
                                                 stop=(c == KC - 1 and x_part is xs_lo))
                        i.then_inc(done[k], 1)

                    def turn_tokens(e):
                        pe.wait_ge(tokens_loaded, 16 * e + 16)
                        for c in range(KC):
                            i = m.transpose(p_x[:, c * P:(c + 1) * P], tokens[:, c * P:(c + 1) * P], ident[:])
                        i.then_inc(xt_full, 1)

                    def turn_hidden(e):
                        for h in range(2):
                            pe.wait_ge(hid_ready, 2 * e + h + 1)
                            for c in range(4 * h, 4 * h + 4):
                                i = m.transpose(p_ht[:, c * P:(c + 1) * P], hid[:, c * P:(c + 1) * P], ident[:])
                            i.then_inc(ht_full, 1)

                    def down(e, first, last=False):
                        key, at = ("g", e + 1) if last else ("d", e)
                        hi, lo = [as_down(w[key][:]) for w in (w_hi, w_lo)]
                        if not first:
                            pe.wait_ge(y_copied, e)
                        for c in range(FC):
                            if c % 4 == 0:
                                pe.wait_ge(ht_lo_ready, 2 * e + c // 4 + 1)
                                pe.wait_ge(split_lo[key], 2 * at + c // 4 + 1)
                            m.matmul(p_y[:], hs_hi[:, c], hi[:, c], start=(c == 0), stop=False)
                            m.matmul(p_y[:], hs_hi[:, c], lo[:, c], start=False, stop=False)
                            i = m.matmul(p_y[:], hs_lo[:, c], hi[:, c], start=False, stop=(c == FC - 1))
                        i.then_inc(done["d"], 1)

                    def body(e, nth, last):
                        if nth != 0:
                            turn_hidden(e - 1)
                            pe.wait_ge(silu_ready, 2 * e)
                        pe.wait_ge(xt_lo_ready, e + 1)
                        wide_product("g", e, p_gate)
                        wide_product("u", e, p_up)
                        if not last:
                            turn_tokens(e + 1)
                        if nth != 0:
                            down(e - 1, nth == 1)

                    turn_tokens(0)
                    body(0, 0, False)
                    body(1, 1, False)
                    pe.wait_ge(list_ready, 1)
                    n = pe.value_load(later_tiles[:], min_val=0, max_val=MAXOV) + NX
                    with pe.Fori(2, n - 1) as e:
                        body(e, None, False)
                    body(n - 1, None, True)
                    turn_hidden(n - 1)
                    down(n - 1, False, last=True)

            with ExitStack() as f:
                rows = [stage["g"].rearrange("p c f -> p (c f)")[0:TP, 0:T * D].rearrange("p (t d) -> p t d", t=T),
                        stage["u"].rearrange("p c f -> p (c f)")[0:TP, 0:T * D].rearrange("p (t d) -> p t d", t=T)]
                block = f.enter_context(nc.Block())

                @block.gpsimd
                def _(pool):
                    for t in range(T):
                        for c, signal in enumerate((first_loaded, second_loaded)):
                            nc.gpsimd.indirect_dma_start(rows[c][:, t], None, y_dram,
                                                         bass.IndirectOffsetOnAxis(ap=y_at[:, c * T + t:c * T + t + 1].bitcast(U32), axis=0)
                                                         ).then_inc(signal[t], 16)

                @block.vector
                def _(dve):
                    v = nc.vector
                    for t in range(T):
                        dve.wait_ge(first_loaded[t], 16)
                        link("dve", dve, v.scalar_tensor_tensor(x_sb[:, t], rows[0][:, t], weight[:, 0, t:t + 1], x_sb[:, t], ALU.mult, ALU.add))
                        dve.wait_ge(second_loaded[t], 16)
                        v.scalar_tensor_tensor(x_sb[:, t], rows[1][:, t], weight[:, 1, t:t + 1], x_sb[:, t], ALU.mult, ALU.add).then_inc(combined, 1)

                @block.sync
                def _(sp):
                    for t in range(T):
                        sp.wait_ge(combined, t + 1)
                        sp.dma_start(out[t * TP:(t + 1) * TP, :], x_sb[:, t]).then_inc(out_stored, 16)
                    sp.wait_ge(out_stored, 16 * T)


NAMES = ["x", "src", "dst", "edge_type_8", "L0_gnn_W_self", "L0_gnn_b_self", "L0_gnn_W_rel", "L0_gnn_b_rel",
         "L0_ffn_router_w", "L0_ffn_gate_w", "L0_ffn_up_w", "L0_ffn_down_w"]


def kernel(**inputs):
    import numpy as np
    from concourse import bacc
    from concourse.bass_utils import run_bass_kernel_spmd

    nc = bacc.Bacc("TRN2", target_bir_lowering=False, num_devices=1)
    arrays = {f"in_{n}": np.ascontiguousarray(inputs[n]) for n in NAMES}
    args = [nc.dram_tensor(n, a.shape, mybir.dt.from_np(a.dtype), kind="ExternalInput").ap() for n, a in arrays.items()]
    out = nc.dram_tensor("out", (N, D), F32, kind="ExternalOutput").ap()
    build(nc, *args, out)
    result = run_bass_kernel_spmd(nc, [arrays], core_ids=[0])
    return result.results[0]["out"]
```
